# Optimizing a Trainium2 kernel written in Bass

```python
import numpy as np
import jax
import jax.numpy as jnp

def _softmax(x, axis=-1):
    return jax.nn.softmax(x, axis=axis)

def _gelu(x):
    return jax.nn.gelu(x, approximate=True)

def _silu(x):
    return jax.nn.silu(x)

def _sigmoid(x):
    return jax.nn.sigmoid(x)

def _layernorm(x, axis=-1, eps=1e-05):
    m = jnp.mean(x, axis=axis, keepdims=True)
    v = jnp.var(x, axis=axis, keepdims=True)
    return (x - m) / jnp.sqrt(v + eps)

def _scatter_add(tgt, idx, src, axis=0):
    return tgt.at[idx].add(src)

def _segment_sum(src, seg, n):
    return jax.ops.segment_sum(src, seg, n)
kernel_name = 'mk_xattn_seq_d2_seqx_r8_4f044a'

def setup_inputs(seed: int=0):
    np.random.seed(seed)
    _w = jnp.asarray

    def _rec_inputs():
        import jax
        import jax.numpy as jnp
        _rk = jax.random.key(seed)
        x = -0.000125 + 0.9999 * jax.random.normal(jax.random.fold_in(_rk, 1), (4, 256, 256), jnp.float32)
        _lenS = 256 - jax.random.randint(jax.random.fold_in(_rk, 7), (4,), 0, max(1, 256 // 4) + 1, jnp.int32)
        _lenS2 = 256 - jax.random.randint(jax.random.fold_in(_rk, 8), (4,), 0, max(1, 256 // 4) + 1, jnp.int32)
        _ctx_1024P = jax.random.normal(jax.random.fold_in(_rk, 11), (4, 16, 128), jnp.float32)
        _ctx_1024c = jax.random.dirichlet(jax.random.fold_in(_rk, 511), 0.3 * jnp.ones((16,), jnp.float32), (4, 256))
        _ctx_1024t = jnp.einsum('bsk,bkd->bsd', _ctx_1024c, _ctx_1024P)
        _ctx_1024t = _ctx_1024t * jax.lax.rsqrt(jnp.mean(jnp.square(_ctx_1024t)) + 1e-12) * 0.953939
        ctx_1024 = 4.13588e-05 + 0.999923 * (_ctx_1024t + 0.3 * jax.random.normal(jax.random.fold_in(_rk, 611), (4, 256, 128), jnp.float32))
        pos_1xS = jnp.broadcast_to(jnp.arange(256, dtype=jnp.int32), (1, 256))
        _validS = jnp.arange(256)[None, :] < _lenS[:, None]
        _validS2 = jnp.arange(256)[None, :] < _lenS2[:, None]
        _causal = jnp.tril(jnp.ones((256, 256), dtype=bool))
        mask_BxS_ik0 = jnp.where(jnp.broadcast_to(_validS[:, :], (4, 256)), 0, 1).astype(jnp.int32)
        return (x, ctx_1024, pos_1xS, mask_BxS_ik0)
    x, ctx_1024, pos_1xS, mask_BxS_ik0 = _rec_inputs()

    def _L0_xattn_setup():
        import jax, jax.numpy as jnp
        import numpy as np
        EPS = 1e-06

        def _rmsnorm(x, w):
            var = jnp.mean(jnp.square(x), axis=-1, keepdims=True)
            return x * jax.lax.rsqrt(var + EPS) * w
        key = jax.random.key(seed)
        ks = jax.random.split(key, 6)
        B, N, M = (4, 512, 256)
        d_model, memory_dim = (256, 128)
        hidden_states = jax.random.normal(ks[0], (B, N, d_model), dtype=jnp.float32)
        memory = jax.random.normal(ks[1], (B, M, memory_dim), dtype=jnp.float32)
        W_mem = jax.random.normal(ks[2], (d_model, memory_dim), dtype=jnp.float32) / np.sqrt(memory_dim)
        W_gate = jax.random.normal(ks[3], (d_model, 2 * d_model), dtype=jnp.float32) / np.sqrt(2 * d_model)
        b_gate = jax.random.normal(ks[4], (d_model,), dtype=jnp.float32) * 0.01
        norm_w = jnp.ones((d_model,), dtype=jnp.float32)
        return {'hidden_states': hidden_states, 'memory': memory, 'W_mem': W_mem, 'W_gate': W_gate, 'b_gate': b_gate, 'norm_w': norm_w}
    _L0_xattn_all = _L0_xattn_setup()
    _L0_xattn_in = {k: v for k, v in _L0_xattn_all.items() if k in ('W_mem', 'W_gate', 'b_gate', 'norm_w')}
    del _L0_xattn_all

    def _L1_xattn_setup():
        import jax, jax.numpy as jnp
        import numpy as np
        H = 256
        NH = 16
        HD = H // NH
        CH = 128
        CC = 128
        CHD = CC // NH
        I = 688
        B = 2
        L = 256
        LE = 128
        EPS = 1e-06

        def rms_norm(x, w):
            xf = x.astype(jnp.float32)
            var = jnp.mean(xf * xf, axis=-1, keepdims=True)
            return (w * (xf * jax.lax.rsqrt(var + EPS))).astype(x.dtype)

        def expert_mask(tt):
            vm = jnp.zeros(tt.shape, dtype=bool)
            vm = vm.at[:, :-1].set((tt[:, :-1] == 1) & (tt[:, 1:] == 1))
            return vm

        def rotate_half(x):
            d = x.shape[-1] // 2
            return jnp.concatenate([-x[..., d:], x[..., :d]], axis=-1)

        def apply_rotary(q, k, position_ids, seq_len):
            inv = 1.0 / 10000.0 ** (jnp.arange(0, HD, 2, dtype=jnp.float32) / HD)
            t = jnp.arange(seq_len, dtype=jnp.float32)
            freqs = jnp.outer(t, inv)
            emb = jnp.concatenate([freqs, freqs], axis=-1)
            cos = jnp.cos(emb)[position_ids][:, None].astype(q.dtype)
            sin = jnp.sin(emb)[position_ids][:, None].astype(q.dtype)
            return (q * cos + rotate_half(q) * sin, k * cos + rotate_half(k) * sin)

        def sdpa(q, k, v, causal):
            scale = 1.0 / np.sqrt(q.shape[-1])
            scores = jnp.einsum('bhqd,bhkd->bhqk', q * scale, k)
            if causal:
                mask = jnp.tril(jnp.ones((q.shape[-2], k.shape[-2]), dtype=bool))
                scores = jnp.where(mask, scores, jnp.finfo(jnp.float32).min)
            p = jax.nn.softmax(scores.astype(jnp.float32), axis=-1).astype(q.dtype)
            return jnp.einsum('bhqk,bhkd->bhqd', p, v)

        def heads(x, nh, hd):
            b, l, _ = x.shape
            return x.reshape(b, l, nh, hd).transpose(0, 2, 1, 3)
        key = jax.random.key(seed)
        ks = jax.random.split(key, 20)
        s = 0.02
        f32 = jnp.float32
        return {'hidden_states': jax.random.normal(ks[0], (B, L, H), f32), 'encoder_outputs': jax.random.normal(ks[1], (B, LE, CH), f32), 'token_type_ids': jax.random.randint(ks[2], (B, L), 0, 2, jnp.int32), 'position_ids': jnp.arange(L, dtype=jnp.int32)[None, :], 'ln_in_w': jnp.ones((H,), f32), 'ln_post_attn_w': jnp.ones((H,), f32), 'ln_post_cross_w': jnp.ones((H,), f32), 'v_qkv': jax.random.normal(ks[3], (H, 3 * H), f32) * s, 'l_qkv': jax.random.normal(ks[4], (H, 3 * H), f32) * s, 'v_dense': jax.random.normal(ks[5], (H, H), f32) * s, 'l_dense': jax.random.normal(ks[6], (H, H), f32) * s, 'cq_w': jax.random.normal(ks[7], (H, CC), f32) * s, 'ckv_w': jax.random.normal(ks[8], (CH, 2 * CC), f32) * s, 'cdense_w': jax.random.normal(ks[9], (CC, H), f32) * s, 'v_gate': jax.random.normal(ks[10], (H, I), f32) * s, 'v_up': jax.random.normal(ks[11], (H, I), f32) * s, 'v_down': jax.random.normal(ks[12], (I, H), f32) * s, 'l_gate': jax.random.normal(ks[13], (H, I), f32) * s, 'l_up': jax.random.normal(ks[14], (H, I), f32) * s, 'l_down': jax.random.normal(ks[15], (I, H), f32) * s}
    _L1_xattn_all = _L1_xattn_setup()
    _L1_xattn_in = {k: v for k, v in _L1_xattn_all.items() if k in ('ln_in_w', 'ln_post_attn_w', 'ln_post_cross_w', 'v_qkv', 'l_qkv', 'v_dense', 'l_dense', 'cq_w', 'ckv_w', 'cdense_w', 'v_gate', 'v_up', 'v_down', 'l_gate', 'l_up', 'l_down')}
    del _L1_xattn_all
    return {'x': x, 'ctx_1024': ctx_1024, 'pos_1xS': pos_1xS, 'mask_BxS_ik0': mask_BxS_ik0, 'L0_xattn_W_mem': _L0_xattn_in['W_mem'], 'L0_xattn_W_gate': _L0_xattn_in['W_gate'], 'L0_xattn_b_gate': _L0_xattn_in['b_gate'], 'L0_xattn_norm_w': _L0_xattn_in['norm_w'], 'L1_xattn_ln_in_w': _L1_xattn_in['ln_in_w'], 'L1_xattn_ln_post_attn_w': _L1_xattn_in['ln_post_attn_w'], 'L1_xattn_ln_post_cross_w': _L1_xattn_in['ln_post_cross_w'], 'L1_xattn_v_qkv': _L1_xattn_in['v_qkv'], 'L1_xattn_l_qkv': _L1_xattn_in['l_qkv'], 'L1_xattn_v_dense': _L1_xattn_in['v_dense'], 'L1_xattn_l_dense': _L1_xattn_in['l_dense'], 'L1_xattn_cq_w': _L1_xattn_in['cq_w'], 'L1_xattn_ckv_w': _L1_xattn_in['ckv_w'], 'L1_xattn_cdense_w': _L1_xattn_in['cdense_w'], 'L1_xattn_v_gate': _L1_xattn_in['v_gate'], 'L1_xattn_v_up': _L1_xattn_in['v_up'], 'L1_xattn_v_down': _L1_xattn_in['v_down'], 'L1_xattn_l_gate': _L1_xattn_in['l_gate'], 'L1_xattn_l_up': _L1_xattn_in['l_up'], 'L1_xattn_l_down': _L1_xattn_in['l_down']}

def reference(x, ctx_1024, pos_1xS, mask_BxS_ik0, L0_xattn_W_mem, L0_xattn_W_gate, L0_xattn_b_gate, L0_xattn_norm_w, L1_xattn_ln_in_w, L1_xattn_ln_post_attn_w, L1_xattn_ln_post_cross_w, L1_xattn_v_qkv, L1_xattn_l_qkv, L1_xattn_v_dense, L1_xattn_l_dense, L1_xattn_cq_w, L1_xattn_ckv_w, L1_xattn_cdense_w, L1_xattn_v_gate, L1_xattn_v_up, L1_xattn_v_down, L1_xattn_l_gate, L1_xattn_l_up, L1_xattn_l_down):
    import jax
    import jax.numpy as jnp

    def _L0_xattn_ref(hidden_states, memory, W_mem, W_gate, b_gate, norm_w):
        import jax, jax.numpy as jnp
        import numpy as np
        EPS = 1e-06

        def _rmsnorm(x, w):
            var = jnp.mean(jnp.square(x), axis=-1, keepdims=True)
            return x * jax.lax.rsqrt(var + EPS) * w
        D = hidden_states.shape[-1]
        memory_proj = jnp.einsum('bme,de->bmd', memory, W_mem)
        scores = jnp.einsum('bnd,bmd->bnm', hidden_states, memory_proj) / jnp.sqrt(jnp.float32(D))
        attn = jax.nn.softmax(scores, axis=-1)
        memory_context = jnp.einsum('bnm,bmd->bnd', attn, memory_proj)
        gate_input = jnp.concatenate([hidden_states, memory_context], axis=-1)
        gate = jax.nn.sigmoid(jnp.einsum('bnf,df->bnd', gate_input, W_gate) + b_gate)
        fused = hidden_states + gate * memory_context
        return _rmsnorm(fused, norm_w)

    def _L1_xattn_ref(hidden_states, encoder_outputs, token_type_ids, position_ids, ln_in_w, ln_post_attn_w, ln_post_cross_w, v_qkv, l_qkv, v_dense, l_dense, cq_w, ckv_w, cdense_w, v_gate, v_up, v_down, l_gate, l_up, l_down):
        import jax, jax.numpy as jnp
        import numpy as np
        H = 256
        NH = 16
        HD = H // NH
        CH = 128
        CC = 128
        CHD = CC // NH
        I = 688
        B = 2
        L = 256
        LE = 128
        EPS = 1e-06

        def rms_norm(x, w):
            xf = x.astype(jnp.float32)
            var = jnp.mean(xf * xf, axis=-1, keepdims=True)
            return (w * (xf * jax.lax.rsqrt(var + EPS))).astype(x.dtype)

        def expert_mask(tt):
            vm = jnp.zeros(tt.shape, dtype=bool)
            vm = vm.at[:, :-1].set((tt[:, :-1] == 1) & (tt[:, 1:] == 1))
            return vm

        def rotate_half(x):
            d = x.shape[-1] // 2
            return jnp.concatenate([-x[..., d:], x[..., :d]], axis=-1)

        def apply_rotary(q, k, position_ids, seq_len):
            inv = 1.0 / 10000.0 ** (jnp.arange(0, HD, 2, dtype=jnp.float32) / HD)
            t = jnp.arange(seq_len, dtype=jnp.float32)
            freqs = jnp.outer(t, inv)
            emb = jnp.concatenate([freqs, freqs], axis=-1)
            cos = jnp.cos(emb)[position_ids][:, None].astype(q.dtype)
            sin = jnp.sin(emb)[position_ids][:, None].astype(q.dtype)
            return (q * cos + rotate_half(q) * sin, k * cos + rotate_half(k) * sin)

        def sdpa(q, k, v, causal):
            scale = 1.0 / np.sqrt(q.shape[-1])
            scores = jnp.einsum('bhqd,bhkd->bhqk', q * scale, k)
            if causal:
                mask = jnp.tril(jnp.ones((q.shape[-2], k.shape[-2]), dtype=bool))
                scores = jnp.where(mask, scores, jnp.finfo(jnp.float32).min)
            p = jax.nn.softmax(scores.astype(jnp.float32), axis=-1).astype(q.dtype)
            return jnp.einsum('bhqk,bhkd->bhqd', p, v)

        def heads(x, nh, hd):
            b, l, _ = x.shape
            return x.reshape(b, l, nh, hd).transpose(0, 2, 1, 3)
        b, l, _ = hidden_states.shape
        vm = expert_mask(token_type_ids)[..., None]
        residual = hidden_states
        x = rms_norm(hidden_states, ln_in_w)
        mixed = jnp.where(vm, x @ v_qkv, x @ l_qkv)
        q, k, v = jnp.split(mixed, 3, axis=-1)
        q, k, v = (heads(q, NH, HD), heads(k, NH, HD), heads(v, NH, HD))
        q, k = apply_rotary(q, k, position_ids, l)
        ctx = sdpa(q, k, v, causal=True)
        ctx = ctx.transpose(0, 2, 1, 3).reshape(b, l, H)
        attn_out = jnp.where(vm, ctx @ v_dense, ctx @ l_dense)
        hidden_states = residual + attn_out
        ci = rms_norm(hidden_states, ln_post_cross_w)
        cq = heads(ci @ cq_w, NH, CHD)
        ckv = encoder_outputs @ ckv_w
        ck, cv = jnp.split(ckv, 2, axis=-1)
        ck, cv = (heads(ck, NH, CHD), heads(cv, NH, CHD))
        cctx = sdpa(cq, ck, cv, causal=False)
        cctx = cctx.transpose(0, 2, 1, 3).reshape(b, l, CC)
        hidden_states = hidden_states + cctx @ cdense_w
        mi = rms_norm(hidden_states, ln_post_attn_w)
        v_out = jax.nn.silu(mi @ v_gate) * (mi @ v_up) @ v_down
        l_out = jax.nn.silu(mi @ l_gate) * (mi @ l_up) @ l_down
        hidden_states = hidden_states + jnp.where(vm, v_out, l_out)
        return hidden_states
    x = _L0_xattn_ref(x, ctx_1024, L0_xattn_W_mem, L0_xattn_W_gate, L0_xattn_b_gate, L0_xattn_norm_w)
    x = _L1_xattn_ref(x, ctx_1024, mask_BxS_ik0, pos_1xS, L1_xattn_ln_in_w, L1_xattn_ln_post_attn_w, L1_xattn_ln_post_cross_w, L1_xattn_v_qkv, L1_xattn_l_qkv, L1_xattn_v_dense, L1_xattn_l_dense, L1_xattn_cq_w, L1_xattn_ckv_w, L1_xattn_cdense_w, L1_xattn_v_gate, L1_xattn_v_up, L1_xattn_v_down, L1_xattn_l_gate, L1_xattn_l_up, L1_xattn_l_down)
    return x

_drawn_inputs = setup_inputs


def setup_inputs(seed=0):
    import zlib

    import numpy as np

    out = dict(_drawn_inputs(seed))
    spreads = {'L0_xattn_norm_w': (1.0, 0.2),
     'L1_xattn_ln_in_w': (1.0, 0.6),
     'L1_xattn_ln_post_attn_w': (1.0, 0.6),
     'L1_xattn_ln_post_cross_w': (1.0, 0.6)}
    factors = {'L0_xattn_b_gate': 8.0,
     'L1_xattn_v_qkv': 8.0,
     'L1_xattn_v_dense': 6.343,
     'L1_xattn_cq_w': 64.0,
     'L1_xattn_v_gate': 5.246,
     'L1_xattn_v_up': 5.18,
     'L1_xattn_v_down': 5.221,
     'L1_xattn_l_dense': 5.017,
     'L1_xattn_ckv_w': 8.0,
     'L1_xattn_cdense_w': 8.0,
     'L1_xattn_l_gate': 4.958,
     'L1_xattn_l_up': 4.845,
     'L1_xattn_l_down': 4.844}
    for name, (base, spread) in spreads.items():
        noise = np.random.default_rng([zlib.crc32(name.encode()), seed]).standard_normal(out[name].shape)
        drawn = base * np.exp(spread * noise) if base else spread * noise
        out[name] = jnp.asarray(drawn.astype(out[name].dtype))
    for name, factor in factors.items():
        out[name] = (out[name] * factor).astype(out[name].dtype)
    return out
```

```python
from contextlib import ExitStack

import numpy as np

import concourse.bass as bass
from concourse import mybir

F32 = mybir.dt.float32
BF16 = mybir.dt.bfloat16
I32 = mybir.dt.int32
ALU = mybir.AluOpType
ACT = mybir.ActivationFunctionType
AX_X = mybir.AxisListType.X

P = 128
BATCH, S, D = 4, 256, 256
C = 128
NH = 16
HD = D // NH
CHD = C // NH
FF = 688
FF2 = 2 * FF
NF = -(-FF2 // P)
EPS = 1e-6
PAIR = 2 * S
NT = PAIR // P
DC = D // P
RING = 8
VW = 32
NEG = -1e30
SELF_Q = (0, 0, 0, 1, 1, 2)
SELF_K = (0, 1, 2, 0, 1, 0)
CROSS_Q = (0, 0, 0, 1, 1, 1, 2, 2, 2)
CROSS_K = (0, 1, 2, 0, 1, 2, 0, 1, 2)
SELF_ROWS = len(SELF_Q) * HD
CROSS_ROWS = len(CROSS_Q) * CHD

C_ID, C_MQ, C_MK, C_T, C_MIX, C_TAB = 0, P, 2 * P, 3 * P, 3 * P + 2, 3 * P + 4
C_END = C_TAB + 2 * 2 * HD


def constants():
    out = np.zeros((P, C_END), np.float32)
    i = np.arange(P)
    out[:, C_ID:C_ID + P] = np.eye(P)
    out[:, C_MQ:C_MQ + P] = np.where(i[None, :] > i[:, None], NEG, 0.0)
    out[:, C_MK:C_MK + P] = np.where(i[:, None] > i[None, :], NEG, 0.0)
    out[:, C_T] = i
    out[:, C_T + 1] = i + P
    first = np.arange(P) + (FF // P) * P < FF
    out[:, C_MIX] = np.where(first, 1.0, -1.0)
    out[:, C_MIX + 1] = np.where(first, 0.0, 1.0)
    inv = (1.0 / np.float32(10000.0) ** (np.arange(0, HD, 2, dtype=np.float32) / np.float32(HD))).astype(np.float32)
    freq = np.outer(np.arange(S, dtype=np.float32), inv).astype(np.float32)
    cos = np.cos(freq.astype(np.float64))
    sin = np.sin(freq.astype(np.float64))
    table = np.concatenate([cos, cos, -sin, sin], axis=1).astype(np.float32)
    out[:, C_TAB:] = table.reshape(2, P, 2 * HD).transpose(1, 0, 2).reshape(P, -1)
    return out


def build(nc, t):
    x_d = t["x"].rearrange("(t b) (s p) d -> t p (b s) d", t=2, p=P)
    ctx_d = t["ctx_1024"].rearrange("(t b) (s p) d -> t p (b s) d", t=2, p=P)
    out_d = t["out"].rearrange("(t b) (s p) d -> t p (b s) d", t=2, p=P)
    mask_d = t["mask_BxS_ik0"].rearrange("(t b) s -> t (b s)", t=2)

    with ExitStack() as stack:
        def sb(name, shape, dt=F32):
            return stack.enter_context(nc.sbuf_tensor(name, shape, dt))

        const = sb("const", [P, C_END])
        ident = const[:, C_ID:C_ID + P]
        bconst = sb("bconst", [P, 3 * P], BF16)
        identb, maskq, maskk = (bconst[:, P * j:P * j + P] for j in range(3))
        half = sb("half", [P, 4])
        posi = sb("posi", [P, S], I32)
        trig = sb("trig", [P, 2, 2 * HD])
        w_mem = sb("w_mem", [P, DC, C])
        w_memT = sb("w_memT", [P, D])
        w_gateT = sb("w_gateT", [P, DC, D])
        w_gatem = sb("w_gatem", [P, D])
        b_gate = sb("b_gate", [P, D])
        norm_w = sb("norm_w", [P, 4, D])
        qkv = sb("qkv", [P, 2, DC, 3 * D])
        dense = sb("dense", [P, 2, DC, D])
        cq_w = sb("cq_w", [P, DC, C])
        ckv_w = sb("ckv_w", [P, 2 * C])
        cdense = sb("cdense", [P, D])
        w_up = sb("w_up", [P, 2, DC, FF2])
        w_down = sb("w_down", [P, NF, D])

        X = sb("X", [P, NT, D])
        mem = sb("mem", [P, NT, C])
        UT = sb("UT", [P, 2, DC, S])
        memT = sb("memT", [P, PAIR])
        yT = sb("yT", [P, PAIR])
        gated = sb("gated", [P, NT, D])
        normed = sb("normed", [P, NT, D])
        TV = sb("TV", [P, 2, DC, S])
        TL = sb("TL", [P, 2, DC, S])
        QR = sb("QR", [P, NT, 2 * D])
        n_q, n_parts = NH * S, 2 * DC * 3 * PAIR
        shared = sb("shared", [P, 2 * n_q + n_parts], BF16)
        Qs = [shared[:, n_q * g:n_q * g + n_q].rearrange("p (h s) -> p h s", h=NH) for g in range(2)]
        parts = shared[:, 2 * n_q:].rearrange("p (k c j s) -> p k c j s", k=2, c=DC, j=3)
        H = shared[:, 0:2 * NF * PAIR].bitcast(F32).rearrange("p (i s) -> p i s", i=NF)
        ck_parts = sb("ck_parts", [P, 3, PAIR], BF16)
        cq_parts = sb("cq_parts", [P, 3, PAIR], BF16)
        rest = sb("rest", [P, 2 * S])
        Ks = [sb(f"Ks{g}", [P, NH, S], BF16) for g in range(2)]
        V = sb("V", [P, NT, NH, VW])
        Vc = sb("Vc", [P, NT, NH, VW])
        probs = sb("probs", [P, RING, PAIR])
        heads = sb("heads", [P, 4, S])
        maski = sb("maski", [P, 2, S], I32)
        is_one = gated[:, 0:2, :]
        vm = sb("vm", [P, 2, S])
        lm = sb("lm", [P, 2, S])
        mixm = sb("mixm", [P, 2, S])
        negmax = sb("negmax", [P, 2, 2, NH])
        nm_parts = sb("nm_parts", [NH, 2, 2, S], BF16)
        sc = sb("sc", [P, 64])
        nm0, l0, r0 = sc[:, 0:4], sc[:, 4:8], sc[:, 8:12]
        sumsq, var, rstd = sc[:, 12:28], sc[:, 28:44], sc[:, 44:60]
        rsum = sb("rsum", [P, NH])

        bank = [stack.enter_context(nc.psum_tensor(f"bank{j}", [P, 512], F32)) for j in range(8)]

        self_d = nc.dram_tensor("self_parts", [2, 2, 3, D, S], BF16, kind="Internal").ap()
        cross_d = nc.dram_tensor("cross_parts", [2, 2, 3, C, S], BF16, kind="Internal").ap()

        class Signal:
            def __init__(self, name, per=0):
                self.sem = stack.enter_context(nc.semaphore(name))
                self.per = per

        c_loaded, pos_loaded = Signal("c_loaded"), Signal("pos_loaded")
        gate_loaded, vec_loaded = Signal("gate_loaded"), Signal("vec_loaded")
        qkv_loaded, dense_loaded = Signal("qkv_loaded"), Signal("dense_loaded")
        cross_loaded, mlp_loaded = Signal("cross_loaded"), Signal("mlp_loaded")
        consts_ready, pre_step = Signal("consts_ready"), Signal("pre_step")
        onehot_ready, trig_psum = Signal("onehot_ready"), Signal("trig_psum")
        prep_psum, prep_ready = Signal("prep_psum"), Signal("prep_ready")
        pair_done = Signal("pair_done", 1)
        x_loaded, mem_loaded = Signal("x_loaded", 16), Signal("mem_loaded", 16)
        mask_loaded, out_stored = Signal("mask_loaded", 16), Signal("out_stored", 16 * NT)
        xT_psum, xT_ready = Signal("xT_psum", 2), Signal("xT_ready", 2)
        memT_psum, memT_ready = Signal("memT_psum", 1), Signal("memT_ready", 1)
        y_psum, y_ready = Signal("y_psum", 1), Signal("y_ready", 1)
        ck_psum, cv_psum, cv_ready = Signal("ck_psum", 1), Signal("cv_psum", 1), Signal("cv_ready", 1)
        s0_psum, nm0_ready = Signal("s0_psum", 2), Signal("nm0_ready", 2)
        e0_ready, p0_ready = Signal("e0_ready", 4), Signal("p0_ready", 4)
        pT_psum, pT_ready = Signal("pT_psum", 2), Signal("pT_ready", 2)
        am_psum, am_ready = Signal("am_psum", 2), Signal("am_ready", 2)
        gate_psum, pre_gate, gate_ready = Signal("gate_psum", 4), Signal("pre_gate", 4), Signal("gate_ready", 4)
        fused = Signal("fused", 16)
        sumsq_ready = Signal("sumsq_ready", 16)
        var_ready, rstd_ready = Signal("var_ready", 8), Signal("rstd_ready", 8)
        normed_ready = Signal("normed_ready", 12)
        nT_psum, nT_ready = Signal("nT_psum", 2), Signal("nT_ready", 2)
        qk_psum, qr_ready = Signal("qk_psum", 4), Signal("qr_ready", 4)
        v_psum, v_ready = Signal("v_psum", 2), Signal("v_ready", 2)
        split_psum = Signal("split_psum", 7)
        first_part = Signal("first_part", 7)
        parts_ready = Signal("parts_ready", 7)
        scratch_w = [Signal(f"scratch_w{g}", 0) for g in range(7)]
        stack_self = [Signal(f"stack_self{g}", 16 * 12) for g in range(2)]
        stack_cross = [Signal(f"stack_cross{g}", 16 * 19) for g in range(2)]
        s_psum, max_ready = Signal("s_psum", 56), Signal("max_ready", 56)
        nm_psum, nm_hi, nm_ready = Signal("nm_psum", 4), Signal("nm_hi", 4), Signal("nm_ready", 4)
        max_rows = [Signal(f"max_rows{g}", 16 * 4) for g in range(2)]
        st_psum, e_ready = Signal("st_psum", 56), Signal("e_ready", 56)
        pv_psum, heads_ready = Signal("pv_psum", 16), Signal("heads_ready", 16)
        hT_psum, ctx_ready = Signal("hT_psum", 8), Signal("ctx_ready", 8)
        cT_psum, cT_ready = Signal("cT_psum", 4), Signal("cT_ready", 4)
        proj_psum = Signal("proj_psum", 4)
        uT_psum, uT_ready = Signal("uT_psum", 4), Signal("uT_ready", 4)
        gu_psum, silu_ready = Signal("gu_psum", 2 * NF), Signal("silu_ready", NF)
        silu_masked, h_ready = Signal("silu_masked", NF), Signal("h_ready", NF)
        down_psum, out_ready = Signal("down_psum", NT), Signal("out_ready", NT)
        masks_ready = Signal("masks_ready", 1)
        v_step = Signal("v_step", V_STEPS)

        def waiter(eng, it):
            seen = {}

            def wait(signal, n):
                if seen.get(signal, 0) < n:
                    seen[signal] = n
                    eng.wait_ge(signal.sem, it * signal.per + n)
            return wait

        def stages():
            yield from (("load",), ("masks",), ("xT",), ("memT",), ("y",), ("ckv",), ("scores0",),
                        ("gate_x", 0), ("probsT",), ("gate_x", 1), ("am",), ("gate_m",), ("fuse",))
            yield from (("normT", 0), ("normT", 1), ("qkv", 0), ("qkv", 1), ("split", 0, 0), ("split", 1, 0),
                        ("split", 0, 1), ("split", 1, 1), ("stack_self", 0), ("stack_self", 1))
            for u in range(12):
                yield ("scores", 0, 0, u)
            for u in range(12):
                yield ("scores", 0, 1, u)
                if u == 3:
                    yield ("rows", 0, 0)
            yield ("rows", 0, 1)
            for hg in range(4):
                yield ("attend", 0, 0, hg)
            after = [("unhead", 0, 0), ("ctxT", 0), ("dense", 0), ("norm", 2, 0)]
            for hg in range(4):
                yield ("attend", 0, 1, hg)
                yield after[hg]
            yield from (("uT", 0, 0), ("cq", 0), ("unhead", 0, 1), ("ctxT", 1), ("stack_cross", 0), ("dense", 1),
                        ("norm", 2, 1), ("uT", 0, 1), ("cq", 1), ("stack_cross", 1))
            for u in range(16):
                yield ("scores", 1, 0, u)
            for u in range(16):
                yield ("scores", 1, 1, u)
                if u == 3:
                    yield ("rows", 1, 0)
            yield ("rows", 1, 1)
            for hg in range(4):
                yield ("attend", 1, 0, hg)
            after = [("unhead", 1, 0), ("cdense", 0), ("norm", 3, 0), ("uT", 1, 0)]
            for hg in range(4):
                yield ("attend", 1, 1, hg)
                yield after[hg]
            yield from (("unhead", 1, 1), ("cdense", 1), ("norm", 3, 1), ("uT", 1, 1))
            yield from (("hidden", i) for i in range(NF))
            yield from (("down", n) for n in range(NT))

        def run(handlers):
            for name, *args in stages():
                if name in handlers:
                    handlers[name](*args)

        def split_no(kind, g=0):
            return {"ck": 0, "q": 1 + 2 * g, "k": 2 + 2 * g, "cq": 5 + g}[kind]

        def score_no(layer, g, u):
            return (24 + 16 * g if layer else 12 * g) + u

        NU = (3, 4)

        def exp_no(layer, g, hg, u):
            return (24 if layer else 0) + NU[layer] * (4 * g + hg) + u

        def head_no(layer, g, hg):
            return 8 * layer + 4 * g + hg

        block = stack.enter_context(nc.Block())

        @block.sync
        def _(sp):
            sp.dma_start(const[:], t["const"]).then_inc(c_loaded.sem, 16)
            sp.dma_start(w_mem[:], t["L0_xattn_W_mem"].rearrange("(c p) e -> p c e", p=P)).then_inc(gate_loaded.sem, 16)
            sp.dma_start(H[:, 0:DC, :],
                         t["L0_xattn_W_gate"].rearrange("(c p) f -> p c f", p=P)).then_inc(gate_loaded.sem, 16)

            def turn(it):
                wait = waiter(sp, it)
                if it > 0:
                    sp.wait_ge(pair_done.sem, it + 1)
                    sp.wait_ge(out_stored.sem, it * out_stored.per)
                sp.dma_start(X[:], x_d[it]).then_inc(x_loaded.sem, 16)
                sp.dma_start(mem[:], ctx_d[it]).then_inc(mem_loaded.sem, 16)
                sp.dma_start(maski[:].rearrange("p b s -> p (b s)"), mask_d[it].partition_broadcast(P)).then_inc(mask_loaded.sem, 16)

                def write(no, g, kind, src, width):
                    wait(parts_ready, no + 1)
                    for c in range(width // P):
                        dst = (self_d if width == D else cross_d)[kind, g][:, P * c:P * c + P, :]
                        sp.dma_start(dst.rearrange("p d t -> d p t"), src(c)).then_inc(scratch_w[no].sem, 16)

                def read(no, g, kind, dst, order, hd, width, signal):
                    n = 16 * (width // P) * (2 if no == 0 else 1)
                    sp.wait_ge(scratch_w[no].sem, it * n + n)
                    src = (self_d if width == D else cross_d)[kind, g]
                    for r, p in enumerate(order):
                        sp.dma_start(dst[hd * r:hd * r + hd], src[p].rearrange("(h d) t -> d h t", d=hd))\
                            .then_inc(signal.sem, 16)

                def split(kind, g):
                    no = split_no("qk"[kind], g)
                    write(no, g, kind, lambda c: parts[:, kind, c, :, S * g:S * g + S], D)

                def stack_self_(g):
                    for kind, dst, order in ((0, Qs[g], SELF_Q), (1, Ks[g], SELF_K)):
                        read(split_no("qk"[kind], g), g, kind, dst, order, HD, D, stack_self[g])

                def rows(layer, g):
                    wait(nm_ready, 2 * layer + g + 1)
                    top = (SELF_ROWS, CROSS_ROWS)[layer]
                    for j in range(2):
                        sp.dma_start(Qs[g][top + j:top + j + 1, :, :], nm_parts[:, g, j:j + 1, :])\
                            .then_inc(max_rows[g].sem, 16)

                def ckv():
                    for g in range(2):
                        write(0, g, 1, lambda c: ck_parts[:, :, S * g:S * g + S], C)

                def stack_cross_(g):
                    write(split_no("cq", g), g, 0, lambda c: cq_parts[:, :, S * g:S * g + S], C)
                    wait(st_psum, exp_no(0, g, 3, 2) + 1)
                    sp.dma_start(Ks[g][CROSS_ROWS:CROSS_ROWS + 2], Ks[g][SELF_ROWS:SELF_ROWS + 2])\
                        .then_inc(stack_cross[g].sem, 16)
                    read(0, g, 1, Ks[g], CROSS_K, CHD, C, stack_cross[g])
                    read(split_no("cq", g), g, 0, Qs[g], CROSS_Q, CHD, C, stack_cross[g])

                def down(n):
                    wait(out_ready, n + 1)
                    sp.dma_start(out_d[it][:, n, :], X[:, n, :]).then_inc(out_stored.sem, 16)

                run({"ckv": ckv, "split": split, "stack_self": stack_self_, "rows": rows,
                     "stack_cross": stack_cross_, "down": down})

            for it in range(2):
                turn(it)
            sp.wait_ge(out_stored.sem, 2 * out_stored.per)

        @block.gpsimd
        def _(pool):
            pool.memset(half[:, 0:2], -0.5).then_inc(consts_ready.sem, 1)
            pool.memset(half[:, 2:4], EPS).then_inc(consts_ready.sem, 1)

            def turn(it):
                wait = waiter(pool, it)

                def norm(k, g):
                    no, cols = 2 * k + g, slice(4 * k + 2 * g, 4 * k + 2 * g + 2)
                    wait(sumsq_ready, 2 * no + 2)
                    pool.tensor_tensor(var[:, cols], sumsq[:, cols], half[:, 2:4], ALU.add)\
                        .then_inc(var_ready.sem, 1)
                    wait(var_ready, no + 1)
                    pool.tensor_tensor(rstd[:, cols], var[:, cols], half[:, 0:2], ALU.pow).then_inc(rstd_ready.sem, 1)

                def fuse():
                    for k in range(2):
                        for g in range(2):
                            norm(k, g)

                def hidden(i):
                    wait(masks_ready, 1)
                    wait(silu_ready, i + 1)
                    if i >= 2:
                        wait(h_ready, i - 1)
                    rows = min(P, FF2 - P * i)
                    m = vm if P * i + rows <= FF else (lm if P * i >= FF else mixm)
                    pool.tensor_tensor(probs[0:rows, 2 + i % 2, :], probs[0:rows, i % 2, :],
                                       m[0:rows].rearrange("p b s -> p (b s)"), ALU.mult)\
                        .then_inc(silu_masked.sem, 1)

                run({"fuse": fuse, "norm": norm, "hidden": hidden})

            pool.wait_ge(consts_ready.sem, N_CONSTS)
            with pool.Fori(0, 2) as it:
                turn(it)

        @block.scalar
        def _(act):
            for name, at in (("L0_xattn_norm_w", norm_w[:, 0]), ("L1_xattn_ln_in_w", norm_w[:, 1]),
                             ("L1_xattn_ln_post_cross_w", norm_w[:, 2]), ("L1_xattn_ln_post_attn_w", norm_w[:, 3]),
                             ("L0_xattn_b_gate", b_gate[:])):
                act.dma_start(at, t[name].partition_broadcast(P)).then_inc(vec_loaded.sem, 16)
            act.dma_start(posi[:], t["pos_1xS"][0].partition_broadcast(P)).then_inc(pos_loaded.sem, 16)
            act.dma_start(ckv_w[:], t["L1_xattn_ckv_w"]).then_inc(cross_loaded.sem, 16)
            act.dma_start(cq_w[:], t["L1_xattn_cq_w"].rearrange("(c p) e -> p c e", p=P)).then_inc(cross_loaded.sem, 16)
            act.dma_start(cdense[:], t["L1_xattn_cdense_w"]).then_inc(cross_loaded.sem, 16)
            for e, n in enumerate("vl"):
                act.dma_start(qkv[:, e], t[f"L1_xattn_{n}_qkv"].rearrange("(c p) n -> p c n", p=P)).then_inc(qkv_loaded.sem, 16)
            for e, n in enumerate("vl"):
                act.dma_start(dense[:, e], t[f"L1_xattn_{n}_dense"].rearrange("(c p) n -> p c n", p=P)).then_inc(dense_loaded.sem, 16)
            for k, w in enumerate(("gate", "up")):
                for e, n in enumerate("vl"):
                    act.dma_start(w_up[:, k, :, FF * e:FF * e + FF],
                                  t[f"L1_xattn_{n}_{w}"].rearrange("(c p) n -> p c n", p=P)).then_inc(mlp_loaded.sem, 16)
            full = FF // P
            edge = FF - full * P
            rest_l = (FF2 - (full + 1) * P) // P
            wv, wl = t["L1_xattn_v_down"], t["L1_xattn_l_down"]
            act.dma_start(w_down[:, 0:full, :], wv[0:full * P].rearrange("(c p) n -> p c n", p=P)).then_inc(mlp_loaded.sem, 16)
            act.dma_start(w_down[0:edge, full, :], wv[full * P:FF]).then_inc(mlp_loaded.sem, 16)
            act.dma_start(w_down[edge:P, full, :], wl[0:P - edge]).then_inc(mlp_loaded.sem, 16)
            act.dma_start(w_down[:, full + 1:full + 1 + rest_l, :],
                          wl[P - edge:P - edge + rest_l * P].rearrange("(c p) n -> p c n", p=P)).then_inc(mlp_loaded.sem, 16)
            last = FF2 - (NF - 1) * P
            act.dma_start(w_down[0:last, NF - 1, :], wl[FF - last:FF]).then_inc(mlp_loaded.sem, 16)

            def turn(it):
                wait = waiter(act, it)

                def xT():
                    for c in range(DC):
                        wait(xT_psum, c + 1)
                        nc.scalar.copy(UT[:, :, c, :], bank[c][:].rearrange("p (g s) -> p g s", g=2))\
                            .then_inc(xT_ready.sem, 1)

                def y():
                    wait(y_psum, 1)
                    nc.scalar.copy(yT[:], bank[3][:]).then_inc(y_ready.sem, 1)

                def first(no, dst, src, scale):
                    wait(split_psum, no + 1)
                    nc.scalar.activation(dst, src, ACT.Copy, scale=scale).then_inc(first_part.sem, 1)

                def ckv():
                    first(0, ck_parts[:, 0, :], bank[4][:], 1.0)
                    wait(cv_psum, 1)
                    nc.scalar.copy(Vc[:].rearrange("p n h w -> p (n h) w")[:, :, 0:CHD],
                                   bank[5][:].rearrange("p (h w) -> p h w", w=CHD)).then_inc(cv_ready.sem, 1)

                def scores0():
                    for n in range(NT):
                        wait(nm0_ready, n // 2 + 1)
                        nc.scalar.activation(normed[:, n, :], bank[6 + n // 2][:, S * (n % 2):S * (n % 2) + S],
                                             ACT.Exp, bias=nm0[:, n:n + 1], scale=float(D) ** -0.5,
                                             accum_out=l0[:, n:n + 1]).then_inc(e0_ready.sem, 1)

                def probsT():
                    for g in range(2):
                        wait(pT_psum, g + 1)
                        nc.scalar.copy(TV[:, g].rearrange("p c s -> p (c s)"), bank[g][:]).then_inc(pT_ready.sem, 1)

                def square(k, n):
                    wait(fused, 4 * k + n + 1)
                    if k > 0:
                        wait(sumsq_ready, 4 * k + n - 3)
                    nc.scalar.activation(QR[:, n, 0:D] if k < 2 else gated[:, n, :], X[:, n, :], ACT.Square, scale=float(D) ** -0.5,
                                         accum_out=sumsq[:, 4 * k + n:4 * k + n + 1]).then_inc(sumsq_ready.sem, 1)

                def fuse():
                    for n in range(NT):
                        wait(pre_gate, n + 1)
                        nc.scalar.activation(gated[:, n, :], gated[:, n, :], ACT.Sigmoid).then_inc(gate_ready.sem, 1)
                    for k in range(2):
                        for n in range(NT):
                            square(k, n)

                def norm(k, g):
                    square(k, 2 * g)
                    square(k, 2 * g + 1)

                def qkv_(g):
                    wait(v_psum, g + 1)
                    nc.scalar.copy(V[:, 2 * g:2 * g + 2].rearrange("p n h w -> p (n h) w")[:, :, 0:HD],
                                   bank[6 + g][:].rearrange("p (h w) -> p h w", w=HD)).then_inc(v_ready.sem, 1)

                def split(kind, g):
                    first(split_no("qk"[kind], g), parts[:, kind, :, 0, S * g:S * g + S],
                          bank[2 * g + kind][:].rearrange("p (c s) -> p c s", c=DC), (float(HD) ** -0.5, 1.0)[kind])

                def rows(layer, g):
                    no = 2 * layer + g
                    wait(nm_psum, no + 1)
                    if no >= 2:
                        act.wait_ge(max_rows[g].sem, it * max_rows[g].per + 32)
                    nc.scalar.copy(nm_parts[:, g, 0, :], bank[6][0:NH, 0:S]).then_inc(nm_hi.sem, 1)

                def attend(layer, g, hg):
                    for u in range(NU[layer]):
                        no = exp_no(layer, g, hg, u)
                        wait(st_psum, no + 1)
                        if no >= RING:
                            wait(pv_psum, pv_of(no - RING) + 1)
                        nc.scalar.activation(probs[:, no % RING, :], bank[2 + no % 2][:], ACT.Exp).then_inc(e_ready.sem, 1)

                def pv_of(no):
                    if no < 24:
                        return no // 3
                    return 8 + (no - 24) // 4

                def uT(which, g):
                    no = 2 * which + g
                    wait(uT_psum, no + 1)
                    nc.scalar.copy(UT[:, g].rearrange("p c s -> p (c s)"), bank[6][:]).then_inc(uT_ready.sem, 1)

                def cq(g):
                    first(split_no("cq", g), cq_parts[:, 0, S * g:S * g + S], bank[7][:, 0:S], float(np.float32(1.0 / np.sqrt(CHD))))

                def cdense_(g):
                    wait(cT_psum, 2 + g + 1)
                    nc.scalar.copy(yT[:, S * g:S * g + S], bank[6][:, 0:S]).then_inc(cT_ready.sem, 1)

                def hidden(i):
                    wait(gu_psum, 2 * i + 1)
                    if i >= 2:
                        wait(silu_masked, i - 1)
                    else:
                        wait(pv_psum, 16)
                    rows = min(P, FF2 - P * i)
                    nc.scalar.activation(probs[0:rows, i % 2, :], bank[2 * (i % 3)][0:rows, :], ACT.Silu)\
                        .then_inc(silu_ready.sem, 1)

                run({"xT": xT, "y": y, "ckv": ckv, "scores0": scores0, "probsT": probsT, "fuse": fuse,
                     "norm": norm, "qkv": qkv_, "split": split, "rows": rows, "attend": attend, "uT": uT,
                     "cq": cq, "cdense": cdense_, "hidden": hidden})

            act.wait_ge(prep_ready.sem, 4)
            with act.Fori(0, 2) as it:
                act.wait_ge(pair_done.sem, it + 1)
                turn(it)

        @block.vector
        def _(dve):
            steps = [0]

            def pre(ins):
                steps[0] += 1
                ins.then_inc(pre_step.sem, 1)
                dve.wait_ge(pre_step.sem, steps[0])

            for g in range(2):
                dve.memset(Ks[g][SELF_ROWS:SELF_ROWS + 2], 1.0).then_inc(consts_ready.sem, 1)
            for v in (V, Vc):
                pre(dve.memset(v[:], 0.0))
                dve.memset(v[:].rearrange("p n h w -> p (n h) w")[:, :, HD:HD + 1], 1.0).then_inc(consts_ready.sem, 1)
            dve.memset(vm[:], 0.0).then_inc(consts_ready.sem, 1)
            dve.wait_ge(c_loaded.sem, 16)
            dve.tensor_copy(bconst[:], const[:, 0:3 * P]).then_inc(consts_ready.sem, 1)
            dve.wait_ge(pos_loaded.sem, 16)
            pos, wrap = gated[:, 0, :], gated[:, 1, :]
            pre(dve.tensor_copy(pos, posi[:]))
            pre(dve.tensor_scalar(wrap, pos, 0.0, float(S), ALU.is_lt, ALU.mult))
            pre(dve.tensor_tensor(pos, pos, wrap, ALU.add))
            pre(dve.tensor_scalar(pos, pos, 0.0, float(S - 1), ALU.max, ALU.min))
            for c in range(2):
                dve.tensor_scalar(normed[:, c, :], pos, const[:, C_T + c:C_T + c + 1], None, ALU.is_equal)\
                    .then_inc(onehot_ready.sem, 1)
            dve.wait_ge(trig_psum.sem, 1)
            dve.tensor_copy(trig[:].rearrange("p n w -> p (n w)"), bank[0][:, 0:4 * HD]).then_inc(prep_ready.sem, 1)
            dve.wait_ge(prep_psum.sem, 1)
            dve.tensor_copy(w_gateT[:].rearrange("p c d -> p (c d)"), bank[1][:]).then_inc(prep_ready.sem, 1)
            dve.tensor_copy(gated[:, 2:4, :].rearrange("p c d -> p (c d)"), bank[2][:]).then_inc(prep_ready.sem, 1)
            dve.tensor_copy(w_memT[:], bank[3][:, 0:D]).then_inc(prep_ready.sem, 1)
            dve.wait_ge(prep_psum.sem, 2)
            dve.tensor_copy(w_gatem[:], bank[4][:, 0:D]).then_inc(prep_ready.sem, 1)
            dve.wait_ge(vec_loaded.sem, 5 * 16)
            dve.wait_ge(prep_ready.sem, 5)

            def turn(it):
                wait = waiter(dve, it)
                chain = [0]

                def step(ins):
                    chain[0] += 1
                    ins.then_inc(v_step.sem, 1)
                    wait(v_step, chain[0])

                def masks():
                    wait(mask_loaded, 16)
                    step(dve.tensor_scalar(is_one[:], maski[:], 1.0, None, ALU.is_equal))
                    step(dve.tensor_tensor(vm[:, :, 0:S - 1], is_one[:, :, 0:S - 1], is_one[:, :, 1:S], ALU.mult))
                    dve.tensor_scalar(lm[:], vm[:], -1.0, 1.0, ALU.mult, ALU.add).then_inc(v_step.sem, 1)
                    chain[0] += 1
                    dve.tensor_scalar(mixm[:], vm[:], const[:, C_MIX:C_MIX + 1], const[:, C_MIX + 1:C_MIX + 2],
                                      ALU.mult, ALU.add).then_inc(masks_ready.sem, 1)

                def memT_():
                    wait(memT_psum, 1)
                    dve.tensor_copy(memT[:], bank[2][:]).then_inc(memT_ready.sem, 1)

                def split_rest(no, parts_of, src, scale, left):
                    wait(first_part, no + 1)
                    step(dve.scalar_tensor_tensor(left, src, scale, parts_of(0), ALU.mult, ALU.subtract))
                    step(dve.tensor_copy(parts_of(1), left))
                    dve.tensor_tensor(parts_of(2), left, parts_of(1), ALU.subtract).then_inc(parts_ready.sem, 1)

                def ckv():
                    split_rest(0, lambda p: ck_parts[:, p, :], bank[4][:], 1.0, rest[:])

                def scores0():
                    for g in range(2):
                        wait(s0_psum, g + 1)
                        step(dve.tensor_reduce(nm0[:, 2 * g:2 * g + 2], bank[6 + g][:].rearrange("p (n s) -> p n s", n=2),
                                               AX_X, ALU.max, negate=True))
                        dve.tensor_scalar(nm0[:, 2 * g:2 * g + 2], nm0[:, 2 * g:2 * g + 2], float(D) ** -0.5, None,
                                          ALU.mult).then_inc(nm0_ready.sem, 1)
                    for n in range(NT):
                        wait(e0_ready, n + 1)
                        step(dve.reciprocal(r0[:, n:n + 1], l0[:, n:n + 1]))
                        dve.tensor_scalar(normed[:, n, :], normed[:, n, :], r0[:, n:n + 1], None, ALU.mult)\
                            .then_inc(p0_ready.sem, 1)

                def am():
                    for g in range(2):
                        wait(am_psum, g + 1)
                        dve.tensor_copy(TL[:, g, 0, :], bank[2 + g][:, 0:S]).then_inc(am_ready.sem, 1)

                def scale_norm(k, n, dst, signal):
                    wait(rstd_ready, 2 * k + n // 2 + 1)
                    col = 4 * k + n
                    dve.scalar_tensor_tensor(dst, X[:, n, :], rstd[:, col:col + 1], norm_w[:, k, :],
                                             ALU.mult, ALU.mult).then_inc(signal.sem, 1)

                def fuse():
                    for n in range(NT):
                        wait(gate_psum, n + 1)
                        dve.tensor_tensor(gated[:, n, :], bank[4 + n][:, 0:D], b_gate[:], ALU.add)\
                            .then_inc(pre_gate.sem, 1)
                    for n in range(NT):
                        wait(gate_ready, n + 1)
                        step(dve.tensor_tensor(gated[:, n, :], bank[4 + n][:, D:2 * D], gated[:, n, :], ALU.mult))
                        dve.tensor_tensor(X[:, n, :], X[:, n, :], gated[:, n, :], ALU.add).then_inc(fused.sem, 1)
                    for n in range(NT):
                        scale_norm(0, n, X[:, n, :], fused)
                    for n in range(NT):
                        wait(fused, 4 + n + 1)
                        scale_norm(1, n, normed[:, n, :], normed_ready)

                def masked(psum, g, signal):
                    src = psum[:].rearrange("p (c s) -> p c s", c=DC)
                    for m, dst in ((vm, TV), (lm, TL)):
                        ins = dve.tensor_tensor(dst[:, g], src, m[:, g:g + 1, :].to_broadcast([P, DC, S]), ALU.mult)
                    ins.then_inc(signal.sem, 1)

                def normT(g):
                    wait(nT_psum, g + 1)
                    masked(bank[g], g, nT_ready)

                def qkv_(g):
                    for n in (2 * g, 2 * g + 1):
                        wait(qk_psum, n + 1)
                        qk = bank[2 + n][:].rearrange("p (h w) -> p h w", w=HD)
                        tab = trig[:, n % 2, :]
                        cos = tab[:, 0:HD].rearrange("p (o w) -> p o w", o=1).to_broadcast([P, 2 * NH, HD])
                        sin = tab[:, HD:2 * HD].rearrange("p (o w) -> p o w", o=1)
                        a = gated[:, 0:2, :].rearrange("p c (h w) -> p (c h) w", w=HD)
                        b = gated[:, 2:4, :].rearrange("p c (h w) -> p (c h) w", w=HD)
                        hw = HD // 2
                        dve.tensor_tensor(a, qk, cos, ALU.mult)
                        dve.tensor_tensor(b[:, :, 0:hw], qk[:, :, hw:HD], sin[:, :, 0:hw].to_broadcast([P, 2 * NH, hw]), ALU.mult)
                        step(dve.tensor_tensor(b[:, :, hw:HD], qk[:, :, 0:hw], sin[:, :, hw:HD].to_broadcast([P, 2 * NH, hw]), ALU.mult))
                        ins = dve.tensor_tensor(QR[:, n, :].rearrange("p (h w) -> p h w", w=HD), a, b, ALU.add)
                        ins.then_inc(qr_ready.sem, 1)
                        wait(qr_ready, n + 1)

                def split(kind, g):
                    split_rest(split_no("qk"[kind], g), lambda p: parts[:, kind, :, p, S * g:S * g + S],
                               bank[2 * g + kind][:].rearrange("p (c s) -> p c s", c=DC),
                               (float(HD) ** -0.5, 1.0)[kind], rest[:].rearrange("p (c s) -> p c s", c=DC))
                    wait(parts_ready, split_no("qk"[kind], g) + 1)

                def scores(layer, g, u):
                    no = score_no(layer, g, u)
                    wait(s_psum, no + 1)
                    if layer == 0 and u < 4:
                        src, dst = bank[no % 2][:].rearrange("p (h k) -> p h k", h=4), negmax[:, g, 0, 4 * u:4 * u + 4]
                    elif layer == 0:
                        v = u - 4
                        src, dst = bank[no % 2][:].rearrange("p (h k) -> p h k", h=2), negmax[:, g, 1, 2 * v:2 * v + 2]
                    else:
                        v = u % 8
                        src, dst = bank[no % 2][:].rearrange("p (h k) -> p h k", h=2), negmax[:, g, u // 8, 2 * v:2 * v + 2]
                    dve.tensor_reduce(dst, src, AX_X, ALU.max, negate=True).then_inc(max_ready.sem, 1)

                def rows(layer, g):
                    no = 2 * layer + g
                    wait(nm_hi, no + 1)
                    dve.tensor_tensor(nm_parts[:, g, 1, :], bank[6][0:NH, 0:S], nm_parts[:, g, 0, :], ALU.subtract)\
                        .then_inc(nm_ready.sem, 1)

                def attend(layer, g, hg):
                    no = head_no(layer, g, hg)
                    wait(pv_psum, no + 1)
                    if no >= 4:
                        wait(hT_psum, 2 * (no // 4))
                    dve.tensor_copy(heads[:, hg, :], bank[4 + no % 2][:, 0:S]).then_inc(heads_ready.sem, 1)

                def unhead(layer, g):
                    w = (HD, CHD)[layer]
                    for j in range(2):
                        no = 4 * layer + 2 * g + j
                        wait(hT_psum, no + 1)
                        src = bank[6 + j][:].rearrange("p (h w) -> p h w", w=VW)
                        step(dve.reciprocal(rsum[:].rearrange("p (h o) -> p h o", o=1), src[:, :, HD:HD + 1]))
                        dst = normed[:, 2 * g + j, 0:NH * w].rearrange("p (h w) -> p h w", w=w)
                        dve.tensor_tensor(dst, src[:, :, 0:w],
                                          rsum[:].rearrange("p (h o) -> p h o", o=1).to_broadcast([P, NH, w]), ALU.mult)\
                            .then_inc(ctx_ready.sem, 1)
                        wait(ctx_ready, no + 1)

                def ctxT(g):
                    wait(cT_psum, g + 1)
                    masked(bank[6], g, cT_ready)

                def add(k, no, g):
                    wait(proj_psum, no + 1)
                    x = X[:, 2 * g:2 * g + 2, :].rearrange("p n d -> p (n d)")
                    dve.tensor_tensor(x, bank[7][:], x, ALU.add).then_inc(fused.sem, 2)

                def norm(k, g):
                    for n in (2 * g, 2 * g + 1):
                        wait(fused, 4 * k + 2 * g + 2)
                        scale_norm(k, n, normed[:, n, :], normed_ready)

                def cq(g):
                    split_rest(split_no("cq", g), lambda p: cq_parts[:, p, S * g:S * g + S], bank[7][:, 0:S],
                               float(np.float32(1.0 / np.sqrt(CHD))), rest[:, 0:S])
                    wait(parts_ready, split_no("cq", g) + 1)

                def hidden(i):
                    rows = min(P, FF2 - P * i)
                    wait(silu_masked, i + 1)
                    wait(gu_psum, 2 * i + 2)
                    dve.tensor_tensor(H[0:rows, i, :], bank[2 * (i % 3) + 1][0:rows, :], probs[0:rows, 2 + i % 2, :],
                                      ALU.mult).then_inc(h_ready.sem, 1)

                def down(n):
                    wait(down_psum, n + 1)
                    dve.tensor_tensor(X[:, n, :], bank[(6, 7, 0, 1)[n]][:, 0:D], X[:, n, :], ALU.add)\
                        .then_inc(out_ready.sem, 1)
                    if n == NT - 1:
                        wait(out_ready, NT)
                        dve.sem_inc(pair_done.sem, 1)

                run({"masks": masks, "memT": memT_, "ckv": ckv, "scores0": scores0, "am": am, "fuse": fuse,
                     "normT": normT, "qkv": qkv_, "split": split, "scores": scores, "rows": rows,
                     "attend": attend, "unhead": unhead, "ctxT": ctxT, "dense": lambda g: add(2, g, g),
                     "norm": norm, "cq": cq, "cdense": lambda g: add(3, 2 + g, g), "hidden": hidden, "down": down})
                assert chain[0] == V_STEPS, chain[0]

            dve.sem_inc(pair_done.sem, 1)
            with dve.Fori(0, 2) as it:
                dve.wait_ge(pair_done.sem, it + 1)
                turn(it)

        @block.tensor
        def _(pe):
            def mm(out, lhsT, rhs, start, stop, **kw):
                return nc.tensor.matmul(out, lhsT, rhs, start=start, stop=stop, **kw)

            pe.wait_ge(c_loaded.sem, 16)
            pe.wait_ge(gate_loaded.sem, 32)
            for h in range(2):
                for c in range(DC):
                    for r in range(DC):
                        nc.tensor.transpose(bank[1 + h][:, D * c + P * r:D * c + P * r + P],
                                            H[:, r, D * h + P * c:D * h + P * c + P], ident)
            for c in range(DC):
                last = nc.tensor.transpose(bank[3][:, P * c:P * c + P], w_mem[:, c, :], ident)
            last.then_inc(prep_psum.sem, 1)
            pe.wait_ge(onehot_ready.sem, 2)
            for n in range(2):
                for c in range(2):
                    last = mm(bank[0][:, 2 * HD * n:2 * HD * n + 2 * HD], normed[:, c, P * n:P * n + P],
                              const[:, C_TAB + 2 * HD * c:C_TAB + 2 * HD * c + 2 * HD], c == 0, c == 1)
            last.then_inc(trig_psum.sem, 1)
            pe.wait_ge(prep_ready.sem, 3)
            for c in range(DC):
                last = mm(bank[4][:, 0:D], w_mem[:, c, :], gated[:, 2 + c, :], c == 0, c == DC - 1)
            last.then_inc(prep_psum.sem, 1)
            pe.wait_ge(prep_ready.sem, 5)
            pe.wait_ge(consts_ready.sem, N_CONSTS)

            def turn(it):
                wait = waiter(pe, it)
                reader = {}

                def claim(b, signal=None, n=0):
                    if b in reader and reader[b][0] is not None:
                        wait(*reader[b])
                    reader[b] = (signal, n)

                def tile(w, n):
                    return lambda c: w[:, n // 2, c, P * (n % 2):P * (n % 2) + P]

                def xT():
                    wait(x_loaded, 16)
                    for c in range(DC):
                        claim(c, xT_ready, c + 1)
                        for n in range(NT):
                            last = nc.tensor.transpose(bank[c][:, P * n:P * n + P], X[:, n, P * c:P * c + P], ident)
                        last.then_inc(xT_psum.sem, 1)

                def memT_():
                    wait(mem_loaded, 16)
                    claim(2, memT_ready, 1)
                    for n in range(NT):
                        last = nc.tensor.transpose(bank[2][:, P * n:P * n + P], mem[:, n, :], ident)
                    last.then_inc(memT_psum.sem, 1)

                def y():
                    wait(xT_ready, 2)
                    claim(3, y_ready, 1)
                    for c in range(DC):
                        last = mm(bank[3][:].rearrange("p (g s) -> p g s", g=2), w_mem[:, c, :], UT[:, :, c, :], c == 0, c == DC - 1)
                    last.then_inc(y_psum.sem, 1)

                def ckv():
                    wait(memT_ready, 1)
                    pe.wait_ge(cross_loaded.sem, 48)
                    claim(4, parts_ready, 1)
                    mm(bank[4][:], ckv_w[:, 0:C], memT[:], True, True).then_inc(split_psum.sem, 1)
                    claim(5, cv_ready, 1)
                    for n in range(NT):
                        last = mm(bank[5][:, C * n:C * n + C], memT[:, P * n:P * n + P], ckv_w[:, C:2 * C], True, True)
                    last.then_inc(cv_psum.sem, 1)

                def scores0():
                    wait(y_ready, 1)
                    for g in range(2):
                        claim(6 + g, e0_ready, 2 * g + 2)
                        for n in (2 * g, 2 * g + 1):
                            last = mm(bank[6 + g][:, S * (n % 2):S * (n % 2) + S], yT[:, P * n:P * n + P],
                                      memT[:, S * g:S * g + S], True, True)
                        last.then_inc(s0_psum.sem, 1)

                def gate_x(g):
                    for n in (2 * g, 2 * g + 1):
                        claim(4 + n, fused, n + 1)
                        for c in range(DC):
                            mm(bank[4 + n][:, 0:D], tile(UT, n)(c), w_gateT[:, c, :], c == 0, False)

                def probsT():
                    for g in range(2):
                        claim(g, pT_ready, g + 1)
                        for n in (2 * g, 2 * g + 1):
                            wait(p0_ready, n + 1)
                            for k in range(2):
                                last = nc.tensor.transpose(bank[g][:, S * k + P * (n % 2):S * k + P * (n % 2) + P],
                                                           normed[:, n, P * k:P * k + P], ident)
                        last.then_inc(pT_psum.sem, 1)

                def am():
                    for g in range(2):
                        wait(pT_ready, g + 1)
                        claim(2 + g, am_ready, g + 1)
                        for k in range(2):
                            last = mm(bank[2 + g][:, 0:S], mem[:, 2 * g + k, :], TV[:, g, k, :], k == 0, k == 1)
                        last.then_inc(am_psum.sem, 1)

                def gate_m():
                    for n in range(NT):
                        wait(am_ready, n // 2 + 1)
                        a = tile(TL, n)(0)
                        mm(bank[4 + n][:, 0:D], a, w_gatem[:], False, True)
                        mm(bank[4 + n][:, D:2 * D], a, w_memT[:], True, True).then_inc(gate_psum.sem, 1)

                def transposed(b, g, width, cols, signal):
                    for c in range(width // P):
                        for j in range(2):
                            last = nc.tensor.transpose(bank[b][:, S * c + P * j:S * c + P * j + P],
                                                       normed[:, 2 * g + j, P * c:P * c + P], ident)
                    last.then_inc(signal.sem, 1)

                def normT(g):
                    wait(normed_ready, 2 * g + 2)
                    claim(g, nT_ready, g + 1)
                    transposed(g, g, D, None, nT_psum)

                def experts(out, n, w, cols):
                    for e, src in enumerate((TV, TL)):
                        for c in range(DC):
                            last = mm(out, tile(src, n)(c), w[:, e, c, cols], e == 0 and c == 0, e == 1 and c == DC - 1)
                    return last

                def qkv_(g):
                    pe.wait_ge(qkv_loaded.sem, 32)
                    wait(nT_ready, g + 1)
                    claim(6 + g, v_ready, g + 1)
                    for n in (2 * g, 2 * g + 1):
                        claim(2 + n, qr_ready, n + 1)
                        experts(bank[2 + n][:], n, qkv, slice(0, 2 * D)).then_inc(qk_psum.sem, 1)
                        last = experts(bank[6 + g][:, S * (n % 2):S * (n % 2) + D], n, qkv, slice(2 * D, 3 * D))
                    last.then_inc(v_psum.sem, 1)

                def split(kind, g):
                    wait(qr_ready, 2 * g + 2)
                    b = 2 * g + kind
                    claim(b, parts_ready, split_no("qk"[kind], g) + 1)
                    for c in range(DC):
                        for j in range(2):
                            col = D * kind + P * c
                            last = nc.tensor.transpose(bank[b][:, S * c + P * j:S * c + P * j + P],
                                                       QR[:, 2 * g + j, col:col + P], ident)
                    last.then_inc(split_psum.sem, 1)

                def scores(layer, g, u):
                    no = score_no(layer, g, u)
                    b = no % 2
                    claim(b, max_ready, no + 1)
                    if layer == 0:
                        wait(stack_self[g], stack_self[g].per)
                        q, k = Qs[g][0:SELF_ROWS], Ks[g][0:SELF_ROWS]
                        if u < 4:
                            for j in range(4):
                                mm(bank[b][:, P * j:P * j + P], q[:, 4 * u + j, 0:P], k[:, 4 * u + j, 0:P],
                                   j == 0, False, skip_group_check=True)
                            last = mm(bank[b][:].rearrange("p (h k) -> p h k", h=4), identb,
                                      maskq.rearrange("p (o k) -> p o k", o=1).to_broadcast([P, 4, P]),
                                      False, True, skip_group_check=True)
                        else:
                            for j in range(2):
                                h = 2 * (u - 4) + j
                                mm(bank[b][:, S * j:S * j + S], q[:, h, P:S], k[:, h, :], j == 0, False, skip_group_check=True)
                            last = mm(bank[b][:].rearrange("p (h k) -> p h k", h=2)[:, :, P:S], identb,
                                      maskq.rearrange("p (o k) -> p o k", o=1).to_broadcast([P, 2, P]),
                                      False, True, skip_group_check=True)
                    else:
                        wait(stack_cross[g], stack_cross[g].per)
                        q, k = Qs[g][0:CROSS_ROWS], Ks[g][0:CROSS_ROWS]
                        for j in range(2):
                            h = 2 * (u % 8) + j
                            last = mm(bank[b][:, S * j:S * j + S], q[:, h, P * (u // 8):P * (u // 8) + P], k[:, h, :],
                                      j == 0, j == 1, skip_group_check=True)
                    last.then_inc(s_psum.sem, 1)

                def rows(layer, g):
                    wait(max_ready, score_no(layer, g, (12, 16)[layer]))
                    claim(6, nm_ready, 2 * layer + g + 1)
                    for j in range(2):
                        last = nc.tensor.transpose(bank[6][0:NH, P * j:P * j + P], negmax[:, g, j, :], ident)
                    last.then_inc(nm_psum.sem, 1)

                def attend(layer, g, hg):
                    if hg == 0:
                        values(layer, g, -1)
                    wait(max_rows[g], 32 * layer + 32)
                    top = (SELF_ROWS, CROSS_ROWS)[layer] + 2
                    q, k = Qs[g][0:top], Ks[g][0:top]
                    for u in range(NU[layer]):
                        no = exp_no(layer, g, hg, u)
                        b = 2 + no % 2
                        claim(b, e_ready, no + 1)
                        if layer == 0 and u < 2:
                            for j in range(2):
                                h = 4 * hg + 2 * u + j
                                mm(bank[b][:, S * j:S * j + S], k[:, h, 0:P], q[:, h, :], j == 0, False, skip_group_check=True)
                            last = mm(bank[b][:].rearrange("p (h q) -> p h q", h=2)[:, :, 0:P], identb,
                                      maskk.rearrange("p (o k) -> p o k", o=1).to_broadcast([P, 2, P]),
                                      False, True, skip_group_check=True)
                        elif layer == 0:
                            for j in range(4):
                                h = 4 * hg + j
                                mm(bank[b][:, P * j:P * j + P], k[:, h, P:S], q[:, h, P:S], j == 0, False, skip_group_check=True)
                            last = mm(bank[b][:].rearrange("p (h q) -> p h q", h=4), identb,
                                      maskk.rearrange("p (o k) -> p o k", o=1).to_broadcast([P, 4, P]),
                                      False, True, skip_group_check=True)
                        else:
                            for j in range(2):
                                h = 4 * hg + 2 * (u % 2) + j
                                last = mm(bank[b][:, S * j:S * j + S], k[:, h, P * (u // 2):P * (u // 2) + P], q[:, h, :],
                                          j == 0, j == 1, skip_group_check=True)
                        last.then_inc(st_psum.sem, 1)
                    if hg > 0:
                        values(layer, g, hg - 1)
                    if hg == 3:
                        values(layer, g, 3)

                def values(layer, g, hg):
                    if hg < 0:
                        return
                    no = head_no(layer, g, hg)
                    b = 4 + no % 2
                    wait(e_ready, exp_no(layer, g, hg, NU[layer]))
                    claim(b, heads_ready, no + 1)
                    v = (V, Vc)[layer]
                    first = exp_no(layer, g, hg, 0)
                    for k in range(2):
                        for j in range(4):
                            lhsT = v[:, 2 * g + k, 4 * hg + j, :]
                            if layer == 0 and k == 1:
                                rhs = probs[:, (first + 2) % RING, P * j:P * j + P]
                                out = bank[b][VW * j:VW * j + VW, P:S]
                            else:
                                rhs = probs[:, (first + 2 * k + j // 2) % RING, S * (j % 2):S * (j % 2) + S]
                                out = bank[b][VW * j:VW * j + VW, 0:S]
                            last = mm(out, lhsT, rhs, k == 0, k == 1, skip_group_check=True)
                    last.then_inc(pv_psum.sem, 1)

                def unhead(layer, g):
                    wait(heads_ready, 8 * layer + 4 * g + 4)
                    for j in range(2):
                        no = 4 * layer + 2 * g + j
                        claim(6 + j, ctx_ready, no + 1)
                        for hg in range(4):
                            last = nc.tensor.transpose(bank[6 + j][:, P * hg:P * hg + P], heads[:, hg, P * j:P * j + P], ident)
                        last.then_inc(hT_psum.sem, 1)

                def ctxT(g):
                    wait(ctx_ready, 2 * g + 2)
                    claim(6, cT_ready, g + 1)
                    transposed(6, g, D, None, cT_psum)

                def dense_(g):
                    pe.wait_ge(dense_loaded.sem, 32)
                    wait(cT_ready, g + 1)
                    claim(7, fused, 8 + 2 * g + 2)
                    for n in (2 * g, 2 * g + 1):
                        last = experts(bank[7][:, D * (n % 2):D * (n % 2) + D], n, dense, slice(0, D))
                    last.then_inc(proj_psum.sem, 1)

                def uT(which, g):
                    wait(normed_ready, 4 + 4 * which + 2 * g + 2)
                    claim(6, uT_ready, 2 * which + g + 1)
                    transposed(6, g, D, None, uT_psum)

                def cq(g):
                    wait(uT_ready, g + 1)
                    claim(7, parts_ready, split_no("cq", g) + 1)
                    for c in range(DC):
                        last = mm(bank[7][:, 0:S], cq_w[:, c, :], UT[:, g, c, :], c == 0, c == DC - 1)
                    last.then_inc(split_psum.sem, 1)

                def cdense_(g):
                    wait(ctx_ready, 4 + 2 * g + 2)
                    claim(6, cT_ready, 2 + g + 1)
                    transposed(6, g, C, None, cT_psum)
                    wait(cT_ready, 2 + g + 1)
                    claim(7, fused, 12 + 2 * g + 2)
                    for n in (2 * g, 2 * g + 1):
                        last = mm(bank[7][:, D * (n % 2):D * (n % 2) + D], yT[:, P * n:P * n + P], cdense[:], True, True)
                    last.then_inc(proj_psum.sem, 1)

                def hidden(i):
                    if i == 0:
                        pe.wait_ge(mlp_loaded.sem, 9 * 16)
                        wait(uT_ready, 4)
                    rows = min(P, FF2 - P * i)
                    for k in range(2):
                        b = 2 * (i % 3) + k
                        claim(b, (silu_ready, h_ready)[k], i + 1)
                        for c in range(DC):
                            last = mm(bank[b][0:rows, :].rearrange("p (g s) -> p g s", g=2),
                                      w_up[:, k, c, P * i:P * i + rows], UT[:, :, c, :], c == 0, c == DC - 1)
                        last.then_inc(gu_psum.sem, 1)

                def down(n):
                    b = (6, 7, 0, 1)[n]
                    claim(b)
                    for i in range(NF):
                        wait(h_ready, i + 1)
                        rows = min(P, FF2 - P * i)
                        last = mm(bank[b][:, 0:D], H[0:rows, i, P * n:P * n + P], w_down[0:rows, i, :], i == 0, i == NF - 1)
                    last.then_inc(down_psum.sem, 1)

                run({"xT": xT, "memT": memT_, "y": y, "ckv": ckv, "scores0": scores0, "gate_x": gate_x,
                     "probsT": probsT, "am": am, "gate_m": gate_m, "normT": normT, "qkv": qkv_, "split": split,
                     "scores": scores, "rows": rows, "attend": attend, "unhead": unhead, "ctxT": ctxT,
                     "dense": dense_, "uT": uT, "cq": cq, "cdense": cdense_, "hidden": hidden, "down": down})

            with pe.Fori(0, 2) as it:
                pe.wait_ge(pair_done.sem, it + 1)
                turn(it)


V_STEPS = 39
N_CONSTS = 8

_INS = ["x", "ctx_1024", "pos_1xS", "mask_BxS_ik0", "L0_xattn_W_mem", "L0_xattn_W_gate", "L0_xattn_b_gate",
        "L0_xattn_norm_w", "L1_xattn_ln_in_w", "L1_xattn_ln_post_attn_w", "L1_xattn_ln_post_cross_w",
        "L1_xattn_v_qkv", "L1_xattn_l_qkv", "L1_xattn_v_dense", "L1_xattn_l_dense", "L1_xattn_cq_w",
        "L1_xattn_ckv_w", "L1_xattn_cdense_w", "L1_xattn_v_gate", "L1_xattn_v_up", "L1_xattn_v_down",
        "L1_xattn_l_gate", "L1_xattn_l_up", "L1_xattn_l_down"]


def kernel(**inputs):
    import concourse.bacc as bacc
    from concourse.bass_utils import run_bass_kernel_spmd

    nc = bacc.Bacc("TRN2", target_bir_lowering=False, num_devices=1)
    arrays, tensors = {}, {}
    named = {name: np.ascontiguousarray(inputs[name]) for name in _INS}
    named["const"] = constants()
    for name, a in named.items():
        arrays[f"in_{name}"] = a
        tensors[name] = nc.dram_tensor(f"in_{name}", a.shape, mybir.dt.from_np(a.dtype), kind="ExternalInput").ap()
    tensors["out"] = nc.dram_tensor("out", (BATCH, S, D), F32, kind="ExternalOutput").ap()
    build(nc, tensors)
    r = run_bass_kernel_spmd(nc, [arrays], core_ids=[0])
    return r.results[0]["out"]
```

```python
from contextlib import ExitStack

import numpy as np

import concourse.bass as bass
from concourse import mybir

F32 = mybir.dt.float32
BF16 = mybir.dt.bfloat16
I32 = mybir.dt.int32
ALU = mybir.AluOpType
ACT = mybir.ActivationFunctionType
AX_X = mybir.AxisListType.X

P = 128
BATCH, S, D = 4, 256, 256
C = 128
NH = 16
HD = D // NH
CHD = C // NH
FF = 688
NFE = FF // P
EDGE = FF - NFE * P
NF = 2 * NFE + 1
EPS = 1e-6
NT = S // P
DC = D // P
RING = 6
VW = 32
NEG = -1e30
SELF_Q = ((3, (0,)), (2, (1,)), (1, (2,)))
SELF_K = ((1, (0, 1, 2)), (1, (0, 1)), (1, (0,)))
CROSS_Q = ((3, (0,)), (3, (1,)), (3, (2,)))
CROSS_K = ((3, (0, 1, 2)),)
SELF_ROWS = 6 * HD
CROSS_ROWS = 9 * CHD

C_ID, C_MQ, C_MK, C_T, C_TAB = 0, P, 2 * P, 3 * P, 3 * P + 2
C_END = C_TAB + 2 * 2 * HD


def constants():
    out = np.zeros((P, C_END), np.float32)
    i = np.arange(P)
    out[:, C_ID:C_ID + P] = np.eye(P)
    out[:, C_MQ:C_MQ + P] = np.where(i[None, :] > i[:, None], NEG, 0.0)
    out[:, C_MK:C_MK + P] = np.where(i[:, None] > i[None, :], NEG, 0.0)
    out[:, C_T] = i
    out[:, C_T + 1] = i + P
    inv = (1.0 / np.float32(10000.0) ** (np.arange(0, HD, 2, dtype=np.float32) / np.float32(HD))).astype(np.float32)
    freq = np.outer(np.arange(S, dtype=np.float32), inv).astype(np.float32)
    cos = np.cos(freq.astype(np.float64))
    sin = np.sin(freq.astype(np.float64))
    table = np.concatenate([cos, cos, -sin, sin], axis=1).astype(np.float32)
    out[:, C_TAB:] = table.reshape(2, P, 2 * HD).transpose(1, 0, 2).reshape(P, -1)
    return out


START = (0.0, 26.0, 130.0, 160.0)
ALONE = (
    ("xT", 0.0), ("memT", 0.5), ("xT.out", 0.9), ("memT.out", 1.0), ("y", 1.3), ("y.out", 2.1),
    ("ckv", 2.3), ("ckv.first", 2.9), ("s0", 3.1), ("cv.out", 3.3), ("ck.rest", 3.5), ("s0.max", 4.6),
    ("s0.exp", 5.3), ("s0.norm", 6.3), ("pT", 7.0), ("pT.out", 7.5), ("am", 8.1), ("am.out", 9.0),
    ("gate", 9.5), ("gate.bias", 12.0), ("gate.tanh", 12.5), ("gate.add", 13.5),
    ("square0", 15.0), ("rstd0", 15.5), ("scale0", 17.5), ("square1", 18.5), ("rstd1", 19.0), ("scale1", 21.0),
    ("nT", 22.0), ("nT.out", 22.5), ("qk0", 24.0), ("rotate0", 27.5), ("qk1", 27.5), ("rotate1", 31.0),
    ("v", 31.0), ("split.q", 34.5), ("v.out", 34.6), ("split.q.first", 35.0), ("split.k", 35.1),
    ("split.q.rest", 35.6), ("split.k.first", 35.6), ("split.k.rest", 37.0), ("stack0", 38.5),
    ("scores0", 46.0), ("rows0", 54.5), ("attend0", 58.0),
    ("unhead0", 69.3), ("unhead0.out", 69.8), ("ctxT", 71.5), ("ctxT.out", 72.0), ("dense", 73.5), ("dense.out", 77.0),
    ("square2", 77.5), ("rstd2", 78.0), ("scale2", 80.0),
    ("ciT", 81.0), ("ciT.out", 81.5), ("cq", 82.5), ("cq.first", 83.5), ("cq.rest", 84.0), ("stack1", 85.0),
    ("scores1", 91.0), ("rows1", 101.5), ("attend1", 105.0),
    ("unhead1", 119.2), ("unhead1.out", 119.7), ("cctxT", 121.0), ("cctxT.out", 121.5), ("cdense", 122.0),
    ("cdense.out", 123.0), ("square3", 123.5), ("rstd3", 124.0), ("scale3", 126.0),
    ("miT", 127.0), ("miT.out", 127.5), ("hidden", 129.0), ("down0", 148.0), ("down0.out", 153.0),
    ("down1", 153.0), ("down1.out", 158.0),
)
EACH = {"scores0": 0.62, "scores1": 0.62, "attend0": 2.5, "attend1": 3.2, "hidden": 1.75}
LATER = {"scores0": 0.5, "scores1": 0.5, "rows0": 0.4, "rows1": 0.4, "attend0": 1.0, "attend1": 1.0, "hidden": 0.9}
MANY = {"scores0": 12, "scores1": 16, "attend0": 5, "attend1": 5, "hidden": NF, "rows0": 1, "rows1": 1}
PREP = (("prep", 6.5), ("prep.out", 7.2), ("trig", 22.5), ("trig.out", 22.9))

LAST_READ = {"ckv": "ck.rest", "s0": "s0.exp", "gate": "gate.add", "qk0": "rotate0", "qk1": "rotate1",
             "split.q": "split.q.rest", "split.k": "split.k.rest", "cq": "cq.rest",
             **{k: k + ".out" for k in ("xT", "memT", "y", "pT", "am", "nT", "v", "scores0", "scores1", "rows0", "rows1",
                                        "attend0", "attend1", "unhead0", "unhead1", "ctxT", "dense", "ciT", "cctxT",
                                        "cdense", "miT", "hidden", "down0", "down1", "prep", "trig")}}
TAKES = {"ckv": 2, "gate": 2, "unhead0": 2, "unhead1": 2, "prep": 3}
SHARED = (("hidden", 1, "down1"), ("rotate0", 1, "split.k"), ("split.q.first", 1, "stack0"), ("ckv.first", 1, "ck.rest"),
          ("cq.first", 1, "stack1"), ("s0.exp", 1, "s0.norm"), ("gate.bias", 1, "gate.add"),
          ("xT.out", 2, "cq"), ("y.out", 2, "cdense"), ("s0.exp", 2, "miT"), ("pT.out", 2, "hidden"), ("memT.out", 2, "s0"),
          ("cv.out", 2, "attend1"), ("v.out", 2, "attend0"), ("stack0", 2, "attend1"), ("attend0", 2, "unhead1"),
          ("rows0", 2, "rows1.out"))


def timeline():
    later = {-1: [(at, stage, 0) for stage, at in PREP]}
    for b in range(BATCH):
        later[b] = []
        for stage, at in ALONE:
            for j in range(MANY.get(stage, 1)):
                at_j = at + j * EACH.get(stage, 0.0)
                later[b].append((at_j, stage, j))
                if stage in LATER:
                    later[b].append((at_j + LATER[stage], stage + ".out", j))
        later[b].sort(key=lambda f: f[0])
    start = {-1: 0.0, **dict(enumerate(START))}
    free, held, bank_of, order, over = [0, 1, 4, 5, 6, 7], {}, {}, [], set()

    def takes(stage, j):
        if stage not in LAST_READ or (stage, j) in (("attend0", 0), ("attend1", 0)):
            return 0
        return TAKES.get(stage, 1)

    def can_go(b):
        _, stage, j = later[b][0]
        if takes(stage, j) > len(free):
            return False
        if stage in ("attend0", "attend1") and j == 0 and attending:
            return False
        return all(stage != s or b < ago or (after, b - ago, MANY.get(after, 1) - 1) in over for s, ago, after in SHARED)

    attending = set()
    while any(later.values()):
        at, b = min((start[b] + later[b][0][0], b) for b in later if later[b] and can_go(b))
        for o in later:
            if later[o]:
                start[o] += max(0.0, at - start[o] - later[o][0][0])
        _, stage, j = later[b].pop(0)
        order.append((stage, b, j))
        over.add((stage, b, j))
        n = takes(stage, j)
        if n:
            bank_of[stage, b, j] = [free.pop(0) for _ in range(n)]
            held[LAST_READ[stage], b, j] = bank_of[stage, b, j]
        free += held.pop((stage, b, j), [])
        if stage in ("attend0", "attend1") and j in (0, 4):
            attending ^= {b}
    return order, bank_of


def build(nc, t):
    order, bank_of = timeline()
    x_d, ctx_d, out_d = (t[n].rearrange("b (s p) d -> b p s d", p=P) for n in ("x", "ctx_1024", "out"))

    exp_no, exp_head = {}, []
    for stage, b, hg in order:
        if stage in ("attend0", "attend1") and hg < 4:
            layer = int(stage[-1])
            for u in range(3 + layer):
                exp_no[layer, b, hg, u] = len(exp_head)
                exp_head.append((layer, b, hg))

    with ExitStack() as stack:
        def sb(name, shape, dt=F32):
            return stack.enter_context(nc.sbuf_tensor(name, shape, dt))

        const = sb("const", [P, C_END])
        ident = const[:, C_ID:C_ID + P]
        bconst = sb("bconst", [P, 3 * P], BF16)
        identb, maskq, maskk = (bconst[:, P * j:P * j + P] for j in range(3))
        half = sb("half", [P, 4])
        trig = sb("trig", [P, NT, 2 * HD])
        w_mem = sb("w_mem", [P, DC, C])
        w_memT = sb("w_memT", [P, D])
        w_gateT = sb("w_gateT", [P, DC, D])
        w_gatem = sb("w_gatem", [P, D])
        b_gate = sb("b_gate", [P, D])
        norm_w = sb("norm_w", [P, 4, D])
        qkv = sb("qkv", [P, 2, DC, 3 * D])
        dense = sb("dense", [P, 2, DC, D])
        cq_w = sb("cq_w", [P, DC, C])
        ck_w = sb("ck_w", [P, C])
        cv_w = sb("cv_w", [P, C])
        cdense = sb("cdense", [P, D])
        w_up = sb("w_up", [P, 2, DC, 2 * FF])
        w_down = sb("w_down", [P, NF, D])

        X = sb("X", [P, BATCH, NT, D])
        mem = sb("mem", [P, BATCH, NT, C])
        vm = sb("vm", [P, BATCH, S], BF16)
        lm = sb("lm", [P, BATCH, S], BF16)

        def two(name, shape, dt=F32):
            return [sb(f"{name}{g}", shape, dt) for g in range(2)]

        UT = two("UT", [P, DC, S])
        memT = two("memT", [P, S])
        yT = two("yT", [P, S])
        normed = two("normed", [P, NT, D])
        TV = two("TV", [P, DC, S])
        TL = two("TL", [P, DC, S])
        Qs = two("Qs", [P, NH, S], BF16)
        Ks = two("Ks", [P, NH, S], BF16)
        V = two("V", [P, NT, NH, VW])
        Vc = two("Vc", [P, NT, NH, VW])
        heads = two("heads", [P, 4, S])

        gated = sb("gated", [P, NT, D])
        spin = sb("spin", [P, 2, 2 * D])
        QR = sb("QR", [P, NT, 2, D])
        parts = {k: sb(f"parts_{k}", [P, w, 3, S], BF16) for k, w in (("q", DC), ("k", DC), ("ck", 1), ("cq", 1))}
        rest = spin[:, 1, :]
        squares = sb("squares", [P, 2, D], BF16)
        probs = sb("probs", [P, RING, 2 * S])
        H = sb("H", [P, NF, S])
        tanh = sb("tanh", [P, 2, S])
        silu = sb("silu", [P, 2, S])
        negmax = sb("negmax", [P, 2, 2, NH])
        nm_parts = sb("nm_parts", [NH, 2, 2, S], BF16)
        sc = sb("sc", [P, 16 + 3 * 32])
        nm0, l0, r0 = sc[:, 0:2], sc[:, 2:4], sc[:, 4:6]
        sumsq, var, rstd = (sc[:, 16 + 32 * j:48 + 32 * j] for j in range(3))
        rsum = sb("rsum", [P, NH])
        maski = QR[:].rearrange("p n k d -> p (n k) d").bitcast(I32)
        posi = silu[:, 0, :].bitcast(I32)
        w_gate = H[:, 0:2 * DC, :].rearrange("p (c h) d -> p c (h d)", c=DC)
        cq_loaded_w = H[:, 2 * DC, :].rearrange("p (c e) -> p c e", c=DC)
        ck_loaded_w = H[:, 2 * DC + 1, 0:C]

        bank = [stack.enter_context(nc.psum_tensor(f"bank{j}", [P, 512], F32)) for j in range(8)]

        scratch = {k: nc.dram_tensor(f"scratch_{k}", [BATCH, 3, w, S], BF16, kind="Internal").ap()
                   for k, w in (("q", D), ("k", D), ("ck", C), ("cq", C))}

        class Signal:
            def __init__(self, name, per=1):
                self.sem = stack.enter_context(nc.semaphore(name))
                self.per = per

        c_loaded, pos_loaded, mask_loaded = Signal("c_loaded"), Signal("pos_loaded"), Signal("mask_loaded")
        gate_loaded, vec_loaded = Signal("gate_loaded"), Signal("vec_loaded")
        qkv_loaded, dense_loaded = Signal("qkv_loaded"), Signal("dense_loaded")
        cdense_loaded, mlp_loaded, wmem_loaded = Signal("cdense_loaded"), Signal("mlp_loaded"), Signal("wmem_loaded")
        bconst_ready, pool_consts, eps_ready = Signal("bconst_ready"), Signal("pool_consts"), Signal("eps_ready")
        cq_loaded, ckv_loaded, ck_turned, cq_turned = (Signal(n) for n in ("cq_loaded", "ckv_loaded", "ck_turned", "cq_turned"))
        pos_step, masks_ready, onehot_ready = Signal("pos_step"), Signal("masks_ready"), Signal("onehot_ready")
        trig_psum, trig_ready = Signal("trig_psum"), Signal("trig_ready")
        prep_psum, prep_ready = Signal("prep_psum"), Signal("prep_ready")
        x_loaded, mem_loaded = ([Signal(f"{n}_loaded{b}") for b in range(BATCH)] for n in ("x", "mem"))
        xT_psum, xT_ready = Signal("xT_psum"), Signal("xT_ready")
        memT_psum, memT_ready = Signal("memT_psum"), Signal("memT_ready")
        y_psum, y_ready = Signal("y_psum"), Signal("y_ready")
        cv_psum, cv_ready = Signal("cv_psum"), Signal("cv_ready")
        s0_psum, nm0_ready, e0_ready, p0_ready = Signal("s0_psum"), Signal("nm0_ready"), Signal("e0_ready", NT), Signal("p0_ready", NT)
        pT_psum, pT_ready, am_psum, am_ready = Signal("pT_psum"), Signal("pT_ready"), Signal("am_psum"), Signal("am_ready")
        gate_psum, pre_gate, gate_ready = Signal("gate_psum", NT), Signal("pre_gate", NT), Signal("gate_ready", NT)
        residual = [Signal(f"residual{k}", NT) for k in range(4)]
        sumsq_ready = [Signal(f"sumsq_ready{k}", NT) for k in range(4)]
        var_ready, rstd_ready = ([Signal(f"{n}_ready{k}") for k in range(4)] for n in ("var", "rstd"))
        normed_ready = [Signal(f"normed_ready{k}", NT) for k in range(4)]
        nT_psum, nT_ready = Signal("nT_psum"), Signal("nT_ready")
        qk_psum, qr_ready, v_psum, v_ready = Signal("qk_psum", NT), Signal("qr_ready", NT), Signal("v_psum"), Signal("v_ready")
        kinds = ("q", "k", "ck", "cq")
        split_psum, first_part, parts_ready, written = (
            {k: Signal(f"{n}_{k}", 16 * (DC if n == "written" and k in "qk" else 1) if n == "written" else 1) for k in kinds}
            for n in ("split_psum", "first_part", "parts_ready", "written"))
        stacked = [[Signal(f"stacked{layer}_{g}", 16 * n) for g in range(2)] for layer, n in enumerate((6, 5))]
        s_psum, max_ready = ([Signal(f"{n}{layer}", (12, 16)[layer]) for layer in range(2)] for n in ("s_psum", "max_ready"))
        nm_psum, nm_hi, nm_ready = ([Signal(f"{n}{layer}") for layer in range(2)] for n in ("nm_psum", "nm_hi", "nm_ready"))
        max_rows = [[Signal(f"max_rows{layer}_{g}", 32) for g in range(2)] for layer in range(2)]
        NU = (3, 4)
        st_psum, e_ready = ([Signal(f"{n}{layer}", 4 * NU[layer]) for layer in range(2)] for n in ("st_psum", "e_ready"))
        pv_psum, heads_ready = ([Signal(f"{n}{layer}", 4) for layer in range(2)] for n in ("pv_psum", "heads_ready"))
        hT_psum, ctx_ready = ([Signal(f"{n}{layer}", NT) for layer in range(2)] for n in ("hT_psum", "ctx_ready"))
        cT_psum, cT_ready, proj_psum = ([Signal(f"{n}{layer}") for layer in range(2)] for n in ("cT_psum", "cT_ready", "proj_psum"))
        ciT_psum, ciT_ready, miT_psum, miT_ready = Signal("ciT_psum"), Signal("ciT_ready"), Signal("miT_psum"), Signal("miT_ready")
        gu_psum, tanh_ready, silu_ready, h_ready = Signal("gu_psum", NF), Signal("tanh_ready", NF), Signal("silu_ready", NF), Signal("h_ready", NF)
        down_psum, out_ready = Signal("down_psum", NT), Signal("out_ready", NT)
        out_stored = Signal("out_stored", 16 * NT)
        v_step = Signal("v_step")

        def waiter(eng):
            seen = {}

            def wait(signal, b, n=None):
                at = b * signal.per + (signal.per if n is None else n)
                if at > 0 and seen.get(signal, 0) < at:
                    seen[signal] = at
                    eng.wait_ge(signal.sem, at)
            return wait

        def run(handlers):
            for stage, b, j in order:
                if stage in handlers:
                    handlers[stage](b, j)

        def turns(k):
            return k // 2

        block = stack.enter_context(nc.Block())

        @block.sync
        def _(sp):
            wait = waiter(sp)
            sp.dma_start(X[:, 0], x_d[0]).then_inc(x_loaded[0].sem, 16)
            sp.dma_start(const[:], t["const"]).then_inc(c_loaded.sem, 16)
            sp.dma_start(mem[:, 0], ctx_d[0]).then_inc(mem_loaded[0].sem, 16)
            sp.dma_start(w_mem[:], t["L0_xattn_W_mem"].rearrange("(c p) e -> p c e", p=P)).then_inc(wmem_loaded.sem, 16)
            sp.dma_start(X[:, 1], x_d[1]).then_inc(x_loaded[1].sem, 16)
            sp.dma_start(mem[:, 1], ctx_d[1]).then_inc(mem_loaded[1].sem, 16)
            for b in (2, 3):
                sp.dma_start(X[:, b], x_d[b]).then_inc(x_loaded[b].sem, 16)
                sp.dma_start(mem[:, b], ctx_d[b]).then_inc(mem_loaded[b].sem, 16)

            def write(k, b):
                wait(parts_ready[k], b)
                for c in range(DC if k in "qk" else 1):
                    sp.dma_start(scratch[k][b, :, P * c:P * c + P, :].rearrange("p d t -> d p t"), parts[k][:, c])\
                        .then_inc(written[k].sem, 16)

            def read(k, b, dst, runs, hd, signal):
                wait(written[k], b)
                src, row = scratch[k][b].rearrange("p (d h) t -> p d (h t)", h=NH), 0
                for often, which in runs:
                    n = len(which) * hd
                    s = src[which[0]:which[0] + len(which)].rearrange("p d n -> (p d) n")
                    out = dst[row:row + often * n].rearrange("r h s -> r (h s)")
                    if often > 1:
                        s = s.rearrange("(o r) n -> o r n", o=1).to_broadcast([often, n, NH * S])
                    sp.dma_start(out, s).then_inc(signal.sem, 16)
                    row += often * n

            def stack0(b, _):
                g = b % 2
                write("q", b)
                write("k", b)
                if b >= 2:
                    wait(st_psum[1], b - 2)
                read("q", b, Qs[g], SELF_Q, HD, stacked[0][g])
                read("k", b, Ks[g], SELF_K, HD, stacked[0][g])

            def ck_rest(b, _):
                write("ck", b)

            def stack1(b, _):
                g = b % 2
                write("cq", b)
                wait(st_psum[0], b)
                sp.dma_start(Ks[g][CROSS_ROWS:CROSS_ROWS + 2], Ks[g][SELF_ROWS:SELF_ROWS + 2]).then_inc(stacked[1][g].sem, 16)
                read("ck", b, Ks[g], CROSS_K, CHD, stacked[1][g])
                read("cq", b, Qs[g], CROSS_Q, CHD, stacked[1][g])

            def rows(layer):
                def rows_(b, _):
                    g, top = b % 2, (SELF_ROWS, CROSS_ROWS)[layer]
                    wait(nm_ready[layer], b)
                    for j in range(2):
                        sp.dma_start(Qs[g][top + j:top + j + 1, :, :], nm_parts[:, g, j:j + 1, :])\
                            .then_inc(max_rows[layer][g].sem, 16)
                return rows_

            def down(n):
                def down_(b, _):
                    wait(out_ready, b, n + 1)
                    sp.dma_start(out_d[b][:, n, :], X[:, b, n, :]).then_inc(out_stored.sem, 16)
                return down_

            run({"stack0": stack0, "ck.rest": ck_rest, "stack1": stack1, "rows0.out": rows(0), "rows1.out": rows(1),
                 "down0.out": down(0), "down1.out": down(1)})
            wait(out_stored, BATCH - 1)

        @block.gpsimd
        def _(pool):
            wait = waiter(pool)
            pool.memset(half[:, 0:2], -0.5).then_inc(eps_ready.sem, 1)
            pool.memset(half[:, 2:4], EPS).then_inc(eps_ready.sem, 1)
            pool.wait_ge(eps_ready.sem, 2)
            pool.memset(w_down[32:64, NF - 1, :], 0.0).then_inc(pool_consts.sem, 1)
            pool.wait_ge(pool_consts.sem, 1)
            pool.wait_ge(ckv_loaded.sem, 2 * 16)
            pool.tensor_copy(ck_w[:].rearrange("p (d h) -> p h d", h=NH), ck_loaded_w.rearrange("p (h d) -> p h d", h=NH))\
                .then_inc(ck_turned.sem, 1)
            for v in (Vc[0], V[0], Vc[1], V[1]):
                pool.memset(v[:], 0.0).then_inc(pool_consts.sem, 1)
            for v, n in ((Vc[0], 2), (V[0], 3), (Vc[1], 4), (V[1], 5)):
                pool.wait_ge(pool_consts.sem, n)
                pool.memset(v[:].rearrange("p n h w -> p (n h) w")[:, :, HD:HD + 1], 1.0).then_inc(pool_consts.sem, 1)
            for g in range(2):
                pool.wait_ge(pool_consts.sem, 9 + g)
                pool.memset(Ks[g][SELF_ROWS:SELF_ROWS + 2], 1.0).then_inc(pool_consts.sem, 1)
            pool.wait_ge(pool_consts.sem, 11)
            pool.wait_ge(cq_loaded.sem, 16)
            pool.tensor_copy(cq_w[:].rearrange("p c (d h) -> p c h d", h=NH),
                             cq_loaded_w.rearrange("p c (h d) -> p c h d", h=NH)).then_inc(cq_turned.sem, 1)

            def rstd_of(k):
                def rstd_(b, _):
                    cols = slice(8 * k + 2 * b, 8 * k + 2 * b + 2)
                    wait(sumsq_ready[k], b)
                    pool.tensor_tensor(var[:, cols], sumsq[:, cols], half[:, 2:4], ALU.add).then_inc(var_ready[k].sem, 1)
                    wait(var_ready[k], b)
                    pool.tensor_tensor(rstd[:, cols], var[:, cols], half[:, 0:2], ALU.pow).then_inc(rstd_ready[k].sem, 1)
                return rstd_

            run({f"rstd{k}": rstd_of(k) for k in range(4)})

        @block.scalar
        def _(act):
            wait = waiter(act)

            def load(at, src, signal):
                act.dma_start(at, src).then_inc(signal.sem, 16)

            load(w_gate, t["L0_xattn_W_gate"].rearrange("(c p) f -> p c f", p=P), gate_loaded)
            load(ck_loaded_w, t["L1_xattn_ckv_w"][:, 0:C], ckv_loaded)
            load(cv_w[:], t["L1_xattn_ckv_w"][:, C:2 * C], ckv_loaded)
            load(maski, t["mask_BxS_ik0"].partition_broadcast(P), mask_loaded)
            load(posi, t["pos_1xS"][0].partition_broadcast(P), pos_loaded)
            for name, at in (("L0_xattn_b_gate", b_gate[:]), ("L0_xattn_norm_w", norm_w[:, 0]),
                             ("L1_xattn_ln_in_w", norm_w[:, 1]), ("L1_xattn_ln_post_cross_w", norm_w[:, 2]),
                             ("L1_xattn_ln_post_attn_w", norm_w[:, 3])):
                load(at, t[name].partition_broadcast(P), vec_loaded)
            for e, n in enumerate("vl"):
                load(qkv[:, e], t[f"L1_xattn_{n}_qkv"].rearrange("(c p) n -> p c n", p=P), qkv_loaded)
            load(cq_loaded_w, t["L1_xattn_cq_w"].rearrange("(c p) e -> p c e", p=P), cq_loaded)
            load(cdense[:], t["L1_xattn_cdense_w"], cdense_loaded)
            for e, n in enumerate("vl"):
                load(dense[:, e], t[f"L1_xattn_{n}_dense"].rearrange("(c p) n -> p c n", p=P), dense_loaded)
            for k, w in enumerate(("gate", "up")):
                for e, n in enumerate("vl"):
                    load(w_up[:, k, :, FF * e:FF * e + FF], t[f"L1_xattn_{n}_{w}"].rearrange("(c p) n -> p c n", p=P), mlp_loaded)
            for e, n in enumerate("vl"):
                w = t[f"L1_xattn_{n}_down"]
                load(w_down[:, NFE * e:NFE * e + NFE, :], w[0:NFE * P].rearrange("(c p) n -> p c n", p=P), mlp_loaded)
            act.wait_ge(pool_consts.sem, 1)
            for e, n in enumerate("vl"):
                load(w_down[64 * e:64 * e + EDGE, NF - 1, :], t[f"L1_xattn_{n}_down"][NFE * P:FF], mlp_loaded)

            def xT(b, _):
                wait(xT_psum, b)
                if b >= 2:
                    wait(split_psum["cq"], b - 2)
                nc.scalar.copy(UT[b % 2][:].rearrange("p c s -> p (c s)"), bank[bank_of["xT", b, 0][0]][:]).then_inc(xT_ready.sem, 1)

            def y(b, _):
                wait(y_psum, b)
                if b >= 2:
                    wait(proj_psum[1], b - 2)
                nc.scalar.copy(yT[b % 2][:], bank[bank_of["y", b, 0][0]][:, 0:S]).then_inc(y_ready.sem, 1)

            def first(k, stage, scale):
                def first_(b, _):
                    w = S * (DC if k in "qk" else 1)
                    wait(split_psum[k], b)
                    if b >= 1:
                        wait(written[k], b - 1)
                    nc.scalar.activation(parts[k][:, :, 0, :], bank[bank_of[stage, b, 0][0]][:, 0:w].rearrange("p (c s) -> p c s", s=S),
                                         ACT.Copy, scale=scale).then_inc(first_part[k].sem, 1)
                return first_

            def cv(b, _):
                wait(cv_psum, b)
                act.wait_ge(pool_consts.sem, 9)
                if b >= 2:
                    wait(pv_psum[1], b - 2)
                nc.scalar.copy(Vc[b % 2][:].rearrange("p n h w -> p (n h) w")[:, :, 0:CHD],
                               bank[bank_of["ckv", b, 0][1]][:, 0:NT * C].rearrange("p (h w) -> p h w", w=CHD)).then_inc(cv_ready.sem, 1)

            def v(b, _):
                wait(v_psum, b)
                if b >= 2:
                    wait(pv_psum[0], b - 2)
                nc.scalar.copy(V[b % 2][:].rearrange("p n h w -> p (n h) w")[:, :, 0:HD],
                               bank[bank_of["v", b, 0][0]][:].rearrange("p (h w) -> p h w", w=HD)).then_inc(v_ready.sem, 1)

            def s0(b, _):
                if b >= 2:
                    wait(miT_psum, b - 2)
                if b >= 1:
                    wait(p0_ready, b - 1)
                for n in range(NT):
                    wait(nm0_ready, b)
                    nc.scalar.activation(normed[b % 2][:, n, :], bank[bank_of["s0", b, 0][0]][:, S * n:S * n + S],
                                         ACT.Exp, bias=nm0[:, n:n + 1], scale=float(D) ** -0.5,
                                         accum_out=l0[:, n:n + 1]).then_inc(e0_ready.sem, 1)

            def pT(b, _):
                wait(pT_psum, b)
                if b >= 2:
                    wait(gu_psum, b - 2)
                nc.scalar.copy(TV[b % 2][:].rearrange("p c s -> p (c s)"), bank[bank_of["pT", b, 0][0]][:]).then_inc(pT_ready.sem, 1)

            def gate(b, _):
                for n in range(NT):
                    wait(pre_gate, b, n + 1)
                    nc.scalar.activation(gated[:, n, :], gated[:, n, :], ACT.Tanh, scale=0.5).then_inc(gate_ready.sem, 1)

            squared = []

            def square(k):
                def square_(b, _):
                    for n in range(NT):
                        wait(residual[k], b, n + 1)
                        if squared:
                            wait(*squared[-1])
                        nc.scalar.activation(squares[:, n, :], X[:, b, n, :], ACT.Square, scale=float(D) ** -0.5,
                                             accum_out=sumsq[:, 8 * k + 2 * b + n:8 * k + 2 * b + n + 1]).then_inc(sumsq_ready[k].sem, 1)
                    squared.append((sumsq_ready[k], b))
                return square_

            def rows(layer):
                def rows_(b, _):
                    g = b % 2
                    wait(nm_psum[layer], b)
                    if layer == 1:
                        wait(max_rows[0][g], turns(b))
                    elif b >= 2:
                        wait(max_rows[1][g], turns(b) - 1)
                    nc.scalar.copy(nm_parts[:, g, 0, :], bank[bank_of[f"rows{layer}", b, 0][0]][0:NH, 0:S]).then_inc(nm_hi[layer].sem, 1)
                return rows_

            def attend(layer):
                def attend_(b, hg):
                    for u in range(NU[layer] if hg < 4 else 0):
                        no = exp_no[layer, b, hg, u]
                        wait(st_psum[layer], b, NU[layer] * hg + u + 1)
                        if no >= RING:
                            la, ba, ha = exp_head[no - RING]
                            wait(pv_psum[la], ba, ha + 1)
                        nc.scalar.activation(probs[:, no % RING, :], bank[2 + no % 2][:], ACT.Exp).then_inc(e_ready[layer].sem, 1)
                return attend_

            def ciT(b, _):
                wait(ciT_psum, b)
                nc.scalar.copy(UT[b % 2][:].rearrange("p c s -> p (c s)"), bank[bank_of["ciT", b, 0][0]][:]).then_inc(ciT_ready.sem, 1)

            def cctxT(b, _):
                wait(cT_psum[1], b)
                nc.scalar.copy(yT[b % 2][:], bank[bank_of["cctxT", b, 0][0]][:, 0:S]).then_inc(cT_ready[1].sem, 1)

            def hidden(b, i):
                wait(gu_psum, b, i + 1)
                if i + b * NF >= 2:
                    wait(silu_ready, 0, i + b * NF - 1)
                nc.scalar.activation(tanh[:, i % 2, :], bank[bank_of["hidden", b, i][0]][:, 0:S], ACT.Tanh, scale=0.5)\
                    .then_inc(tanh_ready.sem, 1)

            run({"xT.out": xT, "y.out": y, "ckv.first": first("ck", "ckv", 1.0), "cv.out": cv, "v.out": v, "s0.exp": s0,
                 "pT.out": pT, "gate.tanh": gate, "rows0.out": rows(0), "rows1.out": rows(1),
                 "split.q.first": first("q", "split.q", float(HD) ** -0.5), "split.k.first": first("k", "split.k", 1.0),
                 "cq.first": first("cq", "cq", CSCALE), "attend0": attend(0), "attend1": attend(1),
                 "ciT.out": ciT, "cctxT.out": cctxT, "hidden.out": hidden, **{f"square{k}": square(k) for k in range(4)}})

        @block.vector
        def _(dve):
            wait = waiter(dve)
            steps = [0]

            def step(ins):
                steps[0] += 1
                ins.then_inc(v_step.sem, 1)
                dve.wait_ge(v_step.sem, steps[0])

            dve.memset(H[64:128, NF - 1, :], 0.0).then_inc(masks_ready.sem, 1)
            dve.memset(H[32:64, NF - 1, :], 0.0).then_inc(masks_ready.sem, 1)
            dve.memset(vm[:, :, S - 1:S], 0.0).then_inc(masks_ready.sem, 1)
            dve.wait_ge(c_loaded.sem, 16)
            dve.tensor_copy(bconst[:], const[:, 0:3 * P]).then_inc(bconst_ready.sem, 1)

            def masks():
                is_one = probs[:, 0:2, :].rearrange("p a (b s) -> p (a b) s", s=S)
                dve.wait_ge(mask_loaded.sem, 16)
                step(dve.tensor_scalar(is_one, maski, 1.0, None, ALU.is_equal))
                dve.tensor_tensor(vm[:, :, 0:S - 1], is_one[:, :, 0:S - 1], is_one[:, :, 1:S], ALU.mult).then_inc(masks_ready.sem, 1)
                dve.wait_ge(masks_ready.sem, 4)
                dve.tensor_scalar(lm[:], vm[:], -1.0, 1.0, ALU.mult, ALU.add).then_inc(masks_ready.sem, 1)
                dve.wait_ge(masks_ready.sem, 5)

            def positions():
                dve.wait_ge(pos_loaded.sem, 16)
                pos, wrap = probs[:, 2, 0:S], probs[:, 2, S:2 * S]
                step(dve.tensor_copy(pos, posi))
                step(dve.tensor_scalar(wrap, pos, 0.0, float(S), ALU.is_lt, ALU.mult))
                step(dve.tensor_tensor(pos, pos, wrap, ALU.add))
                step(dve.tensor_scalar(pos, pos, 0.0, float(S - 1), ALU.max, ALU.min))
                for c in range(2):
                    dve.tensor_scalar(probs[:, 3, S * c:S * c + S], pos, const[:, C_T + c:C_T + c + 1], None, ALU.is_equal)\
                        .then_inc(onehot_ready.sem, 1)

            def prep(_, __):
                a, b, c = bank_of["prep", -1, 0]
                dve.wait_ge(prep_psum.sem, 1)
                dve.tensor_copy(w_gateT[:].rearrange("p c d -> p (c d)"), bank[a][:]).then_inc(prep_ready.sem, 1)
                dve.tensor_copy(spin[:, 0, :], bank[b][:]).then_inc(prep_ready.sem, 1)
                dve.tensor_copy(w_memT[:], bank[c][:, 0:D]).then_inc(prep_ready.sem, 1)
                dve.wait_ge(prep_psum.sem, 2)
                dve.tensor_copy(w_gatem[:], bank[c][:, D:2 * D]).then_inc(prep_ready.sem, 1)
                masks()
                positions()

            def trig_(_, __):
                dve.wait_ge(trig_psum.sem, 1)
                dve.tensor_copy(trig[:].rearrange("p n w -> p (n w)"), bank[bank_of["trig", -1, 0][0]][:, 0:4 * HD])\
                    .then_inc(trig_ready.sem, 1)
                dve.wait_ge(trig_ready.sem, 1)

            def memT_(b, _):
                wait(memT_psum, b)
                if b >= 2:
                    wait(s0_psum, b - 2)
                dve.tensor_copy(memT[b % 2][:], bank[bank_of["memT", b, 0][0]][:, 0:S]).then_inc(memT_ready.sem, 1)

            def split_rest(k, stage, scale):
                def split_(b, _):
                    w = DC if k in "qk" else 1
                    src = bank[bank_of[stage, b, 0][0]][:, 0:w * S].rearrange("p (c s) -> p c s", s=S)
                    left = rest[:, 0:w * S].rearrange("p (c s) -> p c s", s=S)
                    wait(first_part[k], b)
                    step(dve.scalar_tensor_tensor(left, src, scale, parts[k][:, :, 0, :], ALU.mult, ALU.subtract))
                    step(dve.tensor_copy(parts[k][:, :, 1, :], left))
                    dve.tensor_tensor(parts[k][:, :, 2, :], left, parts[k][:, :, 1, :], ALU.subtract).then_inc(parts_ready[k].sem, 1)
                    wait(parts_ready[k], b)
                return split_

            def s0_max(b, _):
                wait(s0_psum, b)
                if b >= 1:
                    wait(e0_ready, b - 1)
                step(dve.tensor_reduce(nm0, bank[bank_of["s0", b, 0][0]][:].rearrange("p (n s) -> p n s", n=2),
                                       AX_X, ALU.max, negate=True))
                dve.tensor_scalar(nm0, nm0, float(D) ** -0.5, None, ALU.mult).then_inc(nm0_ready.sem, 1)

            def s0_norm(b, _):
                wait(e0_ready, b)
                step(dve.reciprocal(r0, l0))
                for n in range(NT):
                    dve.tensor_scalar(normed[b % 2][:, n, :], normed[b % 2][:, n, :], r0[:, n:n + 1], None, ALU.mult)\
                        .then_inc(p0_ready.sem, 1)
                wait(p0_ready, b)

            def am(b, _):
                wait(am_psum, b)
                if b >= 2:
                    wait(gu_psum, b - 2)
                dve.tensor_copy(TL[b % 2][:, 0, :], bank[bank_of["am", b, 0][0]][:, 0:S]).then_inc(am_ready.sem, 1)

            def gate_bias(b, _):
                dve.wait_ge(vec_loaded.sem, 5 * 16)
                for n in range(NT):
                    wait(gate_psum, b, n + 1)
                    dve.tensor_tensor(gated[:, n, :], bank[bank_of["gate", b, 0][n]][:, 0:D], b_gate[:], ALU.add)\
                        .then_inc(pre_gate.sem, 1)

            def gate_add(b, _):
                wait(x_loaded[b], 0, 16)
                for n in range(NT):
                    wait(gate_ready, b, n + 1)
                    step(dve.tensor_scalar(gated[:, n, :], gated[:, n, :], 0.5, 0.5, ALU.mult, ALU.add))
                    step(dve.tensor_tensor(gated[:, n, :], bank[bank_of["gate", b, 0][n]][:, D:2 * D], gated[:, n, :], ALU.mult))
                    dve.tensor_tensor(X[:, b, n, :], X[:, b, n, :], gated[:, n, :], ALU.add).then_inc(residual[0].sem, 1)
                wait(residual[0], b)

            def scale(k):
                def scale_(b, _):
                    wait(rstd_ready[k], b)
                    if k == 1:
                        wait(residual[1], b)
                    for n in range(NT):
                        col = 8 * k + 2 * b + n
                        dst, signal = (X[:, b, n, :], residual[1]) if k == 0 else (normed[b % 2][:, n, :], normed_ready[k])
                        dve.scalar_tensor_tensor(dst, X[:, b, n, :], rstd[:, col:col + 1], norm_w[:, k, :],
                                                 ALU.mult, ALU.mult).then_inc(signal.sem, 1)
                return scale_

            def masked(stage, b, signal):
                src = bank[bank_of[stage, b, 0][0]][:].rearrange("p (c s) -> p c s", c=DC)
                for m, dst in ((vm, TV), (lm, TL)):
                    ins = dve.tensor_tensor(dst[b % 2][:], src, m[:, b:b + 1, :].to_broadcast([P, DC, S]), ALU.mult)
                ins.then_inc(signal.sem, 1)

            def nT(b, _):
                wait(nT_psum, b)
                masked("nT", b, nT_ready)

            def rotate(n):
                def rotate_(b, _):
                    wait(qk_psum, b, n + 1)
                    qk = bank[bank_of[f"qk{n}", b, 0][0]][:].rearrange("p (h w) -> p h w", w=HD)
                    tab = trig[:, n, :]
                    cos = tab[:, 0:HD].rearrange("p (o w) -> p o w", o=1).to_broadcast([P, 2 * NH, HD])
                    sin = tab[:, HD:2 * HD].rearrange("p (o w) -> p o w", o=1)
                    a, s = (spin[:, i, :].rearrange("p (h w) -> p h w", w=HD) for i in range(2))
                    hw = HD // 2
                    dve.tensor_tensor(a, qk, cos, ALU.mult)
                    dve.tensor_tensor(s[:, :, 0:hw], qk[:, :, hw:HD], sin[:, :, 0:hw].to_broadcast([P, 2 * NH, hw]), ALU.mult)
                    step(dve.tensor_tensor(s[:, :, hw:HD], qk[:, :, 0:hw], sin[:, :, hw:HD].to_broadcast([P, 2 * NH, hw]), ALU.mult))
                    if b >= 1:
                        wait(split_psum["k"], b - 1)
                    dve.tensor_tensor(QR[:, n].rearrange("p k (d h) -> p k h d", h=NH),
                                      spin[:, 0, :].rearrange("p (k h d) -> p k h d", k=2, h=NH),
                                      spin[:, 1, :].rearrange("p (k h d) -> p k h d", k=2, h=NH), ALU.add).then_inc(qr_ready.sem, 1)
                    wait(qr_ready, b, n + 1)
                return rotate_

            def scores(layer):
                def scores_(b, u):
                    g = b % 2
                    wait(s_psum[layer], b, u + 1)
                    if layer == 0 and u < 4:
                        n, dst = 4, negmax[:, g, 0, 4 * u:4 * u + 4]
                    elif layer == 0:
                        n, dst = 2, negmax[:, g, 1, 2 * (u - 4):2 * (u - 4) + 2]
                    else:
                        n, dst = 2, negmax[:, g, u // 8, 2 * (u % 8):2 * (u % 8) + 2]
                    dve.tensor_reduce(dst, bank[bank_of[f"scores{layer}", b, u][0]][:].rearrange("p (h k) -> p h k", h=n), AX_X, ALU.max, negate=True)\
                        .then_inc(max_ready[layer].sem, 1)
                return scores_

            def rows(layer):
                def rows_(b, _):
                    g = b % 2
                    wait(nm_hi[layer], b)
                    dve.tensor_tensor(nm_parts[:, g, 1, :], bank[bank_of[f"rows{layer}", b, 0][0]][0:NH, 0:S],
                                      nm_parts[:, g, 0, :], ALU.subtract).then_inc(nm_ready[layer].sem, 1)
                return rows_

            def attend(layer):
                def attend_(b, hg):
                    if hg == 0:
                        return
                    wait(pv_psum[layer], b, hg)
                    if layer == 1:
                        wait(hT_psum[0], b)
                    elif b >= 2:
                        wait(hT_psum[1], b - 2)
                    dve.tensor_copy(heads[b % 2][:, hg - 1, :], bank[bank_of[f"attend{layer}", b, hg][0]][:, 0:S])\
                        .then_inc(heads_ready[layer].sem, 1)
                return attend_

            def unhead(layer):
                def unhead_(b, _):
                    w = (HD, CHD)[layer]
                    for j in range(NT):
                        wait(hT_psum[layer], b, j + 1)
                        src = bank[bank_of[f"unhead{layer}", b, 0][j]][:].rearrange("p (h w) -> p h w", w=VW)
                        step(dve.reciprocal(rsum[:].rearrange("p (h o) -> p h o", o=1), src[:, :, HD:HD + 1]))
                        dst = normed[b % 2][:, j, 0:NH * w].rearrange("p (h w) -> p h w", w=w)
                        dve.tensor_tensor(dst, src[:, :, 0:w],
                                          rsum[:].rearrange("p (h o) -> p h o", o=1).to_broadcast([P, NH, w]), ALU.mult)\
                            .then_inc(ctx_ready[layer].sem, 1)
                        wait(ctx_ready[layer], b, j + 1)
                return unhead_

            def ctxT(b, _):
                wait(cT_psum[0], b)
                masked("ctxT", b, cT_ready[0])

            def add(layer, stage):
                def add_(b, _):
                    wait(proj_psum[layer], b)
                    x = X[:, b].rearrange("p n d -> p (n d)")
                    dve.tensor_tensor(x, bank[bank_of[stage, b, 0][0]][:], x, ALU.add).then_inc(residual[2 + layer].sem, NT)
                    wait(residual[2 + layer], b)
                return add_

            def miT(b, _):
                wait(miT_psum, b)
                masked("miT", b, miT_ready)

            def hidden(b, i):
                psum = bank[bank_of["hidden", b, i][0]]
                wait(tanh_ready, b, i + 1)
                if b >= 1:
                    wait(down_psum, b - 1)
                rows = (slice(0, P),) if i < NF - 1 else (slice(0, EDGE), slice(64, 64 + EDGE))
                for r in rows:
                    last = dve.scalar_tensor_tensor(silu[r, i % 2, :], tanh[r, i % 2, :], 1.0, psum[r, 0:S], ALU.add, ALU.mult)
                last.then_inc(silu_ready.sem, 1)
                wait(silu_ready, b, i + 1)
                for r in rows:
                    last = dve.scalar_tensor_tensor(H[r, i, :], silu[r, i % 2, :], 0.5, psum[r, S:2 * S], ALU.mult, ALU.mult)
                last.then_inc(h_ready.sem, 1)

            def down(n):
                def down_(b, _):
                    wait(down_psum, b, n + 1)
                    dve.tensor_tensor(X[:, b, n, :], bank[bank_of[f"down{n}", b, 0][0]][:, 0:D], X[:, b, n, :], ALU.add)\
                        .then_inc(out_ready.sem, 1)
                return down_

            run({"prep.out": prep, "trig.out": trig_, "memT.out": memT_, "ck.rest": split_rest("ck", "ckv", 1.0),
                 "s0.max": s0_max, "s0.norm": s0_norm, "am.out": am, "gate.bias": gate_bias, "gate.add": gate_add,
                 **{f"scale{k}": scale(k) for k in range(4)}, "nT.out": nT, "rotate0": rotate(0), "rotate1": rotate(1),
                 "split.q.rest": split_rest("q", "split.q", float(HD) ** -0.5), "split.k.rest": split_rest("k", "split.k", 1.0),
                 "scores0.out": scores(0), "scores1.out": scores(1), "rows0.out": rows(0), "rows1.out": rows(1),
                 "attend0.out": attend(0), "attend1.out": attend(1), "unhead0.out": unhead(0), "unhead1.out": unhead(1),
                 "ctxT.out": ctxT, "dense.out": add(0, "dense"), "cq.rest": split_rest("cq", "cq", CSCALE),
                 "cdense.out": add(1, "cdense"), "miT.out": miT, "hidden.out": hidden, "down0.out": down(0), "down1.out": down(1)})

        @block.tensor
        def _(pe):
            wait = waiter(pe)
            reader = {}

            def mm(out, lhsT, rhs, start, stop, **kw):
                return nc.tensor.matmul(out, lhsT, rhs, start=start, stop=stop, **kw)

            def claim(b, signal, batch, n=None):
                if b in reader:
                    wait(*reader[b])
                reader[b] = (signal, batch, n)
                return bank[b]

            pe.wait_ge(c_loaded.sem, 16)

            def prep(_, __):
                banks = bank_of["prep", -1, 0]
                pe.wait_ge(gate_loaded.sem, 16)
                pe.wait_ge(wmem_loaded.sem, 16)
                for b, n in zip(banks, (1, 2, 4)):
                    claim(b, prep_ready, 0, n)
                for h in range(2):
                    for c in range(DC):
                        for r in range(DC):
                            nc.tensor.transpose(bank[banks[h]][:, D * c + P * r:D * c + P * r + P],
                                                w_gate[:, r, D * h + P * c:D * h + P * c + P], ident)
                for c in range(DC):
                    last = nc.tensor.transpose(bank[banks[2]][:, P * c:P * c + P], w_mem[:, c, :], ident)
                last.then_inc(prep_psum.sem, 1)
                pe.wait_ge(prep_ready.sem, 3)
                for c in range(DC):
                    last = mm(bank[banks[2]][:, D:2 * D], w_mem[:, c, :], spin[:, 0, D * c:D * c + D], c == 0, c == DC - 1)
                last.then_inc(prep_psum.sem, 1)

            def trig_(_, __):
                pe.wait_ge(onehot_ready.sem, 2)
                out = claim(bank_of["trig", -1, 0][0], trig_ready, 0, 1)
                for n in range(2):
                    for c in range(2):
                        last = mm(out[:, 2 * HD * n:2 * HD * n + 2 * HD], probs[:, 3, S * c + P * n:S * c + P * n + P],
                                  const[:, C_TAB + 2 * HD * c:C_TAB + 2 * HD * c + 2 * HD], c == 0, c == 1)
                last.then_inc(trig_psum.sem, 1)

            def transposed(out, src, width, signal):
                for c in range(width // P):
                    for n in range(NT):
                        last = nc.tensor.transpose(out[:, S * c + P * n:S * c + P * n + P], src[:, n, P * c:P * c + P], ident)
                last.then_inc(signal.sem, 1)

            def xT(b, _):
                wait(x_loaded[b], 0, 16)
                transposed(claim(bank_of["xT", b, 0][0], xT_ready, b), X[:, b], D, xT_psum)

            def memT_(b, _):
                wait(mem_loaded[b], 0, 16)
                transposed(claim(bank_of["memT", b, 0][0], memT_ready, b), mem[:, b], C, memT_psum)

            def y(b, _):
                wait(xT_ready, b)
                pe.wait_ge(wmem_loaded.sem, 16)
                out = claim(bank_of["y", b, 0][0], y_ready, b)
                for c in range(DC):
                    last = mm(out[:, 0:S], w_mem[:, c, :], UT[b % 2][:, c, :], c == 0, c == DC - 1)
                last.then_inc(y_psum.sem, 1)

            def ckv(b, _):
                wait(memT_ready, b)
                pe.wait_ge(ck_turned.sem, 1)
                pe.wait_ge(ckv_loaded.sem, 2 * 16)
                b0, b1 = bank_of["ckv", b, 0]
                mm(claim(b0, parts_ready["ck"], b)[:, 0:S], ck_w[:], memT[b % 2][:], True, True)\
                    .then_inc(split_psum["ck"].sem, 1)
                out = claim(b1, cv_ready, b)
                for n in range(NT):
                    last = mm(out[:, C * n:C * n + C], memT[b % 2][:, P * n:P * n + P], cv_w[:], True, True)
                last.then_inc(cv_psum.sem, 1)

            def s0(b, _):
                wait(y_ready, b)
                out = claim(bank_of["s0", b, 0][0], e0_ready, b)
                for n in range(NT):
                    last = mm(out[:, S * n:S * n + S], yT[b % 2][:, P * n:P * n + P], memT[b % 2][:], True, True)
                last.then_inc(s0_psum.sem, 1)

            def pT(b, _):
                wait(p0_ready, b)
                transposed(claim(bank_of["pT", b, 0][0], pT_ready, b), normed[b % 2], D, pT_psum)

            def am(b, _):
                wait(pT_ready, b)
                out = claim(bank_of["am", b, 0][0], am_ready, b)
                for k in range(2):
                    last = mm(out[:, 0:S], mem[:, b, k, :], TV[b % 2][:, k, :], k == 0, k == 1)
                last.then_inc(am_psum.sem, 1)

            def gate(b, _):
                wait(am_ready, b)
                pe.wait_ge(prep_ready.sem, 4)
                for n in range(NT):
                    out = claim(bank_of["gate", b, 0][n], residual[0], b, n + 1)
                    a = TL[b % 2][:, 0, P * n:P * n + P]
                    for c in range(DC):
                        mm(out[:, 0:D], UT[b % 2][:, c, P * n:P * n + P], w_gateT[:, c, :], c == 0, False)
                    mm(out[:, 0:D], a, w_gatem[:], False, True)
                    mm(out[:, D:2 * D], a, w_memT[:], True, True).then_inc(gate_psum.sem, 1)

            def nT(b, _):
                wait(normed_ready[1], b)
                transposed(claim(bank_of["nT", b, 0][0], nT_ready, b), normed[b % 2], D, nT_psum)

            def experts(out, b, n, w, cols):
                for e, src in enumerate((TV, TL)):
                    for c in range(DC):
                        last = mm(out, src[b % 2][:, c, P * n:P * n + P], w[:, e, c, cols], e == 0 and c == 0, e == 1 and c == DC - 1)
                return last

            def qk(n):
                def qk_(b, _):
                    pe.wait_ge(qkv_loaded.sem, 32)
                    wait(nT_ready, b)
                    out = claim(bank_of[f"qk{n}", b, 0][0], qr_ready, b, n + 1)
                    experts(out[:], b, n, qkv, slice(0, 2 * D)).then_inc(qk_psum.sem, 1)
                return qk_

            def v(b, _):
                out = claim(bank_of["v", b, 0][0], v_ready, b)
                for n in range(NT):
                    last = experts(out[:, D * n:D * n + D], b, n, qkv, slice(2 * D, 3 * D))
                last.then_inc(v_psum.sem, 1)

            def split(k, kind):
                def split_(b, _):
                    wait(qr_ready, b)
                    transposed(claim(bank_of[f"split.{k}", b, 0][0], parts_ready[k], b), QR[:, :, kind], D, split_psum[k])
                return split_

            def spread(mask, n):
                return mask.rearrange("p (o k) -> p o k", o=1).to_broadcast([P, n, P])

            def scores(layer):
                def scores_(b, u):
                    g, out = b % 2, claim(bank_of[f"scores{layer}", b, u][0], max_ready[layer], b, u + 1)
                    wait(stacked[layer][g], turns(b))
                    top = (SELF_ROWS, CROSS_ROWS)[layer]
                    q, k = Qs[g][0:top], Ks[g][0:top]
                    if layer == 0:
                        pe.wait_ge(bconst_ready.sem, 1)
                    if layer == 0 and u < 4:
                        for j in range(4):
                            mm(out[:, P * j:P * j + P], q[:, 4 * u + j, 0:P], k[:, 4 * u + j, 0:P], j == 0, False, skip_group_check=True)
                        last = mm(out[:].rearrange("p (h k) -> p h k", h=4), identb, spread(maskq, 4), False, True, skip_group_check=True)
                    elif layer == 0:
                        for j in range(2):
                            h = 2 * (u - 4) + j
                            mm(out[:, S * j:S * j + S], q[:, h, P:S], k[:, h, :], j == 0, False, skip_group_check=True)
                        last = mm(out[:].rearrange("p (h k) -> p h k", h=2)[:, :, P:S], identb, spread(maskq, 2), False, True, skip_group_check=True)
                    else:
                        for j in range(2):
                            last = mm(out[:, S * j:S * j + S], q[:, 2 * (u % 8) + j, P * (u // 8):P * (u // 8) + P],
                                      k[:, 2 * (u % 8) + j, :], j == 0, j == 1, skip_group_check=True)
                    last.then_inc(s_psum[layer].sem, 1)
                return scores_

            def rows(layer):
                def rows_(b, _):
                    wait(max_ready[layer], b)
                    out = claim(bank_of[f"rows{layer}", b, 0][0], nm_ready[layer], b)
                    for j in range(NT):
                        last = nc.tensor.transpose(out[0:NH, P * j:P * j + P], negmax[:, b % 2, j, :], ident)
                    last.then_inc(nm_psum[layer].sem, 1)
                return rows_

            def attend(layer):
                def attend_(b, hg):
                    g = b % 2
                    wait(max_rows[layer][g], turns(b))
                    pe.wait_ge(pool_consts.sem, 11)
                    top = (SELF_ROWS, CROSS_ROWS)[layer] + 2
                    q, k = Qs[g][0:top], Ks[g][0:top]
                    for u in range(NU[layer] if hg < 4 else 0):
                        out = claim(2 + exp_no[layer, b, hg, u] % 2, e_ready[layer], b, NU[layer] * hg + u + 1)
                        if layer == 0 and u < 2:
                            for j in range(2):
                                h = 4 * hg + 2 * u + j
                                mm(out[:, S * j:S * j + S], k[:, h, 0:P], q[:, h, :], j == 0, False, skip_group_check=True)
                            last = mm(out[:].rearrange("p (h q) -> p h q", h=2)[:, :, 0:P], identb, spread(maskk, 2),
                                      False, True, skip_group_check=True)
                        elif layer == 0:
                            for j in range(4):
                                mm(out[:, P * j:P * j + P], k[:, 4 * hg + j, P:S], q[:, 4 * hg + j, P:S], j == 0, False, skip_group_check=True)
                            last = mm(out[:].rearrange("p (h q) -> p h q", h=4), identb, spread(maskk, 4), False, True, skip_group_check=True)
                        else:
                            for j in range(2):
                                h = 4 * hg + 2 * (u % 2) + j
                                last = mm(out[:, S * j:S * j + S], k[:, h, P * (u // 2):P * (u // 2) + P], q[:, h, :],
                                          j == 0, j == 1, skip_group_check=True)
                        last.then_inc(st_psum[layer].sem, 1)
                    if hg >= 1:
                        values(layer, b, hg - 1)
                return attend_

            def values(layer, b, hg):
                wait(e_ready[layer], b, NU[layer] * (hg + 1))
                wait((v_ready, cv_ready)[layer], b)
                out = claim(bank_of[f"attend{layer}", b, hg + 1][0], heads_ready[layer], b, hg + 1)
                w = (V, Vc)[layer][b % 2]
                first = exp_no[layer, b, hg, 0]
                for k in range(2):
                    for j in range(4):
                        o = out[VW * j:VW * j + VW, :]
                        if layer == 0 and k == 1:
                            o, rhs = o[:, P:S], probs[:, (first + 2) % RING, P * j:P * j + P]
                        else:
                            o, rhs = o[:, 0:S], probs[:, (first + 2 * k + j // 2) % RING, S * (j % 2):S * (j % 2) + S]
                        last = mm(o, w[:, k, 4 * hg + j, :], rhs, k == 0, k == 1, skip_group_check=True)
                last.then_inc(pv_psum[layer].sem, 1)

            def unhead(layer):
                def unhead_(b, _):
                    wait(heads_ready[layer], b)
                    for j in range(NT):
                        out = claim(bank_of[f"unhead{layer}", b, 0][j], ctx_ready[layer], b, j + 1)
                        for hg in range(4):
                            last = nc.tensor.transpose(out[:, P * hg:P * hg + P], heads[b % 2][:, hg, P * j:P * j + P], ident)
                        last.then_inc(hT_psum[layer].sem, 1)
                return unhead_

            def ctxT(b, _):
                wait(ctx_ready[0], b)
                transposed(claim(bank_of["ctxT", b, 0][0], cT_ready[0], b), normed[b % 2], D, cT_psum[0])

            def dense_(b, _):
                pe.wait_ge(dense_loaded.sem, 32)
                wait(cT_ready[0], b)
                out = claim(bank_of["dense", b, 0][0], residual[2], b)
                for n in range(NT):
                    last = experts(out[:, D * n:D * n + D], b, n, dense, slice(0, D))
                last.then_inc(proj_psum[0].sem, 1)

            def ciT(b, _):
                wait(normed_ready[2], b)
                transposed(claim(bank_of["ciT", b, 0][0], ciT_ready, b), normed[b % 2], D, ciT_psum)

            def cq(b, _):
                wait(ciT_ready, b)
                pe.wait_ge(cq_turned.sem, 1)
                out = claim(bank_of["cq", b, 0][0], parts_ready["cq"], b)
                for c in range(DC):
                    last = mm(out[:, 0:S], cq_w[:, c, :], UT[b % 2][:, c, :], c == 0, c == DC - 1)
                last.then_inc(split_psum["cq"].sem, 1)

            def cctxT(b, _):
                wait(ctx_ready[1], b)
                transposed(claim(bank_of["cctxT", b, 0][0], cT_ready[1], b), normed[b % 2], C, cT_psum[1])

            def cdense_(b, _):
                wait(cT_ready[1], b)
                pe.wait_ge(cdense_loaded.sem, 16)
                out = claim(bank_of["cdense", b, 0][0], residual[3], b)
                for n in range(NT):
                    last = mm(out[:, D * n:D * n + D], yT[b % 2][:, P * n:P * n + P], cdense[:], True, True)
                last.then_inc(proj_psum[1].sem, 1)

            def miT(b, _):
                wait(normed_ready[3], b)
                transposed(claim(bank_of["miT", b, 0][0], miT_ready, b), normed[b % 2], D, miT_psum)

            def hidden(b, i):
                pe.wait_ge(mlp_loaded.sem, 8 * 16)
                wait(miT_ready, b)
                out = claim(bank_of["hidden", b, i][0], h_ready, b, i + 1)
                for k in range(2):
                    if i < NF - 1:
                        e, j = divmod(i, NFE)
                        for c in range(DC):
                            last = mm(out[:, S * k:S * k + S], w_up[:, k, c, FF * e + P * j:FF * e + P * j + P],
                                      (TV, TL)[e][b % 2][:, c, :], c == 0, c == DC - 1)
                    else:
                        for c in range(DC):
                            for e in range(2):
                                col = FF * e + NFE * P
                                last = mm(out[64 * e:64 * e + EDGE, S * k:S * k + S], w_up[:, k, c, col:col + EDGE],
                                          (TV, TL)[e][b % 2][:, c, :], c == 0, c == DC - 1, skip_group_check=True)
                last.then_inc(gu_psum.sem, 1)

            def down(n):
                def down_(b, _):
                    out = claim(bank_of[f"down{n}", b, 0][0], out_ready, b, n + 1)
                    for i in range(NF):
                        wait(h_ready, b, i + 1)
                        rows = P if i < NF - 1 else 64 + EDGE
                        last = mm(out[:, 0:D], H[0:rows, i, P * n:P * n + P], w_down[0:rows, i, :], i == 0, i == NF - 1)
                    last.then_inc(down_psum.sem, 1)
                return down_

            run({"prep": prep, "trig": trig_, "xT": xT, "memT": memT_, "y": y, "ckv": ckv, "s0": s0, "pT": pT, "am": am,
                 "gate": gate, "nT": nT, "qk0": qk(0), "qk1": qk(1), "v": v, "split.q": split("q", 0), "split.k": split("k", 1),
                 "scores0": scores(0), "scores1": scores(1), "rows0": rows(0), "rows1": rows(1), "attend0": attend(0),
                 "attend1": attend(1), "unhead0": unhead(0), "unhead1": unhead(1), "ctxT": ctxT, "dense": dense_,
                 "ciT": ciT, "cq": cq, "cctxT": cctxT, "cdense": cdense_, "miT": miT, "hidden": hidden,
                 "down0": down(0), "down1": down(1)})


CSCALE = float(np.float32(1.0 / np.sqrt(CHD)))

_INS = ["x", "ctx_1024", "pos_1xS", "mask_BxS_ik0", "L0_xattn_W_mem", "L0_xattn_W_gate", "L0_xattn_b_gate",
        "L0_xattn_norm_w", "L1_xattn_ln_in_w", "L1_xattn_ln_post_attn_w", "L1_xattn_ln_post_cross_w",
        "L1_xattn_v_qkv", "L1_xattn_l_qkv", "L1_xattn_v_dense", "L1_xattn_l_dense", "L1_xattn_cq_w",
        "L1_xattn_ckv_w", "L1_xattn_cdense_w", "L1_xattn_v_gate", "L1_xattn_v_up", "L1_xattn_v_down",
        "L1_xattn_l_gate", "L1_xattn_l_up", "L1_xattn_l_down"]


def kernel(**inputs):
    import concourse.bacc as bacc
    from concourse.bass_utils import run_bass_kernel_spmd

    nc = bacc.Bacc("TRN2", target_bir_lowering=False, num_devices=1)
    arrays, tensors = {}, {}
    named = {name: np.ascontiguousarray(inputs[name]) for name in _INS}
    named["const"] = constants()
    for name, a in named.items():
        arrays[f"in_{name}"] = a
        tensors[name] = nc.dram_tensor(f"in_{name}", a.shape, mybir.dt.from_np(a.dtype), kind="ExternalInput").ap()
    tensors["out"] = nc.dram_tensor("out", (BATCH, S, D), F32, kind="ExternalOutput").ap()
    build(nc, tensors)
    r = run_bass_kernel_spmd(nc, [arrays], core_ids=[0])
    return r.results[0]["out"]
```

```python
from contextlib import ExitStack

import numpy as np

import concourse.bass as bass
from concourse import mybir

F32 = mybir.dt.float32
BF16 = mybir.dt.bfloat16
I32 = mybir.dt.int32
ALU = mybir.AluOpType
ACT = mybir.ActivationFunctionType
AX_X = mybir.AxisListType.X

P = 128
BATCH, S, D = 4, 256, 256
C = 128
NH = 16
HD = D // NH
CHD = C // NH
FF = 688
NFE = FF // P
EDGE = FF - NFE * P
NF = 2 * NFE + 1
EPS = 1e-6
NT = S // P
DC = D // P
RING = 6
VW = 32
NEG = -1e30
SELF_Q = ((3, (0,)), (2, (1,)), (1, (2,)))
SELF_K = ((1, (0, 1, 2)), (1, (0, 1)), (1, (0,)))
CROSS_Q = ((3, (0,)), (3, (1,)), (3, (2,)))
CROSS_K = ((3, (0, 1, 2)),)
SELF_ROWS = 6 * HD
CROSS_ROWS = 9 * CHD

C_ID, C_MQ, C_MK, C_T, C_TAB = 0, P, 2 * P, 3 * P, 3 * P + 2
C_END = C_TAB + 2 * 2 * HD


def constants():
    out = np.zeros((P, C_END), np.float32)
    i = np.arange(P)
    out[:, C_ID:C_ID + P] = np.eye(P)
    out[:, C_MQ:C_MQ + P] = np.where(i[None, :] > i[:, None], NEG, 0.0)
    out[:, C_MK:C_MK + P] = np.where(i[:, None] > i[None, :], NEG, 0.0)
    out[:, C_T] = i
    out[:, C_T + 1] = i + P
    inv = (1.0 / np.float32(10000.0) ** (np.arange(0, HD, 2, dtype=np.float32) / np.float32(HD))).astype(np.float32)
    freq = np.outer(np.arange(S, dtype=np.float32), inv).astype(np.float32)
    cos = np.cos(freq.astype(np.float64))
    sin = np.sin(freq.astype(np.float64))
    table = np.concatenate([cos, cos, -sin, sin], axis=1).astype(np.float32)
    out[:, C_TAB:] = table.reshape(2, P, 2 * HD).transpose(1, 0, 2).reshape(P, -1)
    return out


START = (0.0, 21.0, 137.0, 150.0)
ALONE = (
    ("xT", 0.0), ("memT", 0.45), ("xT.out", 0.65), ("memT.out", 0.85), ("y", 1.2), ("ckv", 2.1), ("y.out", 2.3),
    ("ckv.first", 2.9), ("s0", 3.0), ("cv.out", 3.2), ("ck.rest", 3.3), ("s0.max", 4.3), ("s0.exp", 5.3), ("s0.norm", 6.3),
    ("pT", 7.2), ("pT.out", 7.8), ("am", 8.5), ("am.out", 9.5), ("gate", 10.1), ("gate.bias", 11.8), ("gate.tanh", 12.3),
    ("gate.add", 13.6), ("square0", 14.8), ("rstd0", 16.4), ("scale0", 17.4), ("square1", 18.0), ("rstd1", 18.8),
    ("scale1", 19.8),
    ("nT", 20.8), ("nT.out", 21.4), ("qk0", 23.0), ("qk1", 26.4), ("rotate0", 26.6), ("v", 29.8), ("rotate1", 30.0),
    ("split.q", 33.2), ("v.out", 33.4), ("split.k", 33.6), ("split.q.first", 33.8), ("split.k.first", 34.3),
    ("split.q.rest", 34.6), ("write.q", 35.0), ("split.k.rest", 36.5), ("stack0", 37.0),
    ("scores0", 44.0), ("rows0", 48.2), ("attend0", 52.4),
    ("stack.ck", 62.6), ("unhead0", 63.2), ("unhead0.out", 63.7), ("ctxT", 65.4), ("ctxT.out", 66.0), ("dense", 67.6), ("dense.out", 71.2),
    ("square2", 72.0), ("rstd2", 72.8), ("scale2", 73.8),
    ("ciT", 74.8), ("ciT.out", 75.4), ("cq", 76.2), ("cq.first", 77.2), ("cq.rest", 77.6), ("stack1", 78.2),
    ("scores1", 84.2), ("rows1", 89.8), ("attend1", 93.2),
    ("unhead1", 108.2), ("unhead1.out", 108.7), ("cctxT", 110.6), ("cctxT.out", 111.0), ("cdense", 111.6),
    ("cdense.out", 112.6), ("square3", 113.4), ("rstd3", 114.3), ("scale3", 115.3),
    ("miT", 116.3), ("miT.out", 116.9), ("hidden", 118.5), ("down0", 137.9), ("down0.out", 142.8),
    ("down1", 142.7), ("down1.out", 147.6),
)
EACH = {"scores0": 0.62, "scores1": 0.62, "attend0": 2.2, "attend1": 2.9, "hidden": 1.73, "rows0": 3.8, "rows1": 5.1}
LATER = {"scores0": 0.4, "scores1": 0.4, "rows0": 0.4, "rows1": 0.4, "attend0": 2.1, "attend1": 2.8, "hidden": 1.8}
MANY = {"scores0": 12, "scores1": 16, "attend0": 5, "attend1": 5, "hidden": NF, "rows0": 2, "rows1": 2}
YIELD = {}
PREP = (("prep", 4.0), ("prep.out", 7.3), ("product", 8.4), ("product.out", 9.6), ("masks", 10.3), ("positions", 15.9),
        ("trig", 18.8), ("trig.out", 20.9))
TENSOR = {"xT": 0.43, "memT": 0.21, "y": 0.85, "ckv": 0.85, "s0": 0.85, "pT": 0.43, "am": 0.85, "gate": 3.4, "nT": 0.43,
          "qk0": 3.4, "qk1": 3.4, "v": 3.4, "split.q": 0.43, "split.k": 0.43, "scores0": 0.36, "rows0": 0.2, "attend0": 2.0,
          "unhead0": 0.86, "ctxT": 0.43, "dense": 3.4, "ciT": 0.43, "cq": 0.85, "scores1": 0.22, "rows1": 0.2,
          "attend1": 2.7, "unhead1": 0.86, "cctxT": 0.21, "cdense": 0.85, "miT": 0.43, "hidden": 1.7, "down0": 4.7,
          "down1": 4.7, "prep": 1.7, "product": 0.8, "trig": 0.3}
VECTOR = {"memT.out": 0.4, "ck.rest": 1.0, "s0.max": 0.8, "s0.norm": 0.8, "am.out": 0.4, "gate.bias": 0.8, "gate.add": 2.2,
          "scale0": 0.8, "scale1": 0.8, "nT.out": 1.3, "rotate0": 2.0, "rotate1": 2.0, "split.q.rest": 1.8,
          "split.k.rest": 1.8, "scores0.out": 0.6, "rows0.out": 0.4, "attend0.out": 0.4, "unhead0.out": 1.4,
          "ctxT.out": 1.3, "dense.out": 0.6, "scale2": 0.8, "cq.rest": 1.1, "scores1.out": 0.6, "rows1.out": 0.4,
          "attend1.out": 0.4, "unhead1.out": 1.4, "cdense.out": 0.6, "scale3": 0.8, "miT.out": 1.3, "hidden.out": 0.9,
          "down0.out": 0.4, "down1.out": 0.4, "prep.out": 1.2, "product.out": 0.4, "masks": 2.5, "positions": 1.8}

LAST_READ = {"ckv": "ck.rest", "s0": "s0.exp", "gate": "gate.add", "qk0": "rotate0", "qk1": "rotate1",
             "split.q": "split.q.rest", "split.k": "split.k.rest", "cq": "cq.rest",
             **{k: k + ".out" for k in ("xT", "memT", "y", "pT", "am", "nT", "v", "scores0", "scores1", "rows0", "rows1",
                                        "attend0", "attend1", "unhead0", "unhead1", "ctxT", "dense", "ciT", "cctxT",
                                        "cdense", "miT", "hidden", "down0", "down1", "trig")},
             "prep": "product.out"}
TAKES = {"ckv": 2, "gate": 2, "unhead0": 2, "unhead1": 2, "prep": 3}
SHARED = (("hidden", 1, "down1"), ("rotate0", 1, "split.k"), ("split.q.first", 1, "write.q"), ("split.k.first", 1, "stack0"), ("ckv.first", 1, "ck.rest"),
          ("cq.first", 1, "stack1"), ("s0.exp", 1, "s0.norm"), ("gate.bias", 1, "gate.add"),
          ("xT.out", 2, "cq"), ("y.out", 2, "cdense"), ("s0.exp", 2, "miT"), ("pT.out", 3, "hidden"), ("memT.out", 2, "s0"),
          ("cv.out", 2, "attend1"), ("v.out", 2, "attend0"), ("stack0", 2, "attend1"), ("write.q", 1, "write.q"),
          ("rows0", 2, "rows1.out"))


def timeline():
    later = {-1: [(at, stage, 0) for stage, at in PREP]}
    for b in range(BATCH):
        later[b] = []
        for stage, at in ALONE:
            for j in range(MANY.get(stage, 1)):
                at_j = at + j * EACH.get(stage, 0.0)
                later[b].append((at_j, stage, j))
                if stage in LATER:
                    later[b].append((at_j + LATER[stage], stage + ".out", j))
        later[b].sort(key=lambda f: f[0])
    start = {-1: 0.0, **dict(enumerate(START))}
    free, held, bank_of, order, over = [0, 1, 4, 5, 6, 7], {}, {}, [], set()

    def takes(stage, j):
        if stage not in LAST_READ or (stage, j) in (("attend0", 0), ("attend1", 0)):
            return 0
        return TAKES.get(stage, 1)

    def can_go(b):
        _, stage, j = later[b][0]
        if takes(stage, j) > len(free):
            return False
        if stage in ("attend0", "attend1") and j == 0 and attending:
            return False
        return all(stage != s or b < ago or (after, b - ago, MANY.get(after.removesuffix(".out"), 1) - 1) in over for s, ago, after in SHARED)

    attending = set()
    until = [0.0, 0.0]
    costs = (TENSOR, VECTOR)

    def could_start(b):
        at, stage, _ = later[b][0]
        return max([start[b] + at] + [u for u, cost in zip(until, costs) if stage in cost])

    while any(later.values()):
        _, at, b = min((could_start(b) + YIELD.get(later[b][0][1], 0.0), could_start(b), b) for b in later if later[b] and can_go(b))
        for o in later:
            if later[o] and (o == b or not can_go(o)):
                start[o] += max(0.0, at - start[o] - later[o][0][0])
        for k in range(2):
            if later[b][0][1] in costs[k]:
                until[k] = at + costs[k][later[b][0][1]]
        _, stage, j = later[b].pop(0)
        order.append((stage, b, j))
        over.add((stage, b, j))
        n = takes(stage, j)
        if n:
            bank_of[stage, b, j] = [free.pop(0) for _ in range(n)]
            held[LAST_READ[stage], b, j] = bank_of[stage, b, j]
        free += held.pop((stage, b, j), [])
        if stage in ("attend0", "attend1", "unhead0", "unhead1") and j == 0:
            attending ^= {b}
    return order, bank_of


def build(nc, t):
    order, bank_of = timeline()
    x_d, ctx_d, out_d = (t[n].rearrange("b (s p) d -> b p s d", p=P) for n in ("x", "ctx_1024", "out"))

    exp_no, exp_head = {}, []
    for stage, b, hg in order:
        if stage in ("attend0", "attend1") and hg < 4:
            layer = int(stage[-1])
            for u in range(3 + layer):
                exp_no[layer, b, hg, u] = len(exp_head)
                exp_head.append((layer, b, hg))
    turns_of_rows = [(int(stage[-1]), b) for stage, b, half in order if stage in ("rows0", "rows1") and half == 0]
    rows_before = dict(zip(turns_of_rows[1:], turns_of_rows))
    turns_of_heads = [(layer, b) for layer, b, hg in exp_head if hg == 0]
    heads_before = {new: old for old, new in zip(turns_of_heads, turns_of_heads[1:]) if new != old}

    with ExitStack() as stack:
        def sb(name, shape, dt=F32):
            return stack.enter_context(nc.sbuf_tensor(name, shape, dt))

        const = sb("const", [P, C_END])
        ident = const[:, C_ID:C_ID + P]
        bconst = sb("bconst", [P, 3 * P], BF16)
        identb, maskq, maskk = (bconst[:, P * j:P * j + P] for j in range(3))
        half = sb("half", [P, 4])
        trig = sb("trig", [P, NT, 2 * HD])
        w_mem = sb("w_mem", [P, DC, C])
        w_memT = sb("w_memT", [P, D])
        w_gateT = sb("w_gateT", [P, DC, D])
        w_gatem = sb("w_gatem", [P, D])
        b_gate = sb("b_gate", [P, D])
        norm_w = sb("norm_w", [P, 4, D])
        qkv = sb("qkv", [P, 2, DC, 3 * D])
        dense = sb("dense", [P, 2, DC, D])
        cq_w = sb("cq_w", [P, DC, C])
        ck_w = sb("ck_w", [P, C])
        cv_w = sb("cv_w", [P, C])
        cdense = sb("cdense", [P, D])
        w_up = sb("w_up", [P, 2, DC, 2 * FF])
        w_down = sb("w_down", [P, NF, D])

        X = sb("X", [P, BATCH, NT, D])
        mem = sb("mem", [P, BATCH, NT, C])
        vm = sb("vm", [P, BATCH, S], BF16)
        lm = sb("lm", [P, BATCH, S], BF16)

        def two(name, shape, dt=F32):
            return [sb(f"{name}{g}", shape, dt) for g in range(2)]

        UT = two("UT", [P, DC, S])
        memT = two("memT", [P, S])
        yT = two("yT", [P, S])
        normed = two("normed", [P, NT, D])
        Qs = two("Qs", [P, NH, S], BF16)
        Ks = two("Ks", [P, NH, S], BF16)
        V = two("V", [P, NT, NH, VW])
        Vc = two("Vc", [P, NT, NH, VW])

        TV = [sb(f"TV{g}", [P, DC, S]) for g in range(3)]
        TL = [sb(f"TL{g}", [P, DC, S]) for g in range(3)]

        heads = sb("heads", [P, 4, S])
        gated = sb("gated", [P, NT, D])
        spin = sb("spin", [P, 2, 2 * D])
        QR = sb("QR", [P, NT, 2, D])
        parts = {k: sb(f"parts_{k}", [P, w, 3, S], BF16) for k, w in (("q", DC), ("k", DC), ("ck", 1), ("cq", 1))}
        rest = spin[:, 1, :]
        squares = sb("squares", [P, 2, D], BF16)
        probs = sb("probs", [P, RING, 2 * S])
        H = sb("H", [P, NF, S])
        tanh = sb("tanh", [P, 2, S])
        silu = sb("silu", [P, 2, S])
        negmax = sb("negmax", [P, 2, 2, NH])
        nm_parts = sb("nm_parts", [NH // 2, 2, 2, S], BF16)
        sc = sb("sc", [P, 16 + 3 * 32])
        nm0, l0, r0 = sc[:, 0:2], sc[:, 2:4], sc[:, 4:6]
        sumsq, var, rstd = (sc[:, 16 + 32 * j:48 + 32 * j] for j in range(3))
        rsum = sb("rsum", [P, NH])
        maski = QR[:].rearrange("p n k d -> p (n k) d").bitcast(I32)
        posi = silu[:, 0, :].bitcast(I32)
        w_gate = H[:, 0:2 * DC, :].rearrange("p (c h) d -> p c (h d)", c=DC)
        cq_loaded_w = H[:, 2 * DC, :].rearrange("p (c e) -> p c e", c=DC)
        ck_loaded_w = H[:, 2 * DC + 1, 0:C]

        bank = [stack.enter_context(nc.psum_tensor(f"bank{j}", [P, 512], F32)) for j in range(8)]

        scratch = {k: nc.dram_tensor(f"scratch_{k}", [BATCH, 3, w, S], BF16, kind="Internal").ap()
                   for k, w in (("q", D), ("k", D), ("ck", C), ("cq", C))}

        class Signal:
            def __init__(self, name, per=1):
                self.sem = stack.enter_context(nc.semaphore(name))
                self.per = per

        ident_loaded = Signal("ident_loaded")
        c_loaded, pos_loaded, mask_loaded = Signal("c_loaded"), Signal("pos_loaded"), Signal("mask_loaded")
        gate_loaded, vec_loaded = Signal("gate_loaded"), Signal("vec_loaded")
        late_vec_loaded = Signal("late_vec_loaded")
        qkv_loaded, dense_loaded = Signal("qkv_loaded"), Signal("dense_loaded")
        cdense_loaded, mlp_loaded, wmem_loaded = Signal("cdense_loaded"), Signal("mlp_loaded"), Signal("wmem_loaded")
        bconst_ready, pool_consts, eps_ready = Signal("bconst_ready"), Signal("pool_consts"), Signal("eps_ready")
        cq_loaded, ckv_loaded, ck_turned, cq_turned = (Signal(n) for n in ("cq_loaded", "ckv_loaded", "ck_turned", "cq_turned"))
        pos_step, masks_ready, onehot_ready = Signal("pos_step"), Signal("masks_ready"), Signal("onehot_ready")
        trig_psum, trig_ready = Signal("trig_psum"), Signal("trig_ready")
        prep_psum, prep_ready = Signal("prep_psum"), Signal("prep_ready")
        x_loaded, mem_loaded = ([Signal(f"{n}_loaded{b}") for b in range(BATCH)] for n in ("x", "mem"))
        xT_psum, xT_ready = Signal("xT_psum"), Signal("xT_ready")
        memT_psum, memT_ready = Signal("memT_psum"), Signal("memT_ready")
        y_psum, y_ready = Signal("y_psum"), Signal("y_ready")
        cv_psum, cv_ready = Signal("cv_psum"), Signal("cv_ready")
        s0_psum, nm0_ready, e0_ready, p0_ready = Signal("s0_psum"), Signal("nm0_ready"), Signal("e0_ready", NT), Signal("p0_ready", NT)
        pT_psum, pT_ready, am_psum, am_ready = Signal("pT_psum"), Signal("pT_ready"), Signal("am_psum"), Signal("am_ready")
        gate_psum, pre_gate, gate_ready = Signal("gate_psum", NT), Signal("pre_gate", NT), Signal("gate_ready", NT)
        residual = [Signal(f"residual{k}", NT) for k in range(4)]
        sumsq_ready = [Signal(f"sumsq_ready{k}", NT) for k in range(4)]
        var_ready, rstd_ready = ([Signal(f"{n}_ready{k}") for k in range(4)] for n in ("var", "rstd"))
        normed_ready = [Signal(f"normed_ready{k}", NT) for k in range(4)]
        nT_psum, nT_ready = Signal("nT_psum"), Signal("nT_ready")
        qk_psum, qr_ready, v_psum, v_ready = Signal("qk_psum", NT), Signal("qr_ready", NT), Signal("v_psum"), Signal("v_ready")
        kinds = ("q", "k", "ck", "cq")
        split_psum, first_part, parts_ready, written = (
            {k: Signal(f"{n}_{k}", 16 * (DC if n == "written" and k in "qk" else 1) if n == "written" else 1) for k in kinds}
            for n in ("split_psum", "first_part", "parts_ready", "written"))
        stacked0 = [[Signal(f"stacked0_{g}_{half}", 6 * 16) for half in range(2)] for g in range(2)]
        stacked1 = [Signal(f"stacked1_{g}", 5 * 16) for g in range(2)]
        s_psum, max_ready = ([Signal(f"{n}{layer}", (12, 16)[layer]) for layer in range(2)] for n in ("s_psum", "max_ready"))
        nm_psum, nm_hi, nm_ready = ([Signal(f"{n}{layer}", 2) for layer in range(2)] for n in ("nm_psum", "nm_hi", "nm_ready"))
        max_rows = [[[Signal(f"max_rows{layer}_{g}_{half}", 32) for half in range(2)] for g in range(2)] for layer in range(2)]
        NU = (3, 4)
        st_psum, e_ready = ([Signal(f"{n}{layer}", 4 * NU[layer]) for layer in range(2)] for n in ("st_psum", "e_ready"))
        pv_psum, heads_ready = ([Signal(f"{n}{layer}", 4) for layer in range(2)] for n in ("pv_psum", "heads_ready"))
        hT_psum, ctx_ready = ([Signal(f"{n}{layer}", NT) for layer in range(2)] for n in ("hT_psum", "ctx_ready"))
        cT_psum, cT_ready, proj_psum = ([Signal(f"{n}{layer}") for layer in range(2)] for n in ("cT_psum", "cT_ready", "proj_psum"))
        ciT_psum, ciT_ready, miT_psum, miT_ready = Signal("ciT_psum"), Signal("ciT_ready"), Signal("miT_psum"), Signal("miT_ready")
        gu_psum, tanh_ready, silu_ready, h_ready = Signal("gu_psum", NF), Signal("tanh_ready", NF), Signal("silu_ready", NF), Signal("h_ready", NF)
        down_psum, out_ready = Signal("down_psum", NT), Signal("out_ready", NT)
        out_stored = Signal("out_stored", 16 * NT)
        v_step = Signal("v_step")

        def waiter(eng):
            seen = {}

            def wait(signal, b, n=None):
                at = b * signal.per + (signal.per if n is None else n)
                if at > 0 and seen.get(signal, 0) < at:
                    seen[signal] = at
                    eng.wait_ge(signal.sem, at)
            return wait

        def run(handlers):
            for stage, b, j in order:
                if stage in handlers:
                    handlers[stage](b, j)

        def turns(k):
            return k // 2

        def score_heads(layer, u):
            half, u = divmod(u, MANY[f"scores{layer}"] // 2)
            tile = 0 if u < (2, 4)[layer] else 1
            n = 4 if layer == 0 and tile == 0 else 2
            return tile, NH // 2 * half + n * (u - tile * (2, 4)[layer]), n

        block = stack.enter_context(nc.Block())

        @block.sync
        def _(sp):
            wait = waiter(sp)
            sp.dma_start(X[:, 0], x_d[0]).then_inc(x_loaded[0].sem, 16)
            sp.dma_start(ident, t["const"][:, C_ID:C_ID + P]).then_inc(ident_loaded.sem, 16)
            sp.dma_start(w_mem[:], t["L0_xattn_W_mem"].rearrange("(c p) e -> p c e", p=P)).then_inc(wmem_loaded.sem, 16)
            sp.dma_start(mem[:, 0], ctx_d[0]).then_inc(mem_loaded[0].sem, 16)
            sp.dma_start(const[:, C_MQ:], t["const"][:, C_MQ:]).then_inc(c_loaded.sem, 16)

            def load(at, src, signal):
                sp.dma_start(at, src).then_inc(signal.sem, 16)

            load(maski, t["mask_BxS_ik0"].partition_broadcast(P), mask_loaded)
            load(posi, t["pos_1xS"][0].partition_broadcast(P), pos_loaded)
            for e, n in enumerate("vl"):
                load(qkv[:, e], t[f"L1_xattn_{n}_qkv"].rearrange("(c p) n -> p c n", p=P), qkv_loaded)
            load(cq_loaded_w, t["L1_xattn_cq_w"].rearrange("(c p) e -> p c e", p=P), cq_loaded)
            load(cdense[:], t["L1_xattn_cdense_w"], cdense_loaded)
            for name, at in (("L1_xattn_ln_post_cross_w", norm_w[:, 2]), ("L1_xattn_ln_post_attn_w", norm_w[:, 3])):
                load(at, t[name].partition_broadcast(P), late_vec_loaded)
            for e, n in enumerate("vl"):
                load(dense[:, e], t[f"L1_xattn_{n}_dense"].rearrange("(c p) n -> p c n", p=P), dense_loaded)
            for b in range(1, BATCH):
                load(X[:, b], x_d[b], x_loaded[b])
                load(mem[:, b], ctx_d[b], mem_loaded[b])
            for k, w in enumerate(("gate", "up")):
                for e, n in enumerate("vl"):
                    load(w_up[:, k, :, FF * e:FF * e + FF], t[f"L1_xattn_{n}_{w}"].rearrange("(c p) n -> p c n", p=P), mlp_loaded)
            for e, n in enumerate("vl"):
                w = t[f"L1_xattn_{n}_down"]
                load(w_down[:, NFE * e:NFE * e + NFE, :], w[0:NFE * P].rearrange("(c p) n -> p c n", p=P), mlp_loaded)
            sp.wait_ge(pool_consts.sem, 1)
            for e, n in enumerate("vl"):
                load(w_down[64 * e:64 * e + EDGE, NF - 1, :], t[f"L1_xattn_{n}_down"][NFE * P:FF], mlp_loaded)

            def write(k, b):
                wait(parts_ready[k], b)
                for c in range(DC if k in "qk" else 1):
                    sp.dma_start(scratch[k][b, :, P * c:P * c + P, :].rearrange("p d t -> d p t"), parts[k][:, c])\
                        .then_inc(written[k].sem, 16)

            def read(k, b, dst, runs, hd, signal, heads_=slice(0, NH)):
                wait(written[k], b)
                src, row = scratch[k][b].rearrange("p (d h) t -> p d h t", h=NH)[:, :, heads_], 0
                for often, which in runs:
                    n = len(which) * hd
                    s = src[which[0]:which[0] + len(which)].rearrange("p d h t -> (p d) (h t)")
                    out = dst[row:row + often * n, heads_].rearrange("r h s -> r (h s)")
                    if often > 1:
                        s = s.rearrange("(o r) n -> o r n", o=1).to_broadcast([often, n, s.shape[1]])
                    sp.dma_start(out, s).then_inc(signal.sem, 16)
                    row += often * n

            def write_q(b, _):
                write("q", b)

            def write_ck(b, _):
                write("ck", b)

            def stack0(b, _):
                g = b % 2
                write("k", b)
                if b >= 2:
                    wait(st_psum[1], b - 2)
                for half in range(2):
                    heads_ = slice(NH // 2 * half, NH // 2 * (half + 1))
                    read("q", b, Qs[g], SELF_Q, HD, stacked0[g][half], heads_)
                    read("k", b, Ks[g], SELF_K, HD, stacked0[g][half], heads_)

            def stack_ck(b, _):
                g = b % 2
                wait(st_psum[0], b)
                sp.dma_start(Ks[g][CROSS_ROWS:CROSS_ROWS + 2], Ks[g][SELF_ROWS:SELF_ROWS + 2]).then_inc(stacked1[g].sem, 16)
                read("ck", b, Ks[g], CROSS_K, CHD, stacked1[g])

            def stack_cq(b, _):
                write("cq", b)
                read("cq", b, Qs[b % 2], CROSS_Q, CHD, stacked1[b % 2])

            def rows(layer):
                def rows_(b, half):
                    g, top, few = b % 2, (SELF_ROWS, CROSS_ROWS)[layer], NH // 2
                    wait(nm_ready[layer], b, half + 1)
                    for j in range(2):
                        sp.dma_start(Qs[g][top + j:top + j + 1, few * half:few * half + few, :], nm_parts[:, half, j:j + 1, :])\
                            .then_inc(max_rows[layer][g][half].sem, 16)
                return rows_

            def down(n):
                def down_(b, _):
                    wait(out_ready, b, n + 1)
                    sp.dma_start(out_d[b][:, n, :], X[:, b, n, :]).then_inc(out_stored.sem, 16)
                return down_

            run({"write.q": write_q, "stack0": stack0, "ck.rest": write_ck, "stack.ck": stack_ck, "stack1": stack_cq,
                 "rows0.out": rows(0), "rows1.out": rows(1),
                 "down0.out": down(0), "down1.out": down(1)})
            wait(out_stored, BATCH - 1)

        @block.gpsimd
        def _(pool):
            wait = waiter(pool)
            pool.memset(half[:, 0:2], -0.5).then_inc(eps_ready.sem, 1)
            pool.memset(half[:, 2:4], EPS).then_inc(eps_ready.sem, 1)
            pool.wait_ge(eps_ready.sem, 2)
            pool.memset(w_down[32:64, NF - 1, :], 0.0).then_inc(pool_consts.sem, 1)
            pool.wait_ge(pool_consts.sem, 1)
            pool.wait_ge(ckv_loaded.sem, 2 * 16)
            pool.tensor_copy(ck_w[:].rearrange("p (d h) -> p h d", h=NH), ck_loaded_w.rearrange("p (h d) -> p h d", h=NH))\
                .then_inc(ck_turned.sem, 1)
            for v in (Vc[0], V[0], Vc[1], V[1]):
                pool.memset(v[:], 0.0).then_inc(pool_consts.sem, 1)
            for v, n in ((Vc[0], 2), (V[0], 3), (Vc[1], 4), (V[1], 5)):
                pool.wait_ge(pool_consts.sem, n)
                pool.memset(v[:].rearrange("p n h w -> p (n h) w")[:, :, HD:HD + 1], 1.0).then_inc(pool_consts.sem, 1)
            for g in range(2):
                pool.wait_ge(pool_consts.sem, 9 + g)
                pool.memset(Ks[g][SELF_ROWS:SELF_ROWS + 2], 1.0).then_inc(pool_consts.sem, 1)
            pool.wait_ge(pool_consts.sem, 11)
            pool.wait_ge(cq_loaded.sem, 16)
            pool.tensor_copy(cq_w[:].rearrange("p c (d h) -> p c h d", h=NH),
                             cq_loaded_w.rearrange("p c (h d) -> p c h d", h=NH)).then_inc(cq_turned.sem, 1)

            def rstd_of(k):
                def rstd_(b, _):
                    cols = slice(8 * k + 2 * b, 8 * k + 2 * b + 2)
                    wait(sumsq_ready[k], b)
                    pool.tensor_tensor(var[:, cols], sumsq[:, cols], half[:, 2:4], ALU.add).then_inc(var_ready[k].sem, 1)
                    wait(var_ready[k], b)
                    pool.tensor_tensor(rstd[:, cols], var[:, cols], half[:, 0:2], ALU.pow).then_inc(rstd_ready[k].sem, 1)
                return rstd_

            run({f"rstd{k}": rstd_of(k) for k in range(4)})

        @block.scalar
        def _(act):
            wait = waiter(act)

            def load(at, src, signal):
                act.dma_start(at, src).then_inc(signal.sem, 16)

            load(w_gate, t["L0_xattn_W_gate"].rearrange("(c p) f -> p c f", p=P), gate_loaded)
            load(ck_loaded_w, t["L1_xattn_ckv_w"][:, 0:C], ckv_loaded)
            load(cv_w[:], t["L1_xattn_ckv_w"][:, C:2 * C], ckv_loaded)
            for name, at in (("L0_xattn_b_gate", b_gate[:]), ("L0_xattn_norm_w", norm_w[:, 0]),
                             ("L1_xattn_ln_in_w", norm_w[:, 1])):
                load(at, t[name].partition_broadcast(P), vec_loaded)

            def xT(b, _):
                wait(xT_psum, b)
                if b >= 2:
                    wait(split_psum["cq"], b - 2)
                nc.scalar.copy(UT[b % 2][:].rearrange("p c s -> p (c s)"), bank[bank_of["xT", b, 0][0]][:]).then_inc(xT_ready.sem, 1)

            def y(b, _):
                wait(y_psum, b)
                if b >= 2:
                    wait(proj_psum[1], b - 2)
                nc.scalar.copy(yT[b % 2][:], bank[bank_of["y", b, 0][0]][:, 0:S]).then_inc(y_ready.sem, 1)

            def first(k, stage, scale):
                def first_(b, _):
                    w = S * (DC if k in "qk" else 1)
                    wait(split_psum[k], b)
                    if b >= 1:
                        wait(written[k], b - 1)
                    nc.scalar.activation(parts[k][:, :, 0, :], bank[bank_of[stage, b, 0][0]][:, 0:w].rearrange("p (c s) -> p c s", s=S),
                                         ACT.Copy, scale=scale).then_inc(first_part[k].sem, 1)
                return first_

            def cv(b, _):
                wait(cv_psum, b)
                act.wait_ge(pool_consts.sem, 9)
                if b >= 2:
                    wait(pv_psum[1], b - 2)
                nc.scalar.copy(Vc[b % 2][:].rearrange("p n h w -> p (n h) w")[:, :, 0:CHD],
                               bank[bank_of["ckv", b, 0][1]][:, 0:NT * C].rearrange("p (h w) -> p h w", w=CHD)).then_inc(cv_ready.sem, 1)

            def v(b, _):
                wait(v_psum, b)
                if b >= 2:
                    wait(pv_psum[0], b - 2)
                nc.scalar.copy(V[b % 2][:].rearrange("p n h w -> p (n h) w")[:, :, 0:HD],
                               bank[bank_of["v", b, 0][0]][:].rearrange("p (h w) -> p h w", w=HD)).then_inc(v_ready.sem, 1)

            def s0(b, _):
                if b >= 2:
                    wait(miT_psum, b - 2)
                if b >= 1:
                    wait(p0_ready, b - 1)
                for n in range(NT):
                    wait(nm0_ready, b)
                    nc.scalar.activation(normed[b % 2][:, n, :], bank[bank_of["s0", b, 0][0]][:, S * n:S * n + S],
                                         ACT.Exp, bias=nm0[:, n:n + 1], scale=float(D) ** -0.5,
                                         accum_out=l0[:, n:n + 1]).then_inc(e0_ready.sem, 1)

            def pT(b, _):
                wait(pT_psum, b)
                if b >= 3:
                    wait(gu_psum, b - 3)
                nc.scalar.copy(TV[b % 3][:].rearrange("p c s -> p (c s)"), bank[bank_of["pT", b, 0][0]][:]).then_inc(pT_ready.sem, 1)

            def gate(b, _):
                for n in range(NT):
                    wait(pre_gate, b, n + 1)
                    nc.scalar.activation(gated[:, n, :], gated[:, n, :], ACT.Tanh, scale=0.5).then_inc(gate_ready.sem, 1)

            squared = []

            def square(k):
                def square_(b, _):
                    for n in range(NT):
                        wait(residual[k], b, n + 1)
                        if squared:
                            wait(*squared[-1])
                        nc.scalar.activation(squares[:, n, :], X[:, b, n, :], ACT.Square, scale=float(D) ** -0.5,
                                             accum_out=sumsq[:, 8 * k + 2 * b + n:8 * k + 2 * b + n + 1]).then_inc(sumsq_ready[k].sem, 1)
                    squared.append((sumsq_ready[k], b))
                return square_

            def rows(layer):
                def rows_(b, half):
                    wait(nm_psum[layer], b, half + 1)
                    if (layer, b) in rows_before:
                        la, ba = rows_before[layer, b]
                        wait(max_rows[la][ba % 2][half], turns(ba))
                    nc.scalar.copy(nm_parts[:, half, 0, :], bank[bank_of[f"rows{layer}", b, half][0]][0:NH // 2, 0:S])\
                        .then_inc(nm_hi[layer].sem, 1)
                return rows_

            def attend(layer):
                def attend_(b, hg):
                    for u in range(NU[layer] if hg < 4 else 0):
                        no = exp_no[layer, b, hg, u]
                        wait(st_psum[layer], b, NU[layer] * hg + u + 1)
                        if no >= RING:
                            la, ba, ha = exp_head[no - RING]
                            wait(pv_psum[la], ba, ha + 1)
                        nc.scalar.activation(probs[:, no % RING, :], bank[2 + no % 2][:], ACT.Exp).then_inc(e_ready[layer].sem, 1)
                return attend_

            def ciT(b, _):
                wait(ciT_psum, b)
                nc.scalar.copy(UT[b % 2][:].rearrange("p c s -> p (c s)"), bank[bank_of["ciT", b, 0][0]][:]).then_inc(ciT_ready.sem, 1)

            def cctxT(b, _):
                wait(cT_psum[1], b)
                nc.scalar.copy(yT[b % 2][:], bank[bank_of["cctxT", b, 0][0]][:, 0:S]).then_inc(cT_ready[1].sem, 1)

            def hidden(b, i):
                wait(gu_psum, b, i + 1)
                if i + b * NF >= 2:
                    wait(silu_ready, 0, i + b * NF - 1)
                nc.scalar.activation(tanh[:, i % 2, :], bank[bank_of["hidden", b, i][0]][:, 0:S], ACT.Tanh, scale=0.5)\
                    .then_inc(tanh_ready.sem, 1)

            run({"xT.out": xT, "y.out": y, "ckv.first": first("ck", "ckv", 1.0), "cv.out": cv, "v.out": v, "s0.exp": s0,
                 "pT.out": pT, "gate.tanh": gate, "rows0.out": rows(0), "rows1.out": rows(1),
                 "split.q.first": first("q", "split.q", float(HD) ** -0.5), "split.k.first": first("k", "split.k", 1.0),
                 "cq.first": first("cq", "cq", CSCALE), "attend0": attend(0), "attend1": attend(1),
                 "ciT.out": ciT, "cctxT.out": cctxT, "hidden.out": hidden, **{f"square{k}": square(k) for k in range(4)}})

        @block.vector
        def _(dve):
            wait = waiter(dve)
            steps = [0]

            def step(ins):
                steps[0] += 1
                ins.then_inc(v_step.sem, 1)
                dve.wait_ge(v_step.sem, steps[0])

            dve.memset(H[64:128, NF - 1, :], 0.0).then_inc(masks_ready.sem, 1)
            dve.memset(H[32:64, NF - 1, :], 0.0).then_inc(masks_ready.sem, 1)
            dve.memset(vm[:, :, S - 1:S], 0.0).then_inc(masks_ready.sem, 1)
            dve.wait_ge(ident_loaded.sem, 16)
            dve.wait_ge(c_loaded.sem, 16)
            dve.tensor_copy(bconst[:], const[:, 0:3 * P]).then_inc(bconst_ready.sem, 1)

            def masks(_, __):
                is_one = probs[:, 0:2, :].rearrange("p a (b s) -> p (a b) s", s=S)
                dve.wait_ge(mask_loaded.sem, 16)
                step(dve.tensor_scalar(is_one, maski, 1.0, None, ALU.is_equal))
                dve.tensor_tensor(vm[:, :, 0:S - 1], is_one[:, :, 0:S - 1], is_one[:, :, 1:S], ALU.mult).then_inc(masks_ready.sem, 1)
                dve.wait_ge(masks_ready.sem, 4)
                dve.tensor_scalar(lm[:], vm[:], -1.0, 1.0, ALU.mult, ALU.add).then_inc(masks_ready.sem, 1)
                dve.wait_ge(masks_ready.sem, 5)

            def positions(_, __):
                dve.wait_ge(pos_loaded.sem, 16)
                pos, wrap = probs[:, 2, 0:S], probs[:, 2, S:2 * S]
                step(dve.tensor_copy(pos, posi))
                step(dve.tensor_scalar(wrap, pos, 0.0, float(S), ALU.is_lt, ALU.mult))
                step(dve.tensor_tensor(pos, pos, wrap, ALU.add))
                step(dve.tensor_scalar(pos, pos, 0.0, float(S - 1), ALU.max, ALU.min))
                for c in range(2):
                    dve.tensor_scalar(probs[:, 3, S * c:S * c + S], pos, const[:, C_T + c:C_T + c + 1], None, ALU.is_equal)\
                        .then_inc(onehot_ready.sem, 1)

            def prep(_, __):
                a, b, c = bank_of["prep", -1, 0]
                dve.wait_ge(prep_psum.sem, 1)
                dve.tensor_copy(w_gateT[:].rearrange("p c d -> p (c d)"), bank[a][:]).then_inc(prep_ready.sem, 1)
                dve.tensor_copy(spin[:, 0, :], bank[b][:]).then_inc(prep_ready.sem, 1)
                dve.tensor_copy(w_memT[:], bank[c][:, 0:D]).then_inc(prep_ready.sem, 1)

            def product(_, __):
                dve.wait_ge(prep_psum.sem, 2)
                dve.tensor_copy(w_gatem[:], bank[bank_of["prep", -1, 0][2]][:, D:2 * D]).then_inc(prep_ready.sem, 1)

            def trig_(_, __):
                dve.wait_ge(trig_psum.sem, 1)
                dve.tensor_copy(trig[:].rearrange("p n w -> p (n w)"), bank[bank_of["trig", -1, 0][0]][:, 0:4 * HD])\
                    .then_inc(trig_ready.sem, 1)
                dve.wait_ge(trig_ready.sem, 1)

            def memT_(b, _):
                wait(memT_psum, b)
                if b >= 2:
                    wait(s0_psum, b - 2)
                dve.tensor_copy(memT[b % 2][:], bank[bank_of["memT", b, 0][0]][:, 0:S]).then_inc(memT_ready.sem, 1)

            def split_rest(k, stage, scale):
                def split_(b, _):
                    w = DC if k in "qk" else 1
                    src = bank[bank_of[stage, b, 0][0]][:, 0:w * S].rearrange("p (c s) -> p c s", s=S)
                    left = rest[:, 0:w * S].rearrange("p (c s) -> p c s", s=S)
                    wait(first_part[k], b)
                    step(dve.scalar_tensor_tensor(left, src, scale, parts[k][:, :, 0, :], ALU.mult, ALU.subtract))
                    step(dve.tensor_copy(parts[k][:, :, 1, :], left))
                    dve.tensor_tensor(parts[k][:, :, 2, :], left, parts[k][:, :, 1, :], ALU.subtract).then_inc(parts_ready[k].sem, 1)
                    wait(parts_ready[k], b)
                return split_

            def s0_max(b, _):
                wait(s0_psum, b)
                if b >= 1:
                    wait(e0_ready, b - 1)
                step(dve.tensor_reduce(nm0, bank[bank_of["s0", b, 0][0]][:].rearrange("p (n s) -> p n s", n=2),
                                       AX_X, ALU.max, negate=True))
                dve.tensor_scalar(nm0, nm0, float(D) ** -0.5, None, ALU.mult).then_inc(nm0_ready.sem, 1)

            def s0_norm(b, _):
                wait(e0_ready, b)
                step(dve.reciprocal(r0, l0))
                for n in range(NT):
                    dve.tensor_scalar(normed[b % 2][:, n, :], normed[b % 2][:, n, :], r0[:, n:n + 1], None, ALU.mult)\
                        .then_inc(p0_ready.sem, 1)
                wait(p0_ready, b)

            def am(b, _):
                wait(am_psum, b)
                if b >= 3:
                    wait(gu_psum, b - 3)
                dve.tensor_copy(TL[b % 3][:, 0, :], bank[bank_of["am", b, 0][0]][:, 0:S]).then_inc(am_ready.sem, 1)

            def gate_bias(b, _):
                dve.wait_ge(vec_loaded.sem, 3 * 16)
                for n in range(NT):
                    wait(gate_psum, b, n + 1)
                    dve.tensor_tensor(gated[:, n, :], bank[bank_of["gate", b, 0][n]][:, 0:D], b_gate[:], ALU.add)\
                        .then_inc(pre_gate.sem, 1)

            def gate_add(b, _):
                wait(x_loaded[b], 0, 16)
                for n in range(NT):
                    wait(gate_ready, b, n + 1)
                    step(dve.tensor_scalar(gated[:, n, :], gated[:, n, :], 0.5, 0.5, ALU.mult, ALU.add))
                    step(dve.tensor_tensor(gated[:, n, :], bank[bank_of["gate", b, 0][n]][:, D:2 * D], gated[:, n, :], ALU.mult))
                    dve.tensor_tensor(X[:, b, n, :], X[:, b, n, :], gated[:, n, :], ALU.add).then_inc(residual[0].sem, 1)
                wait(residual[0], b)

            def scale(k):
                def scale_(b, _):
                    wait(rstd_ready[k], b)
                    if k == 1:
                        wait(residual[1], b)
                    if k == 2:
                        dve.wait_ge(late_vec_loaded.sem, 2 * 16)
                    for n in range(NT):
                        col = 8 * k + 2 * b + n
                        dst, signal = (X[:, b, n, :], residual[1]) if k == 0 else (normed[b % 2][:, n, :], normed_ready[k])
                        dve.scalar_tensor_tensor(dst, X[:, b, n, :], rstd[:, col:col + 1], norm_w[:, k, :],
                                                 ALU.mult, ALU.mult).then_inc(signal.sem, 1)
                return scale_

            def masked(stage, b, signal):
                src = bank[bank_of[stage, b, 0][0]][:].rearrange("p (c s) -> p c s", c=DC)
                for m, dst in ((vm, TV), (lm, TL)):
                    ins = dve.tensor_tensor(dst[b % 3][:], src, m[:, b:b + 1, :].to_broadcast([P, DC, S]), ALU.mult)
                ins.then_inc(signal.sem, 1)

            def nT(b, _):
                wait(nT_psum, b)
                masked("nT", b, nT_ready)

            def rotate(n):
                def rotate_(b, _):
                    wait(qk_psum, b, n + 1)
                    qk = bank[bank_of[f"qk{n}", b, 0][0]][:].rearrange("p (h w) -> p h w", w=HD)
                    tab = trig[:, n, :]
                    cos = tab[:, 0:HD].rearrange("p (o w) -> p o w", o=1).to_broadcast([P, 2 * NH, HD])
                    sin = tab[:, HD:2 * HD].rearrange("p (o w) -> p o w", o=1)
                    a, s = (spin[:, i, :].rearrange("p (h w) -> p h w", w=HD) for i in range(2))
                    hw = HD // 2
                    dve.tensor_tensor(a, qk, cos, ALU.mult)
                    dve.tensor_tensor(s[:, :, 0:hw], qk[:, :, hw:HD], sin[:, :, 0:hw].to_broadcast([P, 2 * NH, hw]), ALU.mult)
                    step(dve.tensor_tensor(s[:, :, hw:HD], qk[:, :, 0:hw], sin[:, :, hw:HD].to_broadcast([P, 2 * NH, hw]), ALU.mult))
                    if b >= 1:
                        wait(split_psum["k"], b - 1)
                    dve.tensor_tensor(QR[:, n].rearrange("p k (d h) -> p k h d", h=NH),
                                      spin[:, 0, :].rearrange("p (k h d) -> p k h d", k=2, h=NH),
                                      spin[:, 1, :].rearrange("p (k h d) -> p k h d", k=2, h=NH), ALU.add).then_inc(qr_ready.sem, 1)
                    wait(qr_ready, b, n + 1)
                return rotate_

            def scores(layer):
                def scores_(b, u):
                    wait(s_psum[layer], b, u + 1)
                    tile, first, n = score_heads(layer, u)
                    dve.tensor_reduce(negmax[:, b % 2, tile, first:first + n],
                                      bank[bank_of[f"scores{layer}", b, u][0]][:].rearrange("p (h k) -> p h k", h=n),
                                      AX_X, ALU.max, negate=True).then_inc(max_ready[layer].sem, 1)
                return scores_

            def rows(layer):
                def rows_(b, half):
                    wait(nm_hi[layer], b, half + 1)
                    dve.tensor_tensor(nm_parts[:, half, 1, :], bank[bank_of[f"rows{layer}", b, half][0]][0:NH // 2, 0:S],
                                      nm_parts[:, half, 0, :], ALU.subtract).then_inc(nm_ready[layer].sem, 1)
                return rows_

            def attend(layer):
                def attend_(b, hg):
                    if hg == 0:
                        return
                    wait(pv_psum[layer], b, hg)
                    if (layer, b) in heads_before:
                        la, ba = heads_before[layer, b]
                        wait(hT_psum[la], ba)
                    dve.tensor_copy(heads[:, hg - 1, :], bank[bank_of[f"attend{layer}", b, hg][0]][:, 0:S])\
                        .then_inc(heads_ready[layer].sem, 1)
                return attend_

            def unhead(layer):
                def unhead_(b, _):
                    w = (HD, CHD)[layer]
                    for j in range(NT):
                        wait(hT_psum[layer], b, j + 1)
                        src = bank[bank_of[f"unhead{layer}", b, 0][j]][:].rearrange("p (h w) -> p h w", w=VW)
                        step(dve.reciprocal(rsum[:].rearrange("p (h o) -> p h o", o=1), src[:, :, HD:HD + 1]))
                        dst = normed[b % 2][:, j, 0:NH * w].rearrange("p (h w) -> p h w", w=w)
                        dve.tensor_tensor(dst, src[:, :, 0:w],
                                          rsum[:].rearrange("p (h o) -> p h o", o=1).to_broadcast([P, NH, w]), ALU.mult)\
                            .then_inc(ctx_ready[layer].sem, 1)
                        wait(ctx_ready[layer], b, j + 1)
                return unhead_

            def ctxT(b, _):
                wait(cT_psum[0], b)
                masked("ctxT", b, cT_ready[0])

            def add(layer, stage):
                def add_(b, _):
                    wait(proj_psum[layer], b)
                    x = X[:, b].rearrange("p n d -> p (n d)")
                    dve.tensor_tensor(x, bank[bank_of[stage, b, 0][0]][:], x, ALU.add).then_inc(residual[2 + layer].sem, NT)
                    wait(residual[2 + layer], b)
                return add_

            def miT(b, _):
                wait(miT_psum, b)
                masked("miT", b, miT_ready)

            def hidden(b, i):
                psum = bank[bank_of["hidden", b, i][0]]
                wait(tanh_ready, b, i + 1)
                if b >= 1:
                    wait(down_psum, b - 1)
                rows = (slice(0, P),) if i < NF - 1 else (slice(0, EDGE), slice(64, 64 + EDGE))
                for r in rows:
                    last = dve.scalar_tensor_tensor(silu[r, i % 2, :], tanh[r, i % 2, :], 1.0, psum[r, 0:S], ALU.add, ALU.mult)
                last.then_inc(silu_ready.sem, 1)
                wait(silu_ready, b, i + 1)
                for r in rows:
                    last = dve.scalar_tensor_tensor(H[r, i, :], silu[r, i % 2, :], 0.5, psum[r, S:2 * S], ALU.mult, ALU.mult)
                last.then_inc(h_ready.sem, 1)

            def down(n):
                def down_(b, _):
                    wait(down_psum, b, n + 1)
                    dve.tensor_tensor(X[:, b, n, :], bank[bank_of[f"down{n}", b, 0][0]][:, 0:D], X[:, b, n, :], ALU.add)\
                        .then_inc(out_ready.sem, 1)
                return down_

            run({"prep.out": prep, "product.out": product, "masks": masks, "positions": positions,
                 "trig.out": trig_, "memT.out": memT_, "ck.rest": split_rest("ck", "ckv", 1.0),
                 "s0.max": s0_max, "s0.norm": s0_norm, "am.out": am, "gate.bias": gate_bias, "gate.add": gate_add,
                 **{f"scale{k}": scale(k) for k in range(4)}, "nT.out": nT, "rotate0": rotate(0), "rotate1": rotate(1),
                 "split.q.rest": split_rest("q", "split.q", float(HD) ** -0.5), "split.k.rest": split_rest("k", "split.k", 1.0),
                 "scores0.out": scores(0), "scores1.out": scores(1), "rows0.out": rows(0), "rows1.out": rows(1),
                 "attend0.out": attend(0), "attend1.out": attend(1), "unhead0.out": unhead(0), "unhead1.out": unhead(1),
                 "ctxT.out": ctxT, "dense.out": add(0, "dense"), "cq.rest": split_rest("cq", "cq", CSCALE),
                 "cdense.out": add(1, "cdense"), "miT.out": miT, "hidden.out": hidden, "down0.out": down(0), "down1.out": down(1)})

        @block.tensor
        def _(pe):
            wait = waiter(pe)
            reader = {}

            def mm(out, lhsT, rhs, start, stop, **kw):
                return nc.tensor.matmul(out, lhsT, rhs, start=start, stop=stop, **kw)

            def claim(b, signal, batch, n=None):
                if b in reader:
                    wait(*reader[b])
                reader[b] = (signal, batch, n)
                return bank[b]

            pe.wait_ge(ident_loaded.sem, 16)

            def prep(_, __):
                banks = bank_of["prep", -1, 0]
                pe.wait_ge(gate_loaded.sem, 16)
                pe.wait_ge(wmem_loaded.sem, 16)
                for b, n in zip(banks, (1, 2, 4)):
                    claim(b, prep_ready, 0, n)
                for h in range(2):
                    for c in range(DC):
                        for r in range(DC):
                            nc.tensor.transpose(bank[banks[h]][:, D * c + P * r:D * c + P * r + P],
                                                w_gate[:, r, D * h + P * c:D * h + P * c + P], ident)
                for c in range(DC):
                    last = nc.tensor.transpose(bank[banks[2]][:, P * c:P * c + P], w_mem[:, c, :], ident)
                last.then_inc(prep_psum.sem, 1)

            def product(_, __):
                banks = bank_of["prep", -1, 0]
                pe.wait_ge(prep_ready.sem, 3)
                for c in range(DC):
                    last = mm(bank[banks[2]][:, D:2 * D], w_mem[:, c, :], spin[:, 0, D * c:D * c + D], c == 0, c == DC - 1)
                last.then_inc(prep_psum.sem, 1)

            def trig_(_, __):
                pe.wait_ge(onehot_ready.sem, 2)
                out = claim(bank_of["trig", -1, 0][0], trig_ready, 0, 1)
                for n in range(2):
                    for c in range(2):
                        last = mm(out[:, 2 * HD * n:2 * HD * n + 2 * HD], probs[:, 3, S * c + P * n:S * c + P * n + P],
                                  const[:, C_TAB + 2 * HD * c:C_TAB + 2 * HD * c + 2 * HD], c == 0, c == 1)
                last.then_inc(trig_psum.sem, 1)

            def transposed(out, src, width, signal):
                for c in range(width // P):
                    for n in range(NT):
                        last = nc.tensor.transpose(out[:, S * c + P * n:S * c + P * n + P], src[:, n, P * c:P * c + P], ident)
                last.then_inc(signal.sem, 1)

            def xT(b, _):
                wait(x_loaded[b], 0, 16)
                transposed(claim(bank_of["xT", b, 0][0], xT_ready, b), X[:, b], D, xT_psum)

            def memT_(b, _):
                wait(mem_loaded[b], 0, 16)
                transposed(claim(bank_of["memT", b, 0][0], memT_ready, b), mem[:, b], C, memT_psum)

            def y(b, _):
                wait(xT_ready, b)
                pe.wait_ge(wmem_loaded.sem, 16)
                out = claim(bank_of["y", b, 0][0], y_ready, b)
                for c in range(DC):
                    last = mm(out[:, 0:S], w_mem[:, c, :], UT[b % 2][:, c, :], c == 0, c == DC - 1)
                last.then_inc(y_psum.sem, 1)

            def ckv(b, _):
                wait(memT_ready, b)
                pe.wait_ge(ck_turned.sem, 1)
                pe.wait_ge(ckv_loaded.sem, 2 * 16)
                b0, b1 = bank_of["ckv", b, 0]
                mm(claim(b0, parts_ready["ck"], b)[:, 0:S], ck_w[:], memT[b % 2][:], True, True)\
                    .then_inc(split_psum["ck"].sem, 1)
                out = claim(b1, cv_ready, b)
                for n in range(NT):
                    last = mm(out[:, C * n:C * n + C], memT[b % 2][:, P * n:P * n + P], cv_w[:], True, True)
                last.then_inc(cv_psum.sem, 1)

            def s0(b, _):
                wait(y_ready, b)
                out = claim(bank_of["s0", b, 0][0], e0_ready, b)
                for n in range(NT):
                    last = mm(out[:, S * n:S * n + S], yT[b % 2][:, P * n:P * n + P], memT[b % 2][:], True, True)
                last.then_inc(s0_psum.sem, 1)

            def pT(b, _):
                wait(p0_ready, b)
                transposed(claim(bank_of["pT", b, 0][0], pT_ready, b), normed[b % 2], D, pT_psum)

            def am(b, _):
                wait(pT_ready, b)
                out = claim(bank_of["am", b, 0][0], am_ready, b)
                for k in range(2):
                    last = mm(out[:, 0:S], mem[:, b, k, :], TV[b % 3][:, k, :], k == 0, k == 1)
                last.then_inc(am_psum.sem, 1)

            def gate(b, _):
                wait(am_ready, b)
                pe.wait_ge(prep_ready.sem, 4)
                for n in range(NT):
                    out = claim(bank_of["gate", b, 0][n], residual[0], b, n + 1)
                    a = TL[b % 3][:, 0, P * n:P * n + P]
                    for c in range(DC):
                        mm(out[:, 0:D], UT[b % 2][:, c, P * n:P * n + P], w_gateT[:, c, :], c == 0, False)
                    mm(out[:, 0:D], a, w_gatem[:], False, True)
                    mm(out[:, D:2 * D], a, w_memT[:], True, True).then_inc(gate_psum.sem, 1)

            def nT(b, _):
                wait(normed_ready[1], b)
                transposed(claim(bank_of["nT", b, 0][0], nT_ready, b), normed[b % 2], D, nT_psum)

            def experts(out, b, n, w, cols):
                for e, src in enumerate((TV, TL)):
                    for c in range(DC):
                        last = mm(out, src[b % 3][:, c, P * n:P * n + P], w[:, e, c, cols], e == 0 and c == 0, e == 1 and c == DC - 1)
                return last

            def qk(n):
                def qk_(b, _):
                    pe.wait_ge(qkv_loaded.sem, 32)
                    wait(nT_ready, b)
                    out = claim(bank_of[f"qk{n}", b, 0][0], qr_ready, b, n + 1)
                    experts(out[:], b, n, qkv, slice(0, 2 * D)).then_inc(qk_psum.sem, 1)
                return qk_

            def v(b, _):
                out = claim(bank_of["v", b, 0][0], v_ready, b)
                for n in range(NT):
                    last = experts(out[:, D * n:D * n + D], b, n, qkv, slice(2 * D, 3 * D))
                last.then_inc(v_psum.sem, 1)

            def split(k, kind):
                def split_(b, _):
                    wait(qr_ready, b)
                    transposed(claim(bank_of[f"split.{k}", b, 0][0], parts_ready[k], b), QR[:, :, kind], D, split_psum[k])
                return split_

            def spread(mask, n):
                return mask.rearrange("p (o k) -> p o k", o=1).to_broadcast([P, n, P])

            def scores(layer):
                def scores_(b, u):
                    g, out = b % 2, claim(bank_of[f"scores{layer}", b, u][0], max_ready[layer], b, u + 1)
                    wait(stacked0[g][u // 6] if layer == 0 else stacked1[g], turns(b))
                    top = (SELF_ROWS, CROSS_ROWS)[layer]
                    q, k = Qs[g][0:top], Ks[g][0:top]
                    if layer == 0:
                        pe.wait_ge(bconst_ready.sem, 1)
                    tile, first, n = score_heads(layer, u)
                    tokens = slice(P * tile, P * tile + P)
                    if layer == 0 and tile == 0:
                        for j in range(n):
                            mm(out[:, P * j:P * j + P], q[:, first + j, tokens], k[:, first + j, 0:P], j == 0, False, skip_group_check=True)
                        last = mm(out[:].rearrange("p (h k) -> p h k", h=n), identb, spread(maskq, n), False, True, skip_group_check=True)
                    elif layer == 0:
                        for j in range(n):
                            mm(out[:, S * j:S * j + S], q[:, first + j, tokens], k[:, first + j, :], j == 0, False, skip_group_check=True)
                        last = mm(out[:].rearrange("p (h k) -> p h k", h=n)[:, :, P:S], identb, spread(maskq, n), False, True, skip_group_check=True)
                    else:
                        for j in range(n):
                            last = mm(out[:, S * j:S * j + S], q[:, first + j, tokens], k[:, first + j, :], j == 0, j == n - 1,
                                      skip_group_check=True)
                    last.then_inc(s_psum[layer].sem, 1)
                return scores_

            def rows(layer):
                def rows_(b, half):
                    few = NH // 2
                    wait(max_ready[layer], b, MANY[f"scores{layer}"] // 2 * (half + 1))
                    out = claim(bank_of[f"rows{layer}", b, half][0], nm_ready[layer], b, half + 1)
                    for j in range(NT):
                        last = nc.tensor.transpose(out[0:few, P * j:P * j + P], negmax[:, b % 2, j, few * half:few * half + few], ident)
                    last.then_inc(nm_psum[layer].sem, 1)
                return rows_

            def attend(layer):
                def attend_(b, hg):
                    g = b % 2
                    if hg < 4:
                        wait(max_rows[layer][g][hg // 2], turns(b))
                    pe.wait_ge(pool_consts.sem, 11)
                    top = (SELF_ROWS, CROSS_ROWS)[layer] + 2
                    q, k = Qs[g][0:top], Ks[g][0:top]
                    for u in range(NU[layer] if hg < 4 else 0):
                        out = claim(2 + exp_no[layer, b, hg, u] % 2, e_ready[layer], b, NU[layer] * hg + u + 1)
                        if layer == 0 and u < 2:
                            for j in range(2):
                                h = 4 * hg + 2 * u + j
                                mm(out[:, S * j:S * j + S], k[:, h, 0:P], q[:, h, :], j == 0, False, skip_group_check=True)
                            last = mm(out[:].rearrange("p (h q) -> p h q", h=2)[:, :, 0:P], identb, spread(maskk, 2),
                                      False, True, skip_group_check=True)
                        elif layer == 0:
                            for j in range(4):
                                mm(out[:, P * j:P * j + P], k[:, 4 * hg + j, P:S], q[:, 4 * hg + j, P:S], j == 0, False, skip_group_check=True)
                            last = mm(out[:].rearrange("p (h q) -> p h q", h=4), identb, spread(maskk, 4), False, True, skip_group_check=True)
                        else:
                            for j in range(2):
                                h = 4 * hg + 2 * (u % 2) + j
                                last = mm(out[:, S * j:S * j + S], k[:, h, P * (u // 2):P * (u // 2) + P], q[:, h, :],
                                          j == 0, j == 1, skip_group_check=True)
                        last.then_inc(st_psum[layer].sem, 1)
                    if hg >= 1:
                        values(layer, b, hg - 1)
                return attend_

            def values(layer, b, hg):
                wait(e_ready[layer], b, NU[layer] * (hg + 1))
                wait((v_ready, cv_ready)[layer], b)
                out = claim(bank_of[f"attend{layer}", b, hg + 1][0], heads_ready[layer], b, hg + 1)
                w = (V, Vc)[layer][b % 2]
                first = exp_no[layer, b, hg, 0]
                for k in range(2):
                    for j in range(4):
                        o = out[VW * j:VW * j + VW, :]
                        if layer == 0 and k == 1:
                            o, rhs = o[:, P:S], probs[:, (first + 2) % RING, P * j:P * j + P]
                        else:
                            o, rhs = o[:, 0:S], probs[:, (first + 2 * k + j // 2) % RING, S * (j % 2):S * (j % 2) + S]
                        last = mm(o, w[:, k, 4 * hg + j, :], rhs, k == 0, k == 1, skip_group_check=True)
                last.then_inc(pv_psum[layer].sem, 1)

            def unhead(layer):
                def unhead_(b, _):
                    wait(heads_ready[layer], b)
                    for j in range(NT):
                        out = claim(bank_of[f"unhead{layer}", b, 0][j], ctx_ready[layer], b, j + 1)
                        for hg in range(4):
                            last = nc.tensor.transpose(out[:, P * hg:P * hg + P], heads[:, hg, P * j:P * j + P], ident)
                        last.then_inc(hT_psum[layer].sem, 1)
                return unhead_

            def ctxT(b, _):
                wait(ctx_ready[0], b)
                transposed(claim(bank_of["ctxT", b, 0][0], cT_ready[0], b), normed[b % 2], D, cT_psum[0])

            def dense_(b, _):
                pe.wait_ge(dense_loaded.sem, 32)
                wait(cT_ready[0], b)
                out = claim(bank_of["dense", b, 0][0], residual[2], b)
                for n in range(NT):
                    last = experts(out[:, D * n:D * n + D], b, n, dense, slice(0, D))
                last.then_inc(proj_psum[0].sem, 1)

            def ciT(b, _):
                wait(normed_ready[2], b)
                transposed(claim(bank_of["ciT", b, 0][0], ciT_ready, b), normed[b % 2], D, ciT_psum)

            def cq(b, _):
                wait(ciT_ready, b)
                pe.wait_ge(cq_turned.sem, 1)
                out = claim(bank_of["cq", b, 0][0], parts_ready["cq"], b)
                for c in range(DC):
                    last = mm(out[:, 0:S], cq_w[:, c, :], UT[b % 2][:, c, :], c == 0, c == DC - 1)
                last.then_inc(split_psum["cq"].sem, 1)

            def cctxT(b, _):
                wait(ctx_ready[1], b)
                transposed(claim(bank_of["cctxT", b, 0][0], cT_ready[1], b), normed[b % 2], C, cT_psum[1])

            def cdense_(b, _):
                wait(cT_ready[1], b)
                pe.wait_ge(cdense_loaded.sem, 16)
                out = claim(bank_of["cdense", b, 0][0], residual[3], b)
                for n in range(NT):
                    last = mm(out[:, D * n:D * n + D], yT[b % 2][:, P * n:P * n + P], cdense[:], True, True)
                last.then_inc(proj_psum[1].sem, 1)

            def miT(b, _):
                wait(normed_ready[3], b)
                transposed(claim(bank_of["miT", b, 0][0], miT_ready, b), normed[b % 2], D, miT_psum)

            def hidden(b, i):
                pe.wait_ge(mlp_loaded.sem, 8 * 16)
                wait(miT_ready, b)
                out = claim(bank_of["hidden", b, i][0], h_ready, b, i + 1)
                for k in range(2):
                    if i < NF - 1:
                        e, j = divmod(i, NFE)
                        for c in range(DC):
                            last = mm(out[:, S * k:S * k + S], w_up[:, k, c, FF * e + P * j:FF * e + P * j + P],
                                      (TV, TL)[e][b % 3][:, c, :], c == 0, c == DC - 1)
                    else:
                        for c in range(DC):
                            for e in range(2):
                                col = FF * e + NFE * P
                                last = mm(out[64 * e:64 * e + EDGE, S * k:S * k + S], w_up[:, k, c, col:col + EDGE],
                                          (TV, TL)[e][b % 3][:, c, :], c == 0, c == DC - 1, skip_group_check=True)
                last.then_inc(gu_psum.sem, 1)

            def down(n):
                def down_(b, _):
                    out = claim(bank_of[f"down{n}", b, 0][0], out_ready, b, n + 1)
                    for i in range(NF):
                        wait(h_ready, b, i + 1)
                        rows = P if i < NF - 1 else 64 + EDGE
                        last = mm(out[:, 0:D], H[0:rows, i, P * n:P * n + P], w_down[0:rows, i, :], i == 0, i == NF - 1)
                    last.then_inc(down_psum.sem, 1)
                return down_

            run({"prep": prep, "product": product, "trig": trig_, "xT": xT, "memT": memT_, "y": y, "ckv": ckv, "s0": s0, "pT": pT, "am": am,
                 "gate": gate, "nT": nT, "qk0": qk(0), "qk1": qk(1), "v": v, "split.q": split("q", 0), "split.k": split("k", 1),
                 "scores0": scores(0), "scores1": scores(1), "rows0": rows(0), "rows1": rows(1), "attend0": attend(0),
                 "attend1": attend(1), "unhead0": unhead(0), "unhead1": unhead(1), "ctxT": ctxT, "dense": dense_,
                 "ciT": ciT, "cq": cq, "cctxT": cctxT, "cdense": cdense_, "miT": miT, "hidden": hidden,
                 "down0": down(0), "down1": down(1)})


CSCALE = float(np.float32(1.0 / np.sqrt(CHD)))

_INS = ["x", "ctx_1024", "pos_1xS", "mask_BxS_ik0", "L0_xattn_W_mem", "L0_xattn_W_gate", "L0_xattn_b_gate",
        "L0_xattn_norm_w", "L1_xattn_ln_in_w", "L1_xattn_ln_post_attn_w", "L1_xattn_ln_post_cross_w",
        "L1_xattn_v_qkv", "L1_xattn_l_qkv", "L1_xattn_v_dense", "L1_xattn_l_dense", "L1_xattn_cq_w",
        "L1_xattn_ckv_w", "L1_xattn_cdense_w", "L1_xattn_v_gate", "L1_xattn_v_up", "L1_xattn_v_down",
        "L1_xattn_l_gate", "L1_xattn_l_up", "L1_xattn_l_down"]


def kernel(**inputs):
    import concourse.bacc as bacc
    from concourse.bass_utils import run_bass_kernel_spmd

    nc = bacc.Bacc("TRN2", target_bir_lowering=False, num_devices=1)
    arrays, tensors = {}, {}
    named = {name: np.ascontiguousarray(inputs[name]) for name in _INS}
    named["const"] = constants()
    for name, a in named.items():
        arrays[f"in_{name}"] = a
        tensors[name] = nc.dram_tensor(f"in_{name}", a.shape, mybir.dt.from_np(a.dtype), kind="ExternalInput").ap()
    tensors["out"] = nc.dram_tensor("out", (BATCH, S, D), F32, kind="ExternalOutput").ap()
    build(nc, tensors)
    r = run_bass_kernel_spmd(nc, [arrays], core_ids=[0])
    return r.results[0]["out"]
```
